# Optimizing a Trainium2 kernel written in Bass

```python
import numpy as np
import jax
import jax.numpy as jnp

def _softmax(x, axis=-1):
    return jax.nn.softmax(x, axis=axis)

def _gelu(x):
    return jax.nn.gelu(x, approximate=True)

def _silu(x):
    return jax.nn.silu(x)

def _sigmoid(x):
    return jax.nn.sigmoid(x)

def _layernorm(x, axis=-1, eps=1e-05):
    m = jnp.mean(x, axis=axis, keepdims=True)
    v = jnp.var(x, axis=axis, keepdims=True)
    return (x - m) / jnp.sqrt(v + eps)

def _scatter_add(tgt, idx, src, axis=0):
    return tgt.at[idx].add(src)

def _segment_sum(src, seg, n):
    return jax.ops.segment_sum(src, seg, n)
kernel_name = 'mk_prb_d1_jaxref_r8_121abf'

def setup_inputs(seed: int=0):
    np.random.seed(seed)
    _w = jnp.asarray

    def _L0_attn_setup():
        import jax, jax.numpy as jnp
        import numpy as np
        B, T, D = (4, 128, 128)
        H, KVH = (16, 4)
        HD = D // H
        DFF = 512
        WINDOW = 32
        EPS = 1e-05

        def _layernorm(x, g, b):
            mu = jnp.mean(x, axis=-1, keepdims=True)
            var = jnp.mean(jnp.square(x - mu), axis=-1, keepdims=True)
            return (x - mu) * jax.lax.rsqrt(var + EPS) * g + b

        def _rope(x):
            half = HD // 2
            theta = 1.0 / 10000.0 ** (jnp.arange(half, dtype=jnp.float32) / half)
            pos = jnp.arange(x.shape[2], dtype=jnp.float32)
            freqs = jnp.outer(pos, theta)
            cos_f, sin_f = (jnp.cos(freqs), jnp.sin(freqs))
            x1, x2 = (x[..., :half], x[..., half:])
            return jnp.concatenate([x1 * cos_f - x2 * sin_f, x2 * cos_f + x1 * sin_f], axis=-1)
        key = jax.random.key(seed)
        ks = jax.random.split(key, 16)
        s = 0.02
        d = {'x': jax.random.normal(ks[0], (B, T, D), dtype=jnp.float32), 'Wq': jax.random.normal(ks[1], (D, H * HD), dtype=jnp.float32) * s, 'bq': jnp.zeros((H * HD,), jnp.float32), 'Wk': jax.random.normal(ks[2], (D, KVH * HD), dtype=jnp.float32) * s, 'bk': jnp.zeros((KVH * HD,), jnp.float32), 'Wv': jax.random.normal(ks[3], (D, KVH * HD), dtype=jnp.float32) * s, 'bv': jnp.zeros((KVH * HD,), jnp.float32), 'Wo': jax.random.normal(ks[4], (D, D), dtype=jnp.float32) * s, 'bo': jnp.zeros((D,), jnp.float32), 'g1': jnp.ones((D,), jnp.float32), 'b1': jnp.zeros((D,), jnp.float32), 'Wf1': jax.random.normal(ks[5], (D, DFF), dtype=jnp.float32) * s, 'bf1': jnp.zeros((DFF,), jnp.float32), 'Wf2': jax.random.normal(ks[6], (DFF, D), dtype=jnp.float32) * s, 'bf2': jnp.zeros((D,), jnp.float32), 'g2': jnp.ones((D,), jnp.float32), 'b2': jnp.zeros((D,), jnp.float32)}
        return d
    _L0_attn_in = _L0_attn_setup()

    def _L0_ffn_setup():
        import jax, jax.numpy as jnp
        import numpy as np
        E = 8
        H = 128
        F = 448
        JITTER_EPS = 0.01

        def _route(scores):
            vals, idx = jax.lax.top_k(scores, 2)
            neg_inf = -jnp.inf
            t1 = vals[:, 0:1]
            factor1 = jnp.maximum(jnp.abs(scores), t1)
            mask1 = (t1 - scores) / factor1 > 2 * JITTER_EPS
            p1 = jax.nn.softmax(jnp.where(mask1, neg_inf, scores), axis=-1)
            mult1 = jnp.take_along_axis(p1, idx[:, 0:1], axis=-1)
            t2 = vals[:, 1:2]
            factor2 = jnp.maximum(jnp.abs(scores), t2)
            mask2 = (t2 - scores) / factor2 > 2 * JITTER_EPS
            onehot0 = jax.nn.one_hot(idx[:, 0], scores.shape[-1], dtype=bool)
            scores2 = jnp.where(onehot0, neg_inf, scores)
            p2 = jax.nn.softmax(jnp.where(mask2, neg_inf, scores2), axis=-1)
            mult2 = jnp.take_along_axis(p2, idx[:, 1:2], axis=-1)
            return (jnp.concatenate([mult1, mult2], axis=-1), idx)
        key = jax.random.key(seed)
        ks = jax.random.split(key, 5)
        hidden_states = jax.random.normal(ks[0], (2, 128, H), jnp.float32)
        gate_w = jax.random.normal(ks[1], (E, H), jnp.float32) * 0.02
        w1 = jax.random.normal(ks[2], (E, F, H), jnp.float32) * 0.02
        w2 = jax.random.normal(ks[3], (E, H, F), jnp.float32) * 0.02
        w3 = jax.random.normal(ks[4], (E, F, H), jnp.float32) * 0.02
        return {'hidden_states': hidden_states, 'gate_w': gate_w, 'w1': w1, 'w2': w2, 'w3': w3}
    _L0_ffn_in = _L0_ffn_setup()
    _d = {'L0_attn_x': _L0_attn_in['x'], 'L0_attn_Wq': _L0_attn_in['Wq'], 'L0_attn_bq': _L0_attn_in['bq'], 'L0_attn_Wk': _L0_attn_in['Wk'], 'L0_attn_bk': _L0_attn_in['bk'], 'L0_attn_Wv': _L0_attn_in['Wv'], 'L0_attn_bv': _L0_attn_in['bv'], 'L0_attn_Wo': _L0_attn_in['Wo'], 'L0_attn_bo': _L0_attn_in['bo'], 'L0_attn_g1': _L0_attn_in['g1'], 'L0_attn_b1': _L0_attn_in['b1'], 'L0_attn_Wf1': _L0_attn_in['Wf1'], 'L0_attn_bf1': _L0_attn_in['bf1'], 'L0_attn_Wf2': _L0_attn_in['Wf2'], 'L0_attn_bf2': _L0_attn_in['bf2'], 'L0_attn_g2': _L0_attn_in['g2'], 'L0_attn_b2': _L0_attn_in['b2'], 'L0_ffn_gate_w': _L0_ffn_in['gate_w'], 'L0_ffn_w1': _L0_ffn_in['w1'], 'L0_ffn_w2': _L0_ffn_in['w2'], 'L0_ffn_w3': _L0_ffn_in['w3']}
    _x0 = _d['L0_attn_x']
    _d['L0_attn_x'] = jax.random.normal(jax.random.fold_in(jax.random.key(seed), 1), (16, 256, 128), dtype=_x0.dtype)
    del _x0
    return _d

def reference(L0_attn_x, L0_attn_Wq, L0_attn_bq, L0_attn_Wk, L0_attn_bk, L0_attn_Wv, L0_attn_bv, L0_attn_Wo, L0_attn_bo, L0_attn_g1, L0_attn_b1, L0_attn_Wf1, L0_attn_bf1, L0_attn_Wf2, L0_attn_bf2, L0_attn_g2, L0_attn_b2, L0_ffn_gate_w, L0_ffn_w1, L0_ffn_w2, L0_ffn_w3):

    def _L0_attn_ref(x, Wq, bq, Wk, bk, Wv, bv, Wo, bo, g1, b1, Wf1, bf1, Wf2, bf2, g2, b2):
        import jax, jax.numpy as jnp
        import numpy as np
        B, T, D = (4, 128, 128)
        H, KVH = (16, 4)
        HD = D // H
        DFF = 512
        WINDOW = 32
        EPS = 1e-05

        def _layernorm(x, g, b):
            mu = jnp.mean(x, axis=-1, keepdims=True)
            var = jnp.mean(jnp.square(x - mu), axis=-1, keepdims=True)
            return (x - mu) * jax.lax.rsqrt(var + EPS) * g + b

        def _rope(x):
            half = HD // 2
            theta = 1.0 / 10000.0 ** (jnp.arange(half, dtype=jnp.float32) / half)
            pos = jnp.arange(x.shape[2], dtype=jnp.float32)
            freqs = jnp.outer(pos, theta)
            cos_f, sin_f = (jnp.cos(freqs), jnp.sin(freqs))
            x1, x2 = (x[..., :half], x[..., half:])
            return jnp.concatenate([x1 * cos_f - x2 * sin_f, x2 * cos_f + x1 * sin_f], axis=-1)
        Bt, Tt, _ = x.shape
        h = _layernorm(x, g1, b1)
        q = (h @ Wq + bq).reshape(Bt, Tt, H, HD).transpose(0, 2, 1, 3)
        k = (h @ Wk + bk).reshape(Bt, Tt, KVH, HD).transpose(0, 2, 1, 3)
        v = (h @ Wv + bv).reshape(Bt, Tt, KVH, HD).transpose(0, 2, 1, 3)
        group = H // KVH
        k = jnp.repeat(k, group, axis=1)
        v = jnp.repeat(v, group, axis=1)
        q, k = (_rope(q), _rope(k))
        scores = jnp.einsum('bhqd,bhkd->bhqk', q, k) / jnp.sqrt(jnp.float32(HD))
        row = jnp.arange(Tt)[:, None]
        col = jnp.arange(Tt)[None, :]
        valid = (col <= row) & (row - col < WINDOW)
        scores = jnp.where(valid, scores, jnp.float32(-1000000000.0))
        attn = jax.nn.softmax(scores, axis=-1)
        out = jnp.einsum('bhqk,bhkd->bhqd', attn, v)
        out = out.transpose(0, 2, 1, 3).reshape(Bt, Tt, D)
        x = x + (out @ Wo + bo)
        h2 = _layernorm(x, g2, b2)
        ff = jax.nn.gelu(h2 @ Wf1 + bf1, approximate=False) @ Wf2 + bf2
        return x + ff

    def _L0_ffn_ref(hidden_states, gate_w, w1, w2, w3):
        import jax, jax.numpy as jnp
        import numpy as np
        E = 8
        H = 128
        F = 448
        JITTER_EPS = 0.01

        def _route(scores):
            vals, idx = jax.lax.top_k(scores, 2)
            neg_inf = -jnp.inf
            t1 = vals[:, 0:1]
            factor1 = jnp.maximum(jnp.abs(scores), t1)
            mask1 = (t1 - scores) / factor1 > 2 * JITTER_EPS
            p1 = jax.nn.softmax(jnp.where(mask1, neg_inf, scores), axis=-1)
            mult1 = jnp.take_along_axis(p1, idx[:, 0:1], axis=-1)
            t2 = vals[:, 1:2]
            factor2 = jnp.maximum(jnp.abs(scores), t2)
            mask2 = (t2 - scores) / factor2 > 2 * JITTER_EPS
            onehot0 = jax.nn.one_hot(idx[:, 0], scores.shape[-1], dtype=bool)
            scores2 = jnp.where(onehot0, neg_inf, scores)
            p2 = jax.nn.softmax(jnp.where(mask2, neg_inf, scores2), axis=-1)
            mult2 = jnp.take_along_axis(p2, idx[:, 1:2], axis=-1)
            return (jnp.concatenate([mult1, mult2], axis=-1), idx)
        B, S, Hd = hidden_states.shape
        x = hidden_states.reshape(-1, Hd)
        scores = x @ gate_w.T
        mult, idx = _route(scores)
        g = (jax.nn.one_hot(idx, E, dtype=x.dtype) * mult[..., None]).sum(axis=1)
        h1 = jnp.einsum('th,efh->tef', x, w1)
        h3 = jnp.einsum('th,efh->tef', x, w3)
        inter = jax.nn.silu(h1) * h3 * g[:, :, None]
        y = jnp.einsum('tef,ehf->th', inter, w2)
        return y.reshape(B, S, Hd)
    x = L0_attn_x
    xn = _layernorm(x, axis=-1)
    x = x + _L0_attn_ref(xn, L0_attn_Wq, L0_attn_bq, L0_attn_Wk, L0_attn_bk, L0_attn_Wv, L0_attn_bv, L0_attn_Wo, L0_attn_bo, L0_attn_g1, L0_attn_b1, L0_attn_Wf1, L0_attn_bf1, L0_attn_Wf2, L0_attn_bf2, L0_attn_g2, L0_attn_b2) + _L0_ffn_ref(xn, L0_ffn_gate_w, L0_ffn_w1, L0_ffn_w2, L0_ffn_w3)
    return x

_drawn_inputs = setup_inputs


def setup_inputs(seed=0):
    import zlib

    import numpy as np

    out = dict(_drawn_inputs(seed))
    spreads = {'L0_attn_bq': (0.0, 0.8),
     'L0_attn_bk': (0.0, 0.8),
     'L0_attn_bv': (0.0, 0.532),
     'L0_attn_bo': (0.0, 0.69),
     'L0_attn_g1': (1.0, 0.6),
     'L0_attn_b1': (0.0, 0.8),
     'L0_attn_bf1': (0.0, 2.0),
     'L0_attn_bf2': (0.0, 0.644),
     'L0_attn_g2': (1.0, 0.6),
     'L0_attn_b2': (0.0, 2.0)}
    factors = {'L0_attn_Wq': 8.0,
     'L0_attn_Wk': 8.0,
     'L0_attn_Wv': 8.0,
     'L0_attn_Wo': 3.625,
     'L0_ffn_gate_w': 8.0,
     'L0_ffn_w1': 7.415,
     'L0_ffn_w2': 7.36,
     'L0_ffn_w3': 7.356,
     'L0_attn_Wf1': 4.753}
    for name, (base, spread) in spreads.items():
        noise = np.random.default_rng([zlib.crc32(name.encode()), seed]).standard_normal(out[name].shape)
        drawn = base * np.exp(spread * noise) if base else spread * noise
        out[name] = jnp.asarray(drawn.astype(out[name].dtype))
    for name, factor in factors.items():
        out[name] = (out[name] * factor).astype(out[name].dtype)
    return out
```

```python
from contextlib import ExitStack

import numpy as np

import concourse.bass as bass
from concourse import mybir

P = 128
B, T, D = 16, 256, 128
NTOK = B * T
NT = NTOK // P
TPB = T // P
NH, NKV, HD = 16, 4, 8
G = NH // NKV
WIN = 32
NBLK = T // WIN
KW = 2 * WIN
DFF = 512
FC = DFF // P
E, FE = 8, 448
EC = 4
FP = FE // EC
ESTRIDE = 512
LEAD = 4
TILES = 6
SLOT_TILES = TILES * (B - LEAD)
assert SLOT_TILES >= (2 * NTOK + E * (P - 1)) // P
EPS = 1e-5
JITTER2 = 0.02
GROUPS_A = NT // 4
VW = NKV * HD + NKV
NEG = -1e30


def layer(nc, x, wqkv, bqkv, wo, bo, g1, b1, g2, b2, wf1, bf1, wf2, bf2, gate, w1, w3, w2,
          ident, cosf, sinf, maskadd, qmask, vmask, tri, rev, tilegrid, xs, ys, out):
    F32, BF16, I32 = mybir.dt.float32, mybir.dt.bfloat16, mybir.dt.int32
    ALU, ACT, AX = mybir.AluOpType, mybir.ActivationFunctionType, mybir.AxisListType
    ds = bass.ds
    ctx = ExitStack()
    with ctx:
        def sb(name, shape, dt=F32):
            return ctx.enter_context(nc.sbuf_tensor(name, shape, dt))[:]

        def sem(name):
            return ctx.enter_context(nc.semaphore(name))

        x_sb = sb("x_sb", [P, NT, D])
        xn_sb = sb("xn_sb", [P, NT, D])
        x1_sb = sb("x1_sb", [P, NT, D])
        h2T_sb = sb("h2T_sb", [P, NTOK])
        w1_sb = sb("w1_sb", [P, E * ESTRIDE])
        w3_sb = sb("w3_sb", [P, E * ESTRIDE])
        w2_sb = sb("w2_sb", [FP, E * ESTRIDE])
        wqkv_sb = sb("wqkv_sb", [P, 192])
        bqkv_sb = sb("bqkv_sb", [P, 192])
        wo_sb = sb("wo_sb", [P, D])
        bo_sb = sb("bo_sb", [P, D])
        bf2_sb = sb("bf2_sb", [P, D])
        wf1_sb = sb("wf1_sb", [P, DFF])
        wf2_sb = sb("wf2_sb", [P, FC, D])
        cols_sb = sb("cols_sb", [P, 4 + FC])
        gate_sb = sb("gate_sb", [P, E])
        ident_sb = sb("ident_sb", [P, P])
        identb_sb = sb("identb_sb", [P, P], BF16)
        maskb_sb = sb("maskb_sb", [P, NBLK * KW], BF16)
        cos_sb = sb("cos_sb", [P, TPB * 160])
        sin_sb = sb("sin_sb", [P, TPB * 160])
        qmask_sb = sb("qmask_sb", [P, NKV])
        vmask_sb = sb("vmask_sb", [P, VW])
        tri_sb = sb("tri_sb", [P, P])
        ones_sb = sb("ones_sb", [P, P])
        rev_sb = sb("rev_sb", [P, E])
        grid_sb = sb("grid_sb", [P, SLOT_TILES * 7])
        zero_sb = sb("zero_sb", [P, 8 * D])
        nhalf_sb = sb("nhalf_sb", [P, 4])
        eps_sb = sb("eps_sb", [P, 4])
        spare_sb = sb("spare_sb", [P, 8])

        stA = sb("stA", [P, 4, 6])
        mvA = sb("mvA", [P, 2, 4, 2])
        veA = sb("veA", [P, 4])
        rsA = sb("rsA", [P, 2, 4])
        xnst = sb("xnst", [P, 2, 4, D])
        stB = sb("stB", [P, 4, 6])
        mvB = sb("mvB", [P, 2, 4, 2])
        veB = sb("veB", [P, 4])
        mu2_sb = sb("mu2_sb", [P, NT])
        rs2_sb = sb("rs2_sb", [P, NT])
        xnT = sb("xnT", [P, 2, 512])

        arena = sb("arena", [P, 2 * 2 * NBLK * G * WIN])
        used = [0]

        def table(*shape):
            n = int(np.prod(shape))
            used[0] += n
            names = "abcd"[:len(shape)]
            flat = arena[:, used[0] - n:used[0]]
            return flat.rearrange(f"p ({' '.join(names)}) -> p {' '.join(names)}", **dict(zip(names, shape)))

        sc = table(NT, E)
        oh = table(2, NT, E)
        top = table(2, NT)
        tmp = table(2, NT, E)
        dist = table(2, NT, E)
        keep = table(2, NT, E)
        pick = table(NT)
        asum = table(NT, E)
        tot = table(NT, E)
        incl = table(NT, E)
        slotm = table(NT, E)
        cnt = sb("cnt", [P, 3, E])
        mult = sb("mult", [P, NT, 2])
        slotf = sb("slotf", [P, NT, 2])
        slot = sb("slot", [P, NT, 2], I32)
        tef = sb("tef", [P, SLOT_TILES])
        te = sb("te", [P, SLOT_TILES], I32)
        past = table(SLOT_TILES * 7)

        hbuf = sb("hbuf", [P, TPB, D])
        hT = sb("hT", [P, T])
        qkb = sb("qkb", [P, TPB, 160])
        vb = sb("vb", [P, TPB, G, 32])
        ra = sb("ra", [P, TPB, 160])
        rb = sb("rb", [P, TPB, 160])
        qr = sb("qr", [P, TPB, P])
        kr = sb("kr", [P, TPB, G, 32])
        kT = sb("kT", [P, 2, WIN + T])
        qbd = sb("qbd", [P, 2, NBLK, NKV, WIN])
        vt = sb("vt", [P, T])
        vbd = sb("vbd", [P, 2, NBLK + 1, VW])
        rmax = sb("rmax", [P, G, NBLK])
        S = sb("S", [P, G, NBLK * KW])
        pT = arena.rearrange("p (b n g q) -> p b n g q", b=2, n=2 * NBLK, g=G)
        rsum = sb("rsum", [P, NBLK, NKV])
        on = sb("on", [P, T])
        outT = sb("outT", [P, T])
        st2 = sb("st2", [P, TPB, 6])
        mv2 = sb("mv2", [P, TPB, 2])
        ve2 = sb("ve2", [P, TPB])
        rstd2 = sb("rstd2", [P, TPB])
        h2 = sb("h2", [P, TPB, D])
        xstage = sb("xstage", [P, 2, 4, D])
        istage = sb("istage", [P, 2, 8], I32)

        xsb = sb("xsb", [P, 2, D])
        xsT = sb("xsT", [P, 2, P])
        act1 = sb("act1", [P, 2, FE])
        inter = sb("inter", [P, 2, FE])
        iT = xnT[0:FP]
        ysb = sb("ysb", [P, 2, D])

        gT = arena.rearrange("p (b c n) -> p b c n", b=2, c=FC)
        gidx = sb("gidx", [P, 2, 8], I32)
        grow = S.rearrange("p g (a d) -> p (g a) d", d=D).rearrange("p (b n) d -> p b n d", b=2)
        osb = zero_sb.rearrange("p (b t d) -> p b t d", b=2, t=4)

        bank = [ctx.enter_context(nc.psum_tensor(f"bank{i}", [P, 512], F32))[:] for i in range(8)]
        qkv_bank, turn_bank = bank[2], bank[3]
        h1_bank, h3_bank, iT_bank, y_bank = bank[4:8]

        small_in, x_in, weights_in = sem("small_in"), [sem(f"x_in{i}") for i in range(2)], sem("weights_in")
        mask_in = sem("mask_in")
        zeros_set, pool_consts, consts_set = sem("zeros_set"), sem("pool_consts"), sem("consts_set")
        xs_zeroed = sem("xs_zeroed")
        stats_a, aggr_a, rstd_a, var_a = sem("stats_a"), sem("aggr_a"), sem("rstd_a"), sem("var_a")
        xn_ready, stats_b, aggr_b, rstd_b, var_b = (sem("xn_ready"), sem("stats_b"), sem("aggr_b"),
                                                    sem("rstd_b"), sem("var_b"))
        xn_kept, xb_kept = sem("xn_kept"), sem("xb_kept")
        xnT_psum, xnT_ready, gate_psum, gate_kept = (sem("xnT_psum"), sem("xnT_ready"),
                                                     sem("gate_psum"), sem("gate_kept"))
        route_chain, route_exp, ranks_psum, pairs_ready = (sem("route_chain"), sem("route_exp"),
                                                           sem("ranks_psum"), sem("pairs_ready"))
        dist_ready, slots_ready, experts_ready, mult_ready = (sem("dist_ready"), sem("slots_ready"),
                                                              sem("experts_ready"), sem("mult_ready"))
        h_ready, hT_psum, hT_ready, qkv_psum, qkv_biased = (sem("h_ready"), sem("hT_psum"), sem("hT_ready"),
                                                            sem("qkv_psum"), sem("qkv_biased"))
        rope_parts, rope_ready, heads_psum, kT_ready, qbd_ready = (sem("rope_parts"), sem("rope_ready"),
                                                                   sem("heads_psum"), sem("kT_ready"), sem("qbd_ready"))
        vt_ready, vbd_ready, scores_psum, rowmax_ready, shifted = (sem("vt_ready"), sem("vbd_ready"),
                                                                   sem("scores_psum"), sem("rowmax_ready"), sem("shifted"))
        exp_ready, pT_ready, pv_psum, rsum_ready, pv_normed = (sem("exp_ready"), sem("pT_ready"), sem("pv_psum"),
                                                               sem("rsum_ready"), sem("pv_normed"))
        outT_ready, wo_psum, x1_ready, stats_2, aggr_2, var_2, rstd_2 = (
            sem("outT_ready"), sem("wo_psum"), sem("x1_ready"), sem("stats_2"), sem("aggr_2"), sem("var_2"), sem("rstd_2"))
        h2_ready, h2T_psum, h2T_ready = sem("h2_ready"), sem("h2T_psum"), sem("h2T_ready")
        staged, scattered = [sem(f"staged{i}") for i in range(2)], [sem(f"scattered{i}") for i in range(2)]
        slots_in = [sem(f"slots_in{i}") for i in range(2)]
        xsT_psum, xsT_ready, h1_psum, h3_psum = sem("xsT_psum"), sem("xsT_ready"), sem("h1_psum"), sem("h3_psum")
        silu_ready, inter_ready, iT_psum, iT_ready = sem("silu_ready"), sem("inter_ready"), sem("iT_psum"), sem("iT_ready")
        y_psum, y_ready, y_stored = sem("y_psum"), sem("y_ready"), [sem(f"y_stored{i}") for i in range(2)]
        resid_part, resid_ready = sem("resid_part"), sem("resid_ready")
        up_psum, gelu_ready, down_psum, ff_added = sem("up_psum"), sem("gelu_ready"), sem("down_psum"), sem("ff_added")
        gidx_ready, gathered = sem("gidx_ready"), [sem(f"gathered{i}") for i in range(2)]
        first_added, combined, stored = sem("first_added"), sem("combined"), [sem(f"stored{i}") for i in range(2)]

        g1c, b1c, g2c, b2c = (cols_sb[:, i:i + 1] for i in range(4))
        N_SMALL = 21

        spare_column = {s: i for i, s in enumerate(("aggr_a", "stats_a", "stats_b", "x1_ready", "stats_2",
                                                    "staged0", "staged1", "gidx_ready"))}

        def spare_of(name):
            return spare_sb[:, spare_column[name]:spare_column[name] + 1]

        def wait_apart_dve(name, semaphore, value):
            nc.vector.wait_ge(semaphore, value)
            nc.vector.memset(spare_of(name), 0.0)

        def wait_apart_pool(name, semaphore, value):
            nc.gpsimd.wait_ge(semaphore, value)
            nc.gpsimd.tensor_tensor(spare_of(name), eps_sb[:, 0:1], eps_sb[:, 0:1], ALU.add)

        def bc(ap, shape):
            return ap.broadcast_to(shape)

        def exists(b):
            return not isinstance(b, int) or 0 <= b < B

        def within(j):
            return not isinstance(j, int) or j < SLOT_TILES

        def some(n):
            return not isinstance(n, int) or n > 0

        block = ctx.enter_context(nc.Block())

        @block.sync
        def _(sp):
            xv = x.rearrange("(t p) d -> p t d", p=P)
            for i in range(2):
                half = slice(i * NT // 2, (i + 1) * NT // 2)
                sp.dma_start(x_sb[:, half, :], xv[:, half, :]).then_inc(x_in[i], 16)
            small = [(ident_sb, ident), (gate_sb, gate), (wqkv_sb, wqkv), (bqkv_sb, bqkv), (wo_sb, wo), (bo_sb, bo),
                     (bf2_sb, bf2), (wf1_sb, wf1), (cols_sb[:, 0:1], g1), (cols_sb[:, 1:2], b1), (cols_sb[:, 2:3], g2),
                     (cols_sb[:, 3:4], b2), (cols_sb[:, 4:4 + FC], bf1), (cos_sb, cosf), (sin_sb, sinf),
                     (qmask_sb, qmask), (vmask_sb, vmask), (tri_sb, tri), (rev_sb, rev), (grid_sb, tilegrid),
                     (wf2_sb, wf2.rearrange("p (c d) -> p c d", c=FC))]
            assert len(small) == N_SMALL
            for dst, src in small:
                sp.dma_start(dst, src).then_inc(small_in, 16)
            sp.wait_ge(zeros_set, 1)
            xz = xs.rearrange("(p r) d -> p (r d)", p=P)
            for r0 in range(0, SLOT_TILES, 8):
                n = min(8, SLOT_TILES - r0) * D
                sp.dma_start(xz[:, r0 * D:r0 * D + n], zero_sb[:, 0:n]).then_inc(xs_zeroed, 16)
            for dst, src in ((w1_sb, w1), (w3_sb, w3), (w2_sb, w2)):
                sp.dma_start(dst, src).then_inc(weights_in, 16)

            sp.wait_ge(xn_kept, GROUPS_A)
            sp.wait_ge(slots_ready, 1)

            def stage(i, p):
                group = ds((2 * i + p) * 4, 4)
                if some(i):
                    sp.wait_ge(scattered[p], 8 * 16 * i)
                sp.dma_start(xstage[:, p], xn_sb[:, group, :]).then_inc(staged[p], 16)
                sp.dma_start(istage[:, p], slot[:, group, :].rearrange("p t c -> p (t c)")).then_inc(staged[p], 16)

            for p in range(2):
                stage(0, p)
            with sp.Fori(1, GROUPS_A // 2) as i:
                for p in range(2):
                    stage(i, p)
            for p in range(2):
                sp.wait_ge(scattered[p], 8 * 16 * GROUPS_A // 2)

            def load_slots(j, p, first=False):
                if not first:
                    sp.wait_ge(xsT_psum, j - 1)
                sp.dma_start(xsb[:, p, :], xs[ds(j * P, P), :]).then_inc(slots_in[p], 16)

            load_slots(0, 0, first=True)
            load_slots(1, 1, first=True)
            with sp.Fori(0, (SLOT_TILES - 2) // 2) as i:
                load_slots(2 * i + 2, 0)
                load_slots(2 * i + 3, 1)

            ov = out.rearrange("(t p) d -> p t d", p=P)
            with sp.Fori(0, GROUPS_A // 2) as i:
                for p in range(2):
                    sp.wait_ge(combined, 2 * i + p + 1)
                    sp.dma_start(ov[:, ds((2 * i + p) * 4, 4), :], osb[:, p]).then_inc(stored[p], 16)
            for p in range(2):
                sp.wait_ge(stored[p], 16 * GROUPS_A // 2)

        @block.gpsimd
        def _(pool):
            nc.gpsimd.memset(zero_sb, 0.0).then_inc(zeros_set, 1)
            nc.gpsimd.memset(eps_sb, EPS)
            nc.gpsimd.memset(nhalf_sb, -0.5).then_inc(pool_consts, 1)
            pool.wait_ge(small_in, 16 * N_SMALL)
            pool.wait_ge(pool_consts, 1)

            def group_a1(g, p, first):
                pool.wait_ge(aggr_a, g + 1)
                pool.wait_ge(rstd_a, g)
                nc.gpsimd.tensor_tensor(veA, mvA[:, p, :, 1], eps_sb, ALU.add).then_inc(var_a, 1)
                pool.wait_ge(var_a, g + 1)
                if not first:
                    pool.wait_ge(xn_ready, g - 1)
                nc.gpsimd.tensor_tensor(rsA[:, p, :], veA, nhalf_sb, ALU.pow).then_inc(rstd_a, 1)

            def group_a2(g, p):
                pool.wait_ge(aggr_b, g + 1)
                pool.wait_ge(rstd_b, g)
                nc.gpsimd.tensor_tensor(veB, mvB[:, p, :, 1], eps_sb, ALU.add).then_inc(var_b, 1)
                pool.wait_ge(var_b, g + 1)
                nc.gpsimd.tensor_tensor(rs2_sb[:, ds(g * 4, 4)], veB, nhalf_sb, ALU.pow)
                nc.gpsimd.tensor_copy(mu2_sb[:, ds(g * 4, 4)], mvB[:, p, :, 0]).then_inc(rstd_b, 1)
                nc.gpsimd.tensor_tensor(x1_sb[:, ds(g * 4, 4), :], xnst[:, p],
                                        bc(bo_sb.rearrange("p (a d) -> p a d", a=1), [P, 4, D]),
                                        ALU.add).then_inc(xb_kept, 1)

            group_a1(0, 0, True)
            group_a1(1, 1, True)
            group_a2(0, 0)
            with pool.Fori(0, (GROUPS_A - 2) // 2) as i:
                group_a1(2 * i + 2, 0, False)
                group_a2(2 * i + 1, 1)
                group_a1(2 * i + 3, 1, False)
                group_a2(2 * i + 2, 0)
            group_a2(GROUPS_A - 1, 1)

            def rope(b):
                pool.wait_ge(qkv_biased, b + 1)
                flat = "p t c -> p (t c)"
                q4 = qkb.rearrange("p t (n h c) -> p (t n) h c", h=2, c=HD // 2)
                s4 = sin_sb.rearrange("p (n h c) -> p n h c", h=2, c=HD // 2)
                r4 = rb.rearrange("p t (n h c) -> p (t n) h c", h=2, c=HD // 2)
                nc.gpsimd.tensor_tensor(ra.rearrange(flat), qkb.rearrange(flat), cos_sb, ALU.mult)
                nc.gpsimd.tensor_tensor(r4[:, :, 0, :], q4[:, :, 1, :], s4[:, :, 0, :], ALU.mult)
                nc.gpsimd.tensor_tensor(r4[:, :, 1, :], q4[:, :, 0, :], s4[:, :, 1, :], ALU.mult).then_inc(rope_parts, 1)
                pool.wait_ge(rope_parts, b + 1)
                if some(b):
                    pool.wait_ge(heads_psum, b)
                nc.gpsimd.tensor_tensor(qr, ra[:, :, 0:P], rb[:, :, 0:P], ALU.add)
                for t in range(TPB):
                    last = nc.gpsimd.tensor_tensor(
                        kr[:, t], bc(ra[:, t, P:160].rearrange("p (a c) -> p a c", a=1), [P, G, 32]),
                        bc(rb[:, t, P:160].rearrange("p (a c) -> p a c", a=1), [P, G, 32]), ALU.add)
                last.then_inc(rope_ready, 1)

            def rstd2_of(b):
                pool.wait_ge(aggr_2, 2 * b + 2)
                nc.gpsimd.tensor_tensor(ve2, mv2[:, :, 1], eps_sb[:, 0:TPB], ALU.add).then_inc(var_2, 1)
                pool.wait_ge(var_2, b + 1)
                nc.gpsimd.tensor_tensor(rstd2, ve2, nhalf_sb[:, 0:TPB], ALU.pow).then_inc(rstd_2, 1)

            def scatter(i, p):
                wait_apart_pool(f"staged{p}", staged[p], 32 * i + 32)
                for t in range(4):
                    for c in range(2):
                        nc.gpsimd.indirect_dma_start(
                            xs, bass.IndirectOffsetOnAxis(ap=istage[:, p, 2 * t + c:2 * t + c + 1], axis=0),
                            xstage[:, p, t, :], None).then_inc(scattered[p], 16)

            def step(k):
                if exists(k - 2):
                    rstd2_of(k - 2)
                if exists(k + 2):
                    rope(k + 2)

            pool.wait_ge(xn_kept, GROUPS_A)
            rope(0)
            rope(1)
            pool.wait_ge(slots_ready, 1)
            pool.wait_ge(xs_zeroed, 16 * ((SLOT_TILES + 7) // 8))
            for k in range(LEAD):
                step(k)
                with pool.Fori(k * GROUPS_A // 2 // LEAD, (k + 1) * GROUPS_A // 2 // LEAD) as i:
                    for p in range(2):
                        scatter(i, p)
            with pool.Fori(LEAD, B - 3) as k:
                step(k)
            for k in range(B - 3, B + 2):
                step(k)

            pool.wait_ge(x1_ready, B)
            flat = "p t d -> p (t d)"
            nc.gpsimd.tensor_tensor(x_sb.rearrange(flat), x_sb.rearrange(flat), x1_sb.rearrange(flat),
                                    ALU.add).then_inc(resid_part, 1)
            pool.wait_ge(resid_part, 1)
            nc.gpsimd.tensor_tensor(x_sb, x_sb, bc(bf2_sb.rearrange("p (a d) -> p a d", a=1), [P, NT, D]),
                                    ALU.add).then_inc(resid_ready, 1)

            for p in range(2):
                pool.wait_ge(y_stored[p], 16 * ((SLOT_TILES + 1 - p) // 2))

            def gather(i, p, first):
                if not first:
                    pool.wait_ge(gathered[p], 64 * (i - p))
                    pool.wait_ge(combined, i - 1)
                nc.gpsimd.tensor_copy(gidx[:, p, :], slot[:, ds(4 * i, 4), :].rearrange("p t c -> p (t c)")).then_inc(gidx_ready, 1)
                wait_apart_pool("gidx_ready", gidx_ready, i + 1)
                for n in range(8):
                    nc.gpsimd.indirect_dma_start(
                        grow[:, p, n, :], None, ys, bass.IndirectOffsetOnAxis(ap=gidx[:, p, n:n + 1], axis=0)
                    ).then_inc(gathered[p], 16)

            for p in range(2):
                gather(p, p, True)
            with pool.Fori(1, GROUPS_A // 2) as i:
                for p in range(2):
                    gather(2 * i + p, p, False)

        @block.vector
        def _(dve):
            nc.vector.memset(ones_sb, 1.0)
            nc.vector.memset(kT[:, :, 0:WIN], 0.0)
            for p in range(2):
                last = nc.vector.memset(vbd[:, p, 0, :], 0.0)
            last.then_inc(consts_set, 1)
            dve.wait_ge(small_in, 16 * N_SMALL)
            nc.vector.tensor_copy(identb_sb, ident_sb)
            for p in range(2):
                last = nc.vector.tensor_copy(
                    vbd[:, p, 1:NBLK + 1, NKV * HD:VW],
                    bc(vmask_sb[:, NKV * HD:VW].rearrange("p (a c) -> p a c", a=1), [P, NBLK, NKV]))
            last.then_inc(consts_set, 1)

            def stats_of_x(g, p, first):
                wait_apart_dve("aggr_a", aggr_a, g)
                for j in range(4):
                    last = nc.vector.bn_stats(stA[:, j, :], x_sb[:, ds(4 * g + j, 1), :].rearrange("p a d -> p (a d)"))
                last.then_inc(stats_a, 1)
                wait_apart_dve("stats_a", stats_a, g + 1)
                for j in range(4):
                    last = nc.vector.bn_aggr(mvA[:, p, j, :], stA[:, j, :])
                last.then_inc(aggr_a, 1)

            def normalise(g, p, first):
                dve.wait_ge(rstd_a, g + 1)
                if not first:
                    dve.wait_ge(xnT_psum, g - 1)
                    dve.wait_ge(xn_kept, g - 1)
                    dve.wait_ge(xb_kept, g - 1)
                for j in range(4):
                    last = nc.vector.tensor_scalar(
                        xnst[:, p, j, :], x_sb[:, ds(4 * g + j, 1), :].rearrange("p a d -> p (a d)"),
                        mvA[:, p, j, 0:1], rsA[:, p, j:j + 1], ALU.subtract, ALU.mult)
                last.then_inc(xn_ready, 1)
                dve.wait_ge(aggr_b, g)
                dve.wait_ge(xn_ready, g + 1)
                for j in range(4):
                    last = nc.vector.bn_stats(stB[:, j, :], xnst[:, p, j, :])
                last.then_inc(stats_b, 1)
                wait_apart_dve("stats_b", stats_b, g + 1)
                for j in range(4):
                    last = nc.vector.bn_aggr(mvB[:, p, j, :], stB[:, j, :])
                last.then_inc(aggr_b, 1)

            def keep_scores(g, p):
                dve.wait_ge(gate_psum, g + 1)
                nc.vector.tensor_copy(sc[:, ds(4 * g, 4), :].rearrange("p t e -> p (t e)"),
                                      bank[2 + p][:, 0:4 * E]).then_inc(gate_kept, 1)

            dve.wait_ge(x_in[0], 16)
            dve.wait_ge(x_in[1], 16)
            stats_of_x(0, 0, True)
            stats_of_x(1, 1, True)
            normalise(0, 0, True)
            stats_of_x(2, 0, False)
            normalise(1, 1, True)
            with dve.Fori(0, (GROUPS_A - 4) // 2) as i:
                stats_of_x(2 * i + 3, 1, False)
                normalise(2 * i + 2, 0, False)
                keep_scores(2 * i, 0)
                stats_of_x(2 * i + 4, 0, False)
                normalise(2 * i + 3, 1, False)
                keep_scores(2 * i + 1, 1)
            g = GROUPS_A - 4
            stats_of_x(g + 3, 1, False)
            normalise(g + 2, 0, False)
            keep_scores(g, 0)
            normalise(g + 3, 1, False)
            for g in range(GROUPS_A - 3, GROUPS_A):
                keep_scores(g, g % 2)

            steps = [0]

            def link(ins):
                steps[0] += 1
                ins.then_inc(route_chain, 1)
                dve.wait_ge(route_chain, steps[0])

            dve.wait_ge(gate_kept, GROUPS_A)
            full = [P, NT, E]

            def per_tok(ap):
                return bc(ap.rearrange("p (t a) -> p t a", a=1), full)

            def per_exp(ap):
                return bc(ap.rearrange("p (a e) -> p a e", a=1), full)

            rest = sc
            for c in range(2):
                link(nc.vector.tensor_reduce(top[:, c, :], rest, AX.X, ALU.max))
                link(nc.vector.tensor_tensor(tmp[:, 0], rest, per_tok(top[:, c, :]), ALU.is_ge))
                link(nc.vector.tensor_tensor(tmp[:, 0], tmp[:, 0], per_exp(rev_sb), ALU.mult))
                link(nc.vector.tensor_reduce(pick, tmp[:, 0], AX.X, ALU.max))
                link(nc.vector.tensor_tensor(oh[:, c], tmp[:, 0], per_tok(pick), ALU.is_equal))
                if c == 0:
                    link(nc.vector.scalar_tensor_tensor(tmp[:, 1], oh[:, 0], -3e38, sc, ALU.mult, ALU.add))
                    rest = tmp[:, 1]
            nc.vector.tensor_tensor(asum, oh[:, 0], oh[:, 1], ALU.add).then_inc(pairs_ready, 1)
            link(nc.vector.scalar_tensor_tensor(tmp[:, 0], sc, -1.0, sc, ALU.mult, ALU.max))
            for c in range(2):
                link(nc.vector.tensor_tensor(dist[:, c], per_tok(top[:, c, :]), sc, ALU.subtract))
                link(nc.vector.tensor_tensor(tmp[:, 1], tmp[:, 0], per_tok(top[:, c, :]), ALU.max))
                link(nc.vector.scalar_tensor_tensor(keep[:, c], tmp[:, 1], JITTER2, dist[:, c], ALU.mult, ALU.is_ge))
            link(nc.vector.tensor_tensor(tmp[:, 0], keep[:, 1], oh[:, 0], ALU.mult))
            link(nc.vector.tensor_tensor(keep[:, 1], keep[:, 1], tmp[:, 0], ALU.subtract))
            nc.vector.tensor_scalar(dist, dist, 0.0, None, ALU.max).then_inc(dist_ready, 1)

            dve.wait_ge(ranks_psum, 1)
            link(nc.vector.tensor_copy(tot.rearrange("p t e -> p (t e)"), bank[6][:, 256:512]))
            for e in range(E):
                last = nc.vector.tensor_tensor_scan(incl[:, :, e], ones_sb[:, 0:NT], tot[:, :, e], 0.0, ALU.mult, ALU.add)
            link(last)
            link(nc.vector.tensor_tensor(slotm, incl, tot, ALU.subtract))
            link(nc.vector.tensor_tensor(slotm.rearrange("p t e -> p (t e)"), bank[6][:, 0:256],
                                         slotm.rearrange("p t e -> p (t e)"), ALU.add))
            link(nc.vector.tensor_scalar(cnt[:, 0, :], incl[:, NT - 1, :], 1.0 / P, (P - 1) / P - 0.498, ALU.mult, ALU.add))
            link(nc.vector.tensor_scalar(cnt[:, 0, :], cnt[:, 0, :], 8388608.0, None, ALU.add))
            link(nc.vector.tensor_scalar(cnt[:, 0, :], cnt[:, 0, :], -8388608.0, None, ALU.add))
            link(nc.vector.tensor_tensor_scan(cnt[:, 1, :], ones_sb[:, 0:E], cnt[:, 0, :], 0.0, ALU.mult, ALU.add))
            link(nc.vector.tensor_tensor(cnt[:, 2, :], cnt[:, 1, :], cnt[:, 0, :], ALU.subtract))
            link(nc.vector.tensor_scalar(cnt[:, 2, :], cnt[:, 2, :], float(P), None, ALU.mult))
            link(nc.vector.tensor_tensor(slotm, slotm, per_exp(cnt[:, 2, :]), ALU.add))
            for c in range(2):
                link(nc.vector.tensor_tensor(tmp[:, c], slotm, oh[:, c], ALU.mult))
                link(nc.vector.tensor_reduce(slotf[:, :, c], tmp[:, c], AX.X, ALU.add))
            nc.vector.tensor_copy(slot, slotf).then_inc(slots_ready, 1)
            grid3 = [P, SLOT_TILES, 7]
            link(nc.vector.tensor_tensor(past.rearrange("p (j e) -> p j e", e=7), grid_sb.rearrange("p (j e) -> p j e", e=7),
                                         bc(cnt[:, 1, 0:7].rearrange("p (a e) -> p a e", a=1), grid3), ALU.is_ge))
            link(nc.vector.tensor_reduce(tef, past.rearrange("p (j e) -> p j e", e=7), AX.X, ALU.add))
            nc.vector.tensor_scalar(te, tef, float(ESTRIDE), None, ALU.mult).then_inc(experts_ready, 1)
            dve.wait_ge(route_exp, 1)
            link(nc.vector.tensor_tensor(tmp, dist, keep, ALU.mult))
            for c in range(2):
                link(nc.vector.tensor_reduce(mult[:, :, c], tmp[:, c], AX.X, ALU.add))
            nc.vector.reciprocal(mult, mult).then_inc(mult_ready, 1)

            def h_of(b):
                if some(b):
                    dve.wait_ge(hT_psum, b)
                for t in range(TPB):
                    row = ds(b * TPB + t, 1)
                    last = nc.vector.tensor_scalar(
                        hbuf[:, t, :], xn_sb[:, row, :].rearrange("p a d -> p (a d)"),
                        mu2_sb[:, row], rs2_sb[:, row], ALU.subtract, ALU.mult)
                last.then_inc(h_ready, 1)

            def bias(b):
                dve.wait_ge(qkv_psum, b + 1)
                if some(b):
                    dve.wait_ge(rope_ready, b)
                    dve.wait_ge(heads_psum, b)
                src = qkv_bank[:, 0:TPB * 192].rearrange("p (t c) -> p t c", t=TPB)
                nc.vector.tensor_tensor(qkb, src[:, :, 0:160],
                                        bc(bqkv_sb[:, 0:160].rearrange("p (a c) -> p a c", a=1), [P, TPB, 160]), ALU.add)
                for t in range(TPB):
                    last = nc.vector.tensor_tensor(
                        vb[:, t], bc(src[:, t, 160:192].rearrange("p (a c) -> p a c", a=1), [P, G, 32]),
                        bc(bqkv_sb[:, 160:192].rearrange("p (a c) -> p a c", a=1), [P, G, 32]), ALU.add)
                last.then_inc(qkv_biased, 1)

            def values_T(b):
                dve.wait_ge(heads_psum, b + 1)
                if some(b):
                    dve.wait_ge(vbd_ready, b)
                nc.vector.transpose(vt, qkv_bank[:, 0:T]).then_inc(vt_ready, 1)

            def values(b, p):
                dve.wait_ge(vt_ready, b + 1)
                if some(b - 1):
                    dve.wait_ge(pv_psum, b - 1)
                nc.vector.tensor_tensor(
                    vbd[:, p, 1:NBLK + 1, 0:NKV * HD], vt.rearrange("p (n c) -> p n c", n=NBLK),
                    bc(vmask_sb[:, 0:NKV * HD].rearrange("p (a c) -> p a c", a=1), [P, NBLK, NKV * HD]),
                    ALU.mult).then_inc(vbd_ready, 1)

            def shift(b, g):
                src = bank[g % 2].rearrange("p (n k) -> p n k", k=KW)
                dve.wait_ge(scores_psum, G * b + g + 1)
                nc.vector.tensor_reduce(rmax[:, g, :], src, AX.X, ALU.max).then_inc(rowmax_ready, 1)
                dve.wait_ge(rowmax_ready, G * b + g + 1)
                if some(b):
                    dve.wait_ge(pT_ready, G * b + g - (G - 1))
                nc.vector.tensor_tensor(S[:, g, :].rearrange("p (n k) -> p n k", k=KW), src,
                                        bc(rmax[:, g, :].rearrange("p (n a) -> p n a", a=1), [P, NBLK, KW]),
                                        ALU.subtract).then_inc(shifted, 1)

            def weights_T(b, p, g):
                dve.wait_ge(exp_ready, G * b + g + 1)
                if some(b - 1):
                    dve.wait_ge(pv_psum, b - 1)
                nc.vector.transpose(pT[:, p, :, g, :], S[:, g, :].rearrange("p (n q) -> p n q", q=WIN)).then_inc(pT_ready, 1)

            def norm(b):
                dve.wait_ge(pv_psum, b + 1)
                pv = turn_bank[:, 0:NBLK * VW].rearrange("p (n c) -> p n c", c=VW)
                nc.vector.reciprocal(rsum, pv[:, :, NKV * HD:VW]).then_inc(rsum_ready, 1)
                dve.wait_ge(rsum_ready, b + 1)
                nc.vector.tensor_tensor(
                    on.rearrange("p (n h d) -> p n h d", h=NKV, d=HD),
                    pv[:, :, 0:NKV * HD].rearrange("p n (h d) -> p n h d", d=HD),
                    bc(rsum.rearrange("p n (h a) -> p n h a", a=1), [P, NBLK, NKV, HD]), ALU.mult).then_inc(pv_normed, 1)
                dve.wait_ge(pv_normed, b + 1)
                nc.vector.transpose(outT, on).then_inc(outT_ready, 1)

            def residual(b):
                dve.wait_ge(wo_psum, b + 1)
                rows = ds(b * TPB, TPB)
                nc.vector.tensor_tensor(x1_sb[:, rows, :], qkv_bank[:, T:2 * T].rearrange("p (t d) -> p t d", t=TPB),
                                        x1_sb[:, rows, :], ALU.add).then_inc(x1_ready, 1)
                wait_apart_dve("x1_ready", x1_ready, b + 1)
                for t in range(TPB):
                    last = nc.vector.bn_stats(st2[:, t, :], x1_sb[:, ds(b * TPB + t, 1), :].rearrange("p a d -> p (a d)"))
                last.then_inc(stats_2, 1)
                if some(b):
                    dve.wait_ge(h2_ready, b)
                wait_apart_dve("stats_2", stats_2, b + 1)
                for t in range(TPB):
                    nc.vector.bn_aggr(mv2[:, t, :], st2[:, t, :]).then_inc(aggr_2, 1)

            def h2_of(b):
                dve.wait_ge(rstd_2, b + 1)
                if some(b):
                    dve.wait_ge(h2T_psum, b)
                for t in range(TPB):
                    last = nc.vector.tensor_scalar(
                        h2[:, t, :], x1_sb[:, ds(b * TPB + t, 1), :].rearrange("p a d -> p (a d)"),
                        mv2[:, t, 0:1], rstd2[:, t:t + 1], ALU.subtract, ALU.mult)
                last.then_inc(h2_ready, 1)

            def gated(j, p):
                dve.wait_ge(h3_psum, j + 1)
                dve.wait_ge(silu_ready, j + 1)
                if some(j - 1):
                    dve.wait_ge(iT_psum, j - 1)
                nc.vector.tensor_tensor(inter[:, p, :], h3_bank[:, 0:FE], act1[:, p, :], ALU.mult).then_inc(inter_ready, 1)

            def inter_T(j, p):
                dve.wait_ge(iT_psum, j + 1)
                if some(j - 1):
                    dve.wait_ge(y_psum, j - 1)
                nc.vector.tensor_copy(iT[:, p, :], iT_bank[0:FP, :]).then_inc(iT_ready, 1)

            def step(k, p, j=None):
                def tile_gated(i):
                    if j is not None:
                        gated(j + i, i % 2)

                def tile_T(i):
                    if j is not None:
                        inter_T(j + i, i % 2)

                if exists(k - 2):
                    norm(k - 2)
                tile_gated(0)
                if exists(k - 1):
                    weights_T(k - 1, 1 - p, 0)
                    weights_T(k - 1, 1 - p, 1)
                tile_T(0)
                if exists(k + 3):
                    h_of(k + 3)
                if exists(k):
                    shift(k, 0)
                tile_gated(1)
                if exists(k + 1):
                    values_T(k + 1)
                if exists(k - 1):
                    weights_T(k - 1, 1 - p, 2)
                tile_T(1)
                if exists(k):
                    shift(k, 1)
                tile_gated(2)
                if exists(k + 2):
                    bias(k + 2)
                if exists(k - 1):
                    weights_T(k - 1, 1 - p, 3)
                tile_T(2)
                if exists(k):
                    shift(k, 2)
                tile_gated(3)
                if exists(k - 2):
                    residual(k - 2)
                tile_T(3)
                if exists(k):
                    shift(k, 3)
                tile_gated(4)
                if exists(k - 2):
                    h2_of(k - 2)
                tile_T(4)
                tile_gated(5)
                if exists(k + 1):
                    values(k + 1, 1 - p)
                tile_T(5)

            dve.wait_ge(xn_kept, GROUPS_A)
            dve.wait_ge(rstd_b, GROUPS_A)
            dve.wait_ge(xb_kept, GROUPS_A)
            dve.wait_ge(consts_set, 2)
            h_of(0)
            h_of(1)
            bias(0)
            h_of(2)
            values_T(0)
            bias(1)
            values(0, 0)
            for k in range(LEAD):
                step(k, k % 2)
            step(LEAD, LEAD % 2, 0)
            with dve.Fori(0, (B - 4 - LEAD) // 2) as i:
                step(2 * i + LEAD + 1, (LEAD + 1) % 2, (2 * i + 1) * TILES)
                step(2 * i + LEAD + 2, LEAD % 2, (2 * i + 2) * TILES)
            for k in range(B - 3, B):
                step(k, k % 2, (k - LEAD) * TILES)
            for k in range(B, B + 2):
                step(k, k % 2)

            def finish(i, p, first):
                dve.wait_ge(down_psum, i + 1)
                if not first:
                    dve.wait_ge(stored[p], 8 * (i - p))
                nc.vector.tensor_tensor(osb[:, p], bank[p].rearrange("p (t d) -> p t d", t=4),
                                        x_sb[:, ds(4 * i, 4), :], ALU.add).then_inc(ff_added, 1)
                dve.wait_ge(ff_added, i + 1)
                dve.wait_ge(gathered[p], 64 * (i - p) + 128)
                for c in range(2):
                    for t in range(4):
                        last = nc.vector.scalar_tensor_tensor(
                            osb[:, p, t, :], grow[:, p, 2 * t + c, :],
                            mult[:, ds(4 * i + t, 1), :].rearrange("p a c -> p (a c)")[:, c:c + 1],
                            osb[:, p, t, :], ALU.mult, ALU.add)
                    last.then_inc((first_added, combined)[c], 1)
                    if c == 0:
                        dve.wait_ge(first_added, i + 1)

            dve.wait_ge(resid_ready, 1)
            dve.wait_ge(mult_ready, 1)
            for p in range(2):
                finish(p, p, True)
            with dve.Fori(1, GROUPS_A // 2) as i:
                for p in range(2):
                    finish(2 * i + p, p, False)

        @block.scalar
        def _(act):
            act.dma_start(maskb_sb, maskadd).then_inc(mask_in, 16)

            def keep_xn(g, p):
                act.wait_ge(xn_ready, g + 1)
                nc.scalar.activation(xn_sb[:, ds(4 * g, 4), :].rearrange("p t d -> p (t d)"),
                                     xnst[:, p].rearrange("p t d -> p (t d)"), ACT.Copy).then_inc(xn_kept, 1)

            def take_xnT(g, p, first):
                act.wait_ge(xnT_psum, g + 1)
                if not first:
                    act.wait_ge(gate_psum, g - 1)
                nc.scalar.activation(xnT[:, p, :], bank[p], ACT.Copy).then_inc(xnT_ready, 1)

            for p in range(2):
                keep_xn(p, p)
                take_xnT(p, p, True)
            with act.Fori(1, GROUPS_A // 2) as i:
                for p in range(2):
                    keep_xn(2 * i + p, p)
                    take_xnT(2 * i + p, p, False)

            act.wait_ge(dist_ready, 1)
            nc.scalar.activation(dist, dist, ACT.Exp, scale=-1.0).then_inc(route_exp, 1)

            act.wait_ge(small_in, 16 * N_SMALL)

            def take_hT(b):
                act.wait_ge(hT_psum, b + 1)
                if some(b):
                    act.wait_ge(qkv_psum, b)
                nc.scalar.activation(hT, turn_bank[:, T:2 * T], ACT.Identity, bias=b1c, scale=g1c).then_inc(hT_ready, 1)

            def take_h2T(b):
                act.wait_ge(h2T_psum, b + 1)
                nc.scalar.activation(h2T_sb[:, ds(b * T, T)], turn_bank[:, 0:T], ACT.Identity, bias=b2c, scale=g2c
                                     ).then_inc(h2T_ready, 1)

            def take_keys(b, p):
                act.wait_ge(heads_psum, b + 1)
                if some(b - 1):
                    act.wait_ge(scores_psum, G * (b - 1))
                nc.scalar.activation(kT[:, p, WIN:WIN + T], turn_bank[:, T:2 * T], ACT.Copy).then_inc(kT_ready, 1)

            def take_queries(b, p):
                for h in range(NKV):
                    last = nc.scalar.activation(qbd[:, p, :, h, :], turn_bank[:, 0:T].rearrange("p (n q) -> p n q", q=WIN),
                                                ACT.Copy, scale=qmask_sb[:, h:h + 1])
                last.then_inc(qbd_ready, 1)

            def exps(b, g):
                act.wait_ge(shifted, G * b + g + 1)
                nc.scalar.activation(S[:, g, :], S[:, g, :], ACT.Exp).then_inc(exp_ready, 1)

            def take_xsT(j, p):
                act.wait_ge(xsT_psum, j + 1)
                if some(j - 1):
                    act.wait_ge(h3_psum, j - 1)
                nc.scalar.activation(xsT[:, p, :], y_bank[:, D:D + P], ACT.Copy).then_inc(xsT_ready, 1)

            def silu(j, p):
                act.wait_ge(h1_psum, j + 1)
                if some(j - 1):
                    act.wait_ge(inter_ready, j - 1)
                nc.scalar.activation(act1[:, p, :], h1_bank[:, 0:FE], ACT.Silu).then_inc(silu_ready, 1)

            def take_y(j, p):
                act.wait_ge(y_psum, j + 1)
                if some(j - 1):
                    act.wait_ge(y_stored[p], 8 * (j - p))
                nc.scalar.activation(ysb[:, p, :], y_bank[:, 0:D], ACT.Copy).then_inc(y_ready, 1)
                act.wait_ge(y_ready, j + 1)
                act.dma_start(ys[ds(j * P, P), :], ysb[:, p, :]).then_inc(y_stored[p], 16)

            def step(k, p, j=None):
                def tile(i):
                    if j is not None:
                        silu(j + i, i % 2)
                        if some(j + i):
                            take_y(j + i - 1, 1 - i % 2)
                        if within(j + i + 2):
                            take_xsT(j + i + 2, i % 2)

                tile(0)
                if exists(k + 1):
                    take_keys(k + 1, 1 - p)
                    take_queries(k + 1, 1 - p)
                for i in range(1, 4):
                    tile(i)
                if exists(k + 3):
                    take_hT(k + 3)
                if exists(k - 3):
                    take_h2T(k - 3)
                tile(4)
                tile(5)
                if exists(k):
                    for g in range(G):
                        exps(k, g)

            take_hT(0)
            take_hT(1)
            take_keys(0, 0)
            take_queries(0, 0)
            take_hT(2)
            for k in range(LEAD):
                step(k, k % 2)
            take_xsT(0, 0)
            take_xsT(1, 1)
            step(LEAD, LEAD % 2, 0)
            with act.Fori(0, (B - 4 - LEAD) // 2) as i:
                step(2 * i + LEAD + 1, (LEAD + 1) % 2, (2 * i + 1) * TILES)
                step(2 * i + LEAD + 2, LEAD % 2, (2 * i + 2) * TILES)
            for k in range(B - 3, B):
                step(k, k % 2, (k - LEAD) * TILES)
            take_y(SLOT_TILES - 1, 1)
            for k in range(B, B + 3):
                step(k, k % 2)

            def gelu(i, p, first):
                for c in range(FC):
                    act.wait_ge(up_psum, FC * i + c + 1)
                    if not first:
                        act.wait_ge(down_psum, i - 1)
                    nc.scalar.activation(gT[:, p, c, :], bank[4 + c], ACT.Gelu, bias=cols_sb[:, 4 + c:5 + c]
                                         ).then_inc(gelu_ready, 1)

            for p in range(2):
                gelu(p, p, True)
            with act.Fori(1, GROUPS_A // 2) as i:
                for p in range(2):
                    gelu(2 * i + p, p, False)

        @block.tensor
        def _(pe):
            def transpose_xn(g, p, first):
                pe.wait_ge(xn_ready, g + 1)
                if not first:
                    pe.wait_ge(xnT_ready, g - 1)
                for j in range(4):
                    last = nc.tensor.transpose(bank[p][:, j * P:(j + 1) * P], xnst[:, p, j, :], ident_sb)
                last.then_inc(xnT_psum, 1)

            def gates(g, p, first):
                pe.wait_ge(xnT_ready, g + 1)
                if not first:
                    pe.wait_ge(gate_kept, g - 1)
                for j in range(4):
                    last = nc.tensor.matmul(bank[2 + p][:, j * E:(j + 1) * E], xnT[:, p, j * P:(j + 1) * P], gate_sb,
                                            start=True, stop=True)
                last.then_inc(gate_psum, 1)

            pe.wait_ge(small_in, 16 * N_SMALL)
            transpose_xn(0, 0, True)
            transpose_xn(1, 1, True)
            gates(0, 0, True)
            transpose_xn(2, 0, False)
            gates(1, 1, True)
            with pe.Fori(0, (GROUPS_A - 4) // 2) as i:
                transpose_xn(2 * i + 3, 1, False)
                gates(2 * i + 2, 0, False)
                transpose_xn(2 * i + 4, 0, False)
                gates(2 * i + 3, 1, False)
            transpose_xn(GROUPS_A - 1, 1, False)
            gates(GROUPS_A - 2, 0, False)
            gates(GROUPS_A - 1, 1, False)

            pe.wait_ge(consts_set, 2)
            pe.wait_ge(pairs_ready, 1)
            flat = asum.rearrange("p t e -> p (t e)")
            nc.tensor.matmul(bank[6][:, 0:256], tri_sb, flat, start=True, stop=True)
            nc.tensor.matmul(bank[6][:, 256:512], ones_sb, flat, start=True, stop=True).then_inc(ranks_psum, 1)

            def transpose_h(b):
                pe.wait_ge(h_ready, b + 1)
                if some(b):
                    pe.wait_ge(hT_ready, b)
                for t in range(TPB):
                    last = nc.tensor.transpose(turn_bank[:, T + t * P:T + (t + 1) * P], hbuf[:, t, :], ident_sb)
                last.then_inc(hT_psum, 1)

            def qkv(b):
                pe.wait_ge(hT_ready, b + 1)
                if some(b):
                    pe.wait_ge(qkv_biased, b)
                    pe.wait_ge(vt_ready, b)
                if some(b - 4):
                    pe.wait_ge(x1_ready, b - 4)
                for t in range(TPB):
                    last = nc.tensor.matmul(qkv_bank[:, t * 192:(t + 1) * 192], hT[:, t * P:(t + 1) * P], wqkv_sb,
                                            start=True, stop=True)
                last.then_inc(qkv_psum, 1)

            def heads(b, hT_out):
                pe.wait_ge(qkv_biased, b + 1)
                pe.wait_ge(rope_ready, b + 1)
                pe.wait_ge(hT_ready, hT_out)
                if some(b - 2):
                    pe.wait_ge(pv_normed, b - 2)
                if some(b - 3):
                    pe.wait_ge(x1_ready, b - 3)
                for t in range(TPB):
                    cols = slice(t * P, (t + 1) * P)
                    nc.tensor.transpose(turn_bank[:, cols], qr[:, t, :], ident_sb)
                    nc.tensor.transpose(turn_bank[:, T + t * P:T + (t + 1) * P], kr[:, t].rearrange("p g c -> p (g c)"), ident_sb)
                    last = nc.tensor.transpose(qkv_bank[:, cols], vb[:, t].rearrange("p g c -> p (g c)"), ident_sb)
                last.then_inc(heads_psum, 1)

            def scores(b, p, g):
                if g == 0:
                    pe.wait_ge(qbd_ready, b + 1)
                    pe.wait_ge(kT_ready, b + 1)
                if some(G * b + g - 1):
                    pe.wait_ge(shifted, G * b + g - 1)
                nc.tensor.matmul(bank[g % 2], identb_sb, maskb_sb, start=True, stop=False)
                rows = slice(g * 32, (g + 1) * 32)
                for n in range(NBLK):
                    last = nc.tensor.matmul(bank[g % 2][:, n * KW:(n + 1) * KW], qbd[rows, p, n].rearrange("p h q -> p (h q)"),
                                            kT[rows, p, n * WIN:n * WIN + KW], start=False, stop=(n == NBLK - 1))
                last.then_inc(scores_psum, 1)

            def transpose_h2(b):
                pe.wait_ge(h2_ready, b + 1)
                if some(b):
                    pe.wait_ge(h2T_ready, b)
                for t in range(TPB):
                    last = nc.tensor.transpose(turn_bank[:, t * P:(t + 1) * P], h2[:, t, :], ident_sb)
                last.then_inc(h2T_psum, 1)

            def attend(b, p, half, hT_out, h2T_out):
                if half == 0:
                    pe.wait_ge(pT_ready, G * b + G)
                    pe.wait_ge(vbd_ready, b + 1)
                    pe.wait_ge(hT_ready, hT_out)
                    if some(h2T_out):
                        pe.wait_ge(h2T_ready, h2T_out)
                for n in range(half * NBLK // 2, (half + 1) * NBLK // 2):
                    for i in range(2):
                        last = nc.tensor.matmul(turn_bank[:, n * VW:(n + 1) * VW],
                                                pT[:, p, 2 * n + i].rearrange("p g q -> p (g q)"),
                                                vbd[:, p, n + i, :], start=(i == 0), stop=(i == 1))
                if half == 1:
                    last.then_inc(pv_psum, 1)

            def project(b, qkv_out, vt_out):
                pe.wait_ge(outT_ready, b + 1)
                pe.wait_ge(qkv_biased, qkv_out)
                pe.wait_ge(vt_ready, vt_out)
                if some(b):
                    pe.wait_ge(x1_ready, b)
                for t in range(TPB):
                    last = nc.tensor.matmul(qkv_bank[:, T + t * P:T + (t + 1) * P], outT[:, t * P:(t + 1) * P], wo_sb,
                                            start=True, stop=True)
                last.then_inc(wo_psum, 1)

            def expert_of(j):
                return pe.value_load(te[0:1, ds(j, 1)], min_val=0, max_val=(E - 1) * ESTRIDE)

            def transpose_xs(j, p):
                pe.wait_ge(slots_in[p], 8 * (j - p) + 16)
                if some(j):
                    pe.wait_ge(xsT_ready, j)
                if some(j - 2):
                    pe.wait_ge(y_ready, j - 2)
                nc.tensor.transpose(y_bank[:, D:D + P], xsb[:, p, :], ident_sb).then_inc(xsT_psum, 1)

            def up_products(j, p):
                at = expert_of(j)
                pe.wait_ge(xsT_ready, j + 1)
                if some(j):
                    pe.wait_ge(silu_ready, j)
                    pe.wait_ge(inter_ready, j)
                nc.tensor.matmul(h1_bank[:, 0:FE], xsT[:, p, :], w1_sb[:, ds(at, FE)], start=True, stop=True).then_inc(h1_psum, 1)
                nc.tensor.matmul(h3_bank[:, 0:FE], xsT[:, p, :], w3_sb[:, ds(at, FE)], start=True, stop=True).then_inc(h3_psum, 1)

            def transpose_inter(j, p):
                pe.wait_ge(inter_ready, j + 1)
                if some(j):
                    pe.wait_ge(iT_ready, j)
                for c in range(EC):
                    last = nc.tensor.transpose(iT_bank[0:FP, c * P:(c + 1) * P], inter[:, p, c * FP:(c + 1) * FP], ident_sb)
                last.then_inc(iT_psum, 1)

            def down_product(j, p, xsT_out):
                at = expert_of(j)
                pe.wait_ge(iT_ready, j + 1)
                pe.wait_ge(xsT_ready, xsT_out)
                if some(j):
                    pe.wait_ge(y_ready, j)
                for c in range(EC):
                    last = nc.tensor.matmul(y_bank[:, 0:D], iT[:, p, c * P:(c + 1) * P], w2_sb[:, ds(at + c * P, P)],
                                            start=(c == 0), stop=(c == EC - 1))
                last.then_inc(y_psum, 1)

            def step(k, p, j=None):
                def tile_up(i):
                    if j is not None:
                        up_products(j + i, i % 2)
                        if some(j + i):
                            down_product(j + i - 1, 1 - i % 2, j + i + 2 if within(j + i + 1) else SLOT_TILES)

                def tile_T(i):
                    if j is not None:
                        transpose_inter(j + i, i % 2)
                        if within(j + i + 2):
                            transpose_xs(j + i + 2, i % 2)

                hT_out = k + 4 if exists(k + 3) else B

                tile_up(0)
                if exists(k):
                    scores(k, p, 0)
                if exists(k + 1):
                    heads(k + 1, k + 3 if exists(k + 2) else B)
                tile_T(0)
                tile_up(1)
                if exists(k):
                    scores(k, p, 1)
                if exists(k + 2):
                    qkv(k + 2)
                tile_T(1)
                tile_up(2)
                if exists(k):
                    scores(k, p, 2)
                if exists(k - 2):
                    project(k - 2, k + 3 if exists(k + 2) else B, k + 2 if exists(k + 1) else B)
                tile_T(2)
                tile_up(3)
                if exists(k):
                    scores(k, p, 3)
                if exists(k + 1):
                    pe.wait_ge(kT_ready, k + 2)
                    pe.wait_ge(qbd_ready, k + 2)
                elif exists(k - 2):
                    pe.wait_ge(pv_normed, k - 1)
                if exists(k - 3):
                    transpose_h2(k - 3)
                if exists(k + 3):
                    transpose_h(k + 3)
                tile_T(3)
                tile_up(4)
                if exists(k - 1):
                    attend(k - 1, 1 - p, 0, hT_out, k - 2)
                tile_T(4)
                tile_up(5)
                if exists(k - 1):
                    attend(k - 1, 1 - p, 1, hT_out, k - 2)
                tile_T(5)

            pe.wait_ge(mask_in, 16)
            transpose_h(0)
            qkv(0)
            transpose_h(1)
            heads(0, 2)
            qkv(1)
            pe.wait_ge(kT_ready, 1)
            pe.wait_ge(qbd_ready, 1)
            transpose_h(2)
            for k in range(LEAD):
                step(k, k % 2)
            pe.wait_ge(experts_ready, 1)
            pe.wait_ge(weights_in, 48)
            transpose_xs(0, 0)
            transpose_xs(1, 1)
            step(LEAD, LEAD % 2, 0)
            with pe.Fori(0, (B - 4 - LEAD) // 2) as i:
                step(2 * i + LEAD + 1, (LEAD + 1) % 2, (2 * i + 1) * TILES)
                step(2 * i + LEAD + 2, LEAD % 2, (2 * i + 2) * TILES)
            for k in range(B - 3, B):
                step(k, k % 2, (k - LEAD) * TILES)
            down_product(SLOT_TILES - 1, 1, SLOT_TILES)
            for k in range(B, B + 3):
                step(k, k % 2)

            pe.wait_ge(y_ready, SLOT_TILES)
            pe.wait_ge(h2T_ready, B)
            pe.wait_ge(x1_ready, B)
            pe.wait_ge(shifted, G * B)

            def up(i, first):
                for c in range(FC):
                    if not first:
                        pe.wait_ge(gelu_ready, FC * i + c - (FC - 1))
                    nc.tensor.matmul(bank[4 + c], wf1_sb[:, c * P:(c + 1) * P], h2T_sb[:, ds(i * 512, 512)],
                                     start=True, stop=True).then_inc(up_psum, 1)

            def down(i, p, first):
                pe.wait_ge(gelu_ready, FC * i + FC)
                if not first:
                    pe.wait_ge(ff_added, i - 1)
                for t in range(4):
                    for c in range(FC):
                        last = nc.tensor.matmul(bank[p][:, t * D:(t + 1) * D], gT[:, p, c, t * P:(t + 1) * P],
                                                wf2_sb[:, c, :], start=(c == 0), stop=(c == FC - 1))
                last.then_inc(down_psum, 1)

            up(0, True)
            for p in range(2):
                up(p + 1, False)
                down(p, p, True)
            with pe.Fori(1, GROUPS_A // 2 - 1) as i:
                for p in range(2):
                    up(2 * i + p + 1, False)
                    down(2 * i + p, p, False)
            n = GROUPS_A - 2
            up(n + 1, False)
            down(n, 0, False)
            down(n + 1, 1, False)


def constants():
    f32 = np.float32
    p = np.arange(P)
    half = HD // 2
    theta = (1.0 / 10000.0 ** (np.arange(half, dtype=f32) / f32(half))).astype(f32)
    pos = np.arange(T, dtype=f32)
    freqs = np.outer(pos, theta).astype(f32)
    c, s = np.cos(freqs).astype(f32), np.sin(freqs).astype(f32)
    cosf = np.tile(np.concatenate([c, c], 1), (1, 20)).reshape(TPB, P, 160).transpose(1, 0, 2).reshape(P, -1)
    sinf = np.tile(np.concatenate([-s, s], 1), (1, 20)).reshape(TPB, P, 160).transpose(1, 0, 2).reshape(P, -1)
    q, k = (p % WIN)[:, None], np.arange(KW)[None, :]
    valid = (k - WIN <= q) & (k > q)
    allowed = np.repeat(valid[:, None, :], NBLK, 1)
    allowed[:, 0, :WIN] = False
    maskadd = np.where(allowed, 0.0, NEG).reshape(P, -1).astype(f32)
    qmask = np.where((p // HD % NKV)[:, None] == np.arange(NKV), 1.0 / np.sqrt(f32(HD)), 0.0).astype(f32)
    col = np.concatenate([np.repeat(np.arange(NKV), HD), np.arange(NKV)])
    vmask = ((p // WIN)[:, None] == col).astype(f32)
    tri = (p[:, None] < p[None, :]).astype(f32)
    rev = np.broadcast_to(E - np.arange(E), (P, E)).astype(f32)
    grid = np.broadcast_to(np.arange(SLOT_TILES)[:, None], (P, SLOT_TILES, 7)).reshape(P, -1).astype(f32)
    return {"ident": np.eye(P, dtype=f32), "cosf": cosf, "sinf": sinf, "maskadd": maskadd, "qmask": qmask,
            "vmask": vmask, "tri": tri, "rev": rev, "tilegrid": grid}


def laid_out(i):
    def rows(v):
        return np.broadcast_to(v, (P, v.shape[0]))

    heads = (NKV, G, HD)
    wq = i["L0_attn_Wq"].reshape(D, *heads).transpose(0, 2, 1, 3).reshape(D, D)
    bq = i["L0_attn_bq"].reshape(heads).transpose(1, 0, 2).reshape(D)

    def experts(w):
        wide = np.zeros((D, E, ESTRIDE), w.dtype)
        wide[:, :, :FE] = w.transpose(2, 0, 1)
        return wide.reshape(D, -1)

    w2 = i["L0_ffn_w2"].reshape(E, D, EC, FP).transpose(3, 0, 2, 1).reshape(FP, -1)
    return {
        "x": i["L0_attn_x"].reshape(NTOK, D),
        "wqkv": np.concatenate([wq, i["L0_attn_Wk"], i["L0_attn_Wv"]], 1),
        "bqkv": rows(np.concatenate([bq, i["L0_attn_bk"], i["L0_attn_bv"]])),
        "wo": i["L0_attn_Wo"].reshape(*heads, D).transpose(1, 0, 2, 3).reshape(D, D),
        "bo": rows(i["L0_attn_bo"]),
        "g1": i["L0_attn_g1"].reshape(D, 1), "b1": i["L0_attn_b1"].reshape(D, 1),
        "g2": i["L0_attn_g2"].reshape(D, 1), "b2": i["L0_attn_b2"].reshape(D, 1),
        "wf1": i["L0_attn_Wf1"], "bf1": i["L0_attn_bf1"].reshape(FC, P).T,
        "wf2": i["L0_attn_Wf2"].reshape(FC, P, D).transpose(1, 0, 2).reshape(P, -1),
        "bf2": rows(i["L0_attn_bf2"]),
        "gate": i["L0_ffn_gate_w"].T,
        "w1": experts(i["L0_ffn_w1"]), "w3": experts(i["L0_ffn_w3"]), "w2": w2,
    }


def kernel(**inputs):
    import concourse.bacc as bacc
    import ml_dtypes
    from concourse.bass_utils import run_bass_kernel_spmd

    arrays = laid_out({k: np.asarray(v) for k, v in inputs.items()})
    arrays.update(constants())
    arrays["maskadd"] = arrays["maskadd"].astype(ml_dtypes.bfloat16)
    nc = bacc.Bacc("TRN2", target_bir_lowering=False, num_devices=1)
    feeds, aps = {}, {}
    for name, a in arrays.items():
        a = np.ascontiguousarray(a)
        feeds[f"in_{name}"] = a
        aps[name] = nc.dram_tensor(f"in_{name}", a.shape, mybir.dt.from_np(a.dtype), kind="ExternalInput").ap()
    for name in ("xs", "ys"):
        aps[name] = nc.dram_tensor(f"scratch_{name}", (SLOT_TILES * P, D), mybir.dt.float32, kind="Internal").ap()
    aps["out"] = nc.dram_tensor("out_dram", (NTOK, D), mybir.dt.float32, kind="ExternalOutput").ap()
    layer(nc, **aps)
    r = run_bass_kernel_spmd(nc, [feeds], core_ids=[0])
    return r.results[0]["out_dram"].reshape(B, T, D)
```

```python
from contextlib import ExitStack

import numpy as np

import concourse.bass as bass
from concourse import mybir

P = 128
B, T, D = 16, 256, 128
NTOK = B * T
NT = NTOK // P
TPB = T // P
NH, NKV, HD = 16, 4, 8
G = NH // NKV
WIN = 32
NBLK = T // WIN
KW = 2 * WIN
UNITS = NBLK // 2
assert 2 * G * KW == 512 and UNITS == G
DFF = 512
FC = DFF // P
E, FE = 8, 448
EC = 4
FP = FE // EC
ESTRIDE = 512
LEAD = 3
TILES = 6
EARLY = LEAD + 2
MSTEPS = B - 1 - LEAD
SLOT_TILES = TILES * MSTEPS
assert SLOT_TILES >= (2 * NTOK + E * (P - 1)) // P
EPS = 1e-5
JITTER2 = 0.02
GROUPS_A = NT // 4
assert GROUPS_A // 2 == 1 + LEAD
VW = NKV * HD + NKV
XW = D + 2
NO_PAIR = 1e6
NEG = -1e30


def layer(nc, x, wqkv, bqkv, wo, bo, g1, b1, g2, b2, wf1, bf1, wf2, bf2, gate, w1, w3, w2,
          ident, cosf, sinf, maskadd, qmask, vmask, tri, rev, tilegrid, slotgrid, xs, ys, out):
    F32, BF16, I32 = mybir.dt.float32, mybir.dt.bfloat16, mybir.dt.int32
    ALU, ACT, AX = mybir.AluOpType, mybir.ActivationFunctionType, mybir.AxisListType
    ds = bass.ds
    ctx = ExitStack()
    with ctx:
        def sb(name, shape, dt=F32):
            return ctx.enter_context(nc.sbuf_tensor(name, shape, dt))[:]

        def sem(name):
            return ctx.enter_context(nc.semaphore(name))

        x_sb = sb("x_sb", [P, NT, D])
        xn_sb = sb("xn_sb", [P, NT, XW])
        x1_sb = sb("x1_sb", [P, NT, D])
        h2T_sb = sb("h2T_sb", [P, NTOK])
        w1_sb = sb("w1_sb", [P, E * ESTRIDE])
        w3_sb = sb("w3_sb", [P, E * ESTRIDE])
        w2_sb = sb("w2_sb", [FP, E * ESTRIDE])
        wqkv_sb = sb("wqkv_sb", [P, 192])
        bqkv_sb = sb("bqkv_sb", [P, 192])
        wo_sb = sb("wo_sb", [P, D])
        bo_sb = sb("bo_sb", [P, D])
        bf2_sb = sb("bf2_sb", [P, D])
        wf1_sb = sb("wf1_sb", [P, DFF])
        wf2_sb = sb("wf2_sb", [P, FC, D])
        cols_sb = sb("cols_sb", [P, 4 + FC])
        gate_sb = sb("gate_sb", [P, E])
        ident_sb = sb("ident_sb", [P, P])
        identb_sb = sb("identb_sb", [P, P], BF16)
        maskb_sb = sb("maskb_sb", [P, NBLK * KW], BF16)
        cos_sb = sb("cos_sb", [P, TPB * 160])
        sin_sb = sb("sin_sb", [P, TPB * 160])
        qmask_sb = sb("qmask_sb", [P, NKV])
        vmask_sb = sb("vmask_sb", [P, VW])
        tri_sb = sb("tri_sb", [P, P])
        ones_sb = sb("ones_sb", [P, P])
        rev_sb = sb("rev_sb", [P, E])
        grid_sb = sb("grid_sb", [P, SLOT_TILES * 7])
        blank_sb = sb("blank_sb", [P, 8, XW])
        slotgrid_sb = sb("slotgrid_sb", [P, SLOT_TILES])
        nhalf_sb = sb("nhalf_sb", [P, 4])
        eps_sb = sb("eps_sb", [P, 4])
        spare_sb = sb("spare_sb", [P, 10])

        stA = sb("stA", [P, 4, 6])
        mvA = sb("mvA", [P, 2, 4, 2])
        veA = sb("veA", [P, 4])
        rsA = sb("rsA", [P, 2, 4])
        xnst = sb("xnst", [P, 2, 4, D])
        xnT = sb("xnT", [P, 2, 512])

        used = [0]

        def table(*shape):
            n = int(np.prod(shape))
            used[0] += n
            names = "abcd"[:len(shape)]
            flat = h2T_sb[:, used[0] - n:used[0]]
            return flat.rearrange(f"p ({' '.join(names)}) -> p {' '.join(names)}", **dict(zip(names, shape)))

        sc = table(NT, E)
        oh = table(2, NT, E)
        top = table(2, NT)
        tmp = table(2, NT, E)
        dist = table(2, NT, E)
        keep = table(2, NT, E)
        pick = table(NT)
        asum = table(NT, E)
        tot = table(NT, E)
        incl = table(NT, E)
        slotm = table(NT, E)
        cnt = sb("cnt", [P, 3, E])
        mult = sb("mult", [P, NT, 2])
        slotf = sb("slotf", [P, NT, 2])
        slot = sb("slot", [P, NT, 2], I32)
        tef = sb("tef", [P, SLOT_TILES])
        te = sb("te", [P, SLOT_TILES], I32)

        st1 = sb("st1", [P, TPB, 6])
        mv1 = sb("mv1", [P, TPB, 2])
        ve1 = sb("ve1", [P, TPB])
        rstd1 = sb("rstd1", [P, TPB])
        hbuf = sb("hbuf", [P, TPB, D])
        hT = sb("hT", [P, T])
        qkb = sb("qkb", [P, TPB, 160])
        vb = sb("vb", [P, TPB, G, 32])
        ra = sb("ra", [P, TPB, 160])
        rb = sb("rb", [P, TPB, 160])
        qr = sb("qr", [P, TPB, P])
        kr = sb("kr", [P, TPB, G, 32])
        kT = sb("kT", [P, 2, G, WIN + T])
        qbd = sb("qbd", [P, 2, NBLK, NKV, WIN])
        vt = sb("vt", [P, T])
        vbd = sb("vbd", [P, 2, NBLK + 1, VW])
        rmax = sb("rmax", [P, UNITS, 2, G])
        S = sb("S", [P, UNITS, 512])
        past = S.rearrange("p u c -> p (u c)")[:, 0:SLOT_TILES * 7]
        pT = sb("pT", [P, 2 * NBLK, G, WIN])
        rsum = sb("rsum", [P, NBLK, NKV])
        on = sb("on", [P, T])
        outT = sb("outT", [P, T])
        st2 = sb("st2", [P, TPB, 6])
        mv2 = sb("mv2", [P, TPB, 2])
        ve2 = sb("ve2", [P, TPB])
        rstd2 = sb("rstd2", [P, TPB])
        h2 = sb("h2", [P, TPB, D])
        xstage = sb("xstage", [P, 2, 4, XW])
        istage = sb("istage", [P, 2, 8], I32)

        xsb = sb("xsb", [P, 3, XW])
        pair = sb("pair", [P, 3], I32)
        xsT = sb("xsT", [P, 2, P])
        act1 = sb("act1", [P, 2, FE])
        inter = sb("inter", [P, 2, FE])
        iT = xnT[0:FP]
        ysb = sb("ysb", [P, 3, D])

        gT = [w.rearrange("p (b c n) -> p b c n", b=2, c=FC)[:, b] for w in (w1_sb, w3_sb) for b in range(2)]
        yrow = xn_sb.rearrange("p t c -> p (t c)")[:, 0:NT * D].rearrange("p (b t c) -> p b t c", b=4, t=4)
        osb = blank_sb.rearrange("p r d -> p (r d)")[:, 0:8 * D].rearrange("p (b t d) -> p b t d", b=2, t=4)

        bank = [ctx.enter_context(nc.psum_tensor(f"bank{i}", [P, 512], F32))[:] for i in range(8)]
        qkv_bank, turn_bank = bank[2], bank[3]
        h1_bank, h3_bank, iT_bank, y_bank = bank[4:8]

        small_in, x_in, weights_in = sem("small_in"), [sem(f"x_in{i}") for i in range(4)], sem("weights_in")
        mask_in, gate_in = sem("mask_in"), sem("gate_in")
        zeros_set, pool_consts, consts_set = sem("zeros_set"), sem("pool_consts"), sem("consts_set")
        xs_zeroed = sem("xs_zeroed")
        stats_a, aggr_a, rstd_a, var_a = sem("stats_a"), sem("aggr_a"), sem("rstd_a"), sem("var_a")
        xn_ready, stats_1, aggr_1, rstd_1, var_1 = (sem("xn_ready"), sem("stats_1"), sem("aggr_1"),
                                                    sem("rstd_1"), sem("var_1"))
        xn_kept, xb_kept = sem("xn_kept"), sem("xb_kept")
        xnT_psum, xnT_ready, gate_psum, gate_kept = (sem("xnT_psum"), sem("xnT_ready"),
                                                     sem("gate_psum"), sem("gate_kept"))
        route_chain, route_exp, ranks_psum, pairs_ready = (sem("route_chain"), sem("route_exp"),
                                                           sem("ranks_psum"), sem("pairs_ready"))
        dist_ready, slots_ready, experts_ready, mult_ready = (sem("dist_ready"), sem("slots_ready"),
                                                              sem("experts_ready"), sem("mult_ready"))
        h_ready, hT_psum, hT_ready, qkv_psum, qkv_biased = (sem("h_ready"), sem("hT_psum"), sem("hT_ready"),
                                                            sem("qkv_psum"), sem("qkv_biased"))
        rope_parts, rope_ready, heads_psum, kT_ready, qbd_ready = (sem("rope_parts"), sem("rope_ready"),
                                                                   sem("heads_psum"), sem("kT_ready"), sem("qbd_ready"))
        rope_parts_dve, rope_ready_dve = sem("rope_parts_dve"), sem("rope_ready_dve")
        vt_ready, vbd_ready, scores_psum, rowmax_ready, shifted = (sem("vt_ready"), sem("vbd_ready"),
                                                                   sem("scores_psum"), sem("rowmax_ready"), sem("shifted"))
        exp_ready, pT_ready, pv_psum, rsum_ready, pv_normed = (sem("exp_ready"), sem("pT_ready"), sem("pv_psum"),
                                                               sem("rsum_ready"), sem("pv_normed"))
        outT_ready, wo_psum, x1_ready, stats_2, aggr_2, var_2, rstd_2 = (
            sem("outT_ready"), sem("wo_psum"), sem("x1_ready"), sem("stats_2"), sem("aggr_2"), sem("var_2"), sem("rstd_2"))
        h2_ready, h2T_psum, h2T_ready = sem("h2_ready"), sem("h2T_psum"), sem("h2T_ready")
        staged, scattered = [sem(f"staged{i}") for i in range(2)], [sem(f"scattered{i}") for i in range(2)]
        slots_in = [sem(f"slots_in{i}") for i in range(3)]
        xsT_psum, xsT_ready, h1_psum, h3_psum = sem("xsT_psum"), sem("xsT_ready"), sem("h1_psum"), sem("h3_psum")
        silu_ready, inter_ready, iT_psum, iT_ready = sem("silu_ready"), sem("inter_ready"), sem("iT_psum"), sem("iT_ready")
        y_psum, y_ready, y_stored = sem("y_psum"), sem("y_ready"), [sem(f"y_stored{i}") for i in range(3)]
        resid_part, resid_ready = sem("resid_part"), sem("resid_ready")
        up_psum, gelu_ready, down_psum, ff_added = sem("up_psum"), sem("gelu_ready"), sem("down_psum"), sem("ff_added")
        pair_ready, y_waited, pairs_in = sem("pair_ready"), sem("y_waited"), [sem(f"pairs_in{i}") for i in range(4)]
        first_added, combined, stored = sem("first_added"), sem("combined"), [sem(f"stored{i}") for i in range(2)]

        g1c, b1c, g2c, b2c = (cols_sb[:, i:i + 1] for i in range(4))
        N_SMALL = 20

        spare_column = {s: i for i, s in enumerate(("aggr_a", "stats_a", "aggr_1", "stats_1", "x1_ready", "stats_2",
                                                    "staged0", "staged1", "y_ready", "x1_added"))}

        def spare_of(name):
            return spare_sb[:, spare_column[name]:spare_column[name] + 1]

        def wait_apart_dve(name, semaphore, value):
            nc.vector.wait_ge(semaphore, value)
            nc.vector.memset(spare_of(name), 0.0)

        def wait_apart_pool(name, semaphore, value):
            nc.gpsimd.wait_ge(semaphore, value)
            return nc.gpsimd.tensor_tensor(spare_of(name), eps_sb[:, 0:1], eps_sb[:, 0:1], ALU.add)

        def bc(ap, shape):
            return ap.broadcast_to(shape)

        def exists(b):
            return not isinstance(b, int) or 0 <= b < B

        def is_last(k):
            return isinstance(k, int) and k == B - 1

        def within(j):
            return not isinstance(j, int) or j < SLOT_TILES

        def some(n):
            return not isinstance(n, int) or n > 0

        def early(b):
            return isinstance(b, int) and b < EARLY

        def rope_count(b):
            return (rope_ready_dve, b + 1) if early(b) else (rope_ready, b + 1 - EARLY)

        def rotate(ops, eng, b):
            parts, ready, n = (rope_parts_dve, rope_ready_dve, b) if early(b) else (rope_parts, rope_ready, b - EARLY)
            eng.wait_ge(qkv_biased, b + 1)
            flat = "p t c -> p (t c)"
            q4 = qkb.rearrange("p t (n h c) -> p (t n) h c", h=2, c=HD // 2)
            s4 = sin_sb.rearrange("p (n h c) -> p n h c", h=2, c=HD // 2)
            r4 = rb.rearrange("p t (n h c) -> p (t n) h c", h=2, c=HD // 2)
            ops.tensor_tensor(ra.rearrange(flat), qkb.rearrange(flat), cos_sb, ALU.mult)
            ops.tensor_tensor(r4[:, :, 0, :], q4[:, :, 1, :], s4[:, :, 0, :], ALU.mult)
            ops.tensor_tensor(r4[:, :, 1, :], q4[:, :, 0, :], s4[:, :, 1, :], ALU.mult).then_inc(parts, 1)
            eng.wait_ge(parts, n + 1)
            if some(b):
                eng.wait_ge(heads_psum, b)
            ops.tensor_tensor(qr, ra[:, :, 0:P], rb[:, :, 0:P], ALU.add)
            for t in range(TPB):
                last = ops.tensor_tensor(
                    kr[:, t], bc(ra[:, t, P:160].rearrange("p (a c) -> p a c", a=1), [P, G, 32]),
                    bc(rb[:, t, P:160].rearrange("p (a c) -> p a c", a=1), [P, G, 32]), ALU.add)
            last.then_inc(ready, 1)

        block = ctx.enter_context(nc.Block())

        @block.sync
        def _(sp):
            xv = x.rearrange("(t p) d -> p t d", p=P)
            for i in range(4):
                part = slice(4 * i, 4 * i + 4 if i < 3 else NT)
                sp.dma_start(x_sb[:, part, :], xv[:, part, :]).then_inc(x_in[i], 16)
            small = [(wqkv_sb, wqkv), (bqkv_sb, bqkv), (wo_sb, wo), (bo_sb, bo),
                     (bf2_sb, bf2), (wf1_sb, wf1), (cols_sb[:, 0:1], g1), (cols_sb[:, 1:2], b1), (cols_sb[:, 2:3], g2),
                     (cols_sb[:, 3:4], b2), (cols_sb[:, 4:4 + FC], bf1), (cos_sb, cosf), (sin_sb, sinf),
                     (qmask_sb, qmask), (vmask_sb, vmask), (tri_sb, tri), (rev_sb, rev), (slotgrid_sb, slotgrid), (grid_sb, tilegrid),
                     (wf2_sb, wf2.rearrange("p (c d) -> p c d", c=FC))]
            assert len(small) == N_SMALL
            for dst, src in small:
                sp.dma_start(dst, src).then_inc(small_in, 16)
            sp.wait_ge(zeros_set, 1)
            xz = xs.rearrange("(p r) d -> p (r d)", p=P)
            for r0 in range(0, SLOT_TILES, 8):
                n = min(8, SLOT_TILES - r0) * XW
                sp.dma_start(xz[:, r0 * XW:r0 * XW + n], blank_sb.rearrange("p r d -> p (r d)")[:, 0:n]).then_inc(xs_zeroed, 16)
            for dst, src in ((w1_sb, w1), (w3_sb, w3), (w2_sb, w2)):
                sp.dma_start(dst, src).then_inc(weights_in, 16)

            sp.wait_ge(xn_kept, GROUPS_A)
            sp.wait_ge(slots_ready, 1)

            def stage(i, p):
                group = ds((2 * i + p) * 4, 4)
                if some(i):
                    sp.wait_ge(scattered[p], 8 * 16 * i)
                sp.dma_start(xstage[:, p], xn_sb[:, group, :]).then_inc(staged[p], 16)
                sp.dma_start(istage[:, p], slot[:, group, :].rearrange("p t c -> p (t c)")).then_inc(staged[p], 16)

            for p in range(2):
                stage(0, p)
            with sp.Fori(1, GROUPS_A // 2) as i:
                for p in range(2):
                    stage(i, p)
            for p in range(2):
                sp.wait_ge(scattered[p], 8 * 16 * GROUPS_A // 2)

            def load_slots(n, p):
                if some(n):
                    sp.wait_ge(xsT_psum, 3 * n + p - 2)
                    sp.wait_ge(pair_ready, 3 * n + p - 2)
                sp.dma_start(xsb[:, p, :], xs[ds((3 * n + p) * P, P), :]).then_inc(slots_in[p], 16)

            for p in range(3):
                load_slots(0, p)
            with sp.Fori(1, SLOT_TILES // 3) as n:
                for p in range(3):
                    load_slots(n, p)

            ov = out.rearrange("(t p) d -> p t d", p=P)
            yv = ys.rearrange("(t p c) d -> p t (c d)", p=P, c=2)
            for p in range(3):
                sp.wait_ge(y_stored[p], 16 * SLOT_TILES // 3)
            sp.wait_ge(h_ready, B)

            def load_pairs(i):
                sp.dma_start(yrow[:, i % 4], yv[:, 4 * i:4 * i + 4, :]).then_inc(pairs_in[i % 4], 16)

            for i in range(4):
                load_pairs(i)
            for i in range(GROUPS_A):
                sp.wait_ge(combined, i + 1)
                sp.dma_start(ov[:, 4 * i:4 * i + 4, :], osb[:, i % 2]).then_inc(stored[i % 2], 16)
                if i + 4 < GROUPS_A:
                    load_pairs(i + 4)
            for p in range(2):
                sp.wait_ge(stored[p], 16 * GROUPS_A // 2)

        @block.gpsimd
        def _(pool):
            nc.gpsimd.memset(blank_sb[:, :, 0:D], 0.0)
            nc.gpsimd.memset(blank_sb[:, :, D:D + 1], NO_PAIR)
            nc.gpsimd.memset(blank_sb[:, :, D + 1:XW], -1.0).then_inc(zeros_set, 1)
            nc.gpsimd.memset(eps_sb, EPS)
            nc.gpsimd.memset(nhalf_sb, -0.5).then_inc(pool_consts, 1)
            pool.wait_ge(pool_consts, 1)

            def group_a1(g, p, first):
                pool.wait_ge(aggr_a, g + 1)
                pool.wait_ge(rstd_a, g)
                nc.gpsimd.tensor_tensor(veA, mvA[:, p, :, 1], eps_sb, ALU.add).then_inc(var_a, 1)
                pool.wait_ge(var_a, g + 1)
                if not first:
                    pool.wait_ge(xn_ready, g - 1)
                nc.gpsimd.tensor_tensor(rsA[:, p, :], veA, nhalf_sb, ALU.pow).then_inc(rstd_a, 1)

            def group_a2(g, p):
                pool.wait_ge(xn_ready, g + 1)
                nc.gpsimd.tensor_tensor(x1_sb[:, ds(g * 4, 4), :], xnst[:, p],
                                        bc(bo_sb.rearrange("p (a d) -> p a d", a=1), [P, 4, D]),
                                        ALU.add).then_inc(xb_kept, 1)

            group_a1(0, 0, True)
            group_a1(1, 1, True)
            pool.wait_ge(small_in, 16 * N_SMALL)
            group_a2(0, 0)
            with pool.Fori(0, (GROUPS_A - 2) // 2) as i:
                group_a1(2 * i + 2, 0, False)
                group_a2(2 * i + 1, 1)
                group_a1(2 * i + 3, 1, False)
                group_a2(2 * i + 2, 0)
            group_a2(GROUPS_A - 1, 1)

            def rstd1_of(b):
                pool.wait_ge(aggr_1, b + 1)
                nc.gpsimd.tensor_tensor(ve1, mv1[:, :, 1], eps_sb[:, 0:TPB], ALU.add).then_inc(var_1, 1)
                pool.wait_ge(var_1, b + 1)
                nc.gpsimd.tensor_tensor(rstd1, ve1, nhalf_sb[:, 0:TPB], ALU.pow).then_inc(rstd_1, 1)

            def rstd2_of(b):
                pool.wait_ge(aggr_2, 2 * b + 2)
                nc.gpsimd.tensor_tensor(ve2, mv2[:, :, 1], eps_sb[:, 0:TPB], ALU.add).then_inc(var_2, 1)
                pool.wait_ge(var_2, b + 1)
                nc.gpsimd.tensor_tensor(rstd2, ve2, nhalf_sb[:, 0:TPB], ALU.pow).then_inc(rstd_2, 1)

            def scatter(i, p):
                wait_apart_pool(f"staged{p}", staged[p], 32 * i + 32)
                for t in range(4):
                    for c in range(2):
                        nc.gpsimd.indirect_dma_start(
                            xs, bass.IndirectOffsetOnAxis(ap=istage[:, p, 2 * t + c:2 * t + c + 1], axis=0),
                            xstage[:, p, t, :], None).then_inc(scattered[p], 16)

            def scatter_y(m, i):
                if some(TILES * m + i):
                    pool.wait_ge(y_waited, TILES * m + i)
                pool.wait_ge(pair_ready, TILES * m + i + 1)
                wait_apart_pool("y_ready", y_ready, TILES * m + i + 1).then_inc(y_waited, 1)
                nc.gpsimd.indirect_dma_start(
                    ys, bass.IndirectOffsetOnAxis(ap=pair[:, i % 3:i % 3 + 1], axis=0), ysb[:, i % 3, :], None,
                    bounds_check=2 * NTOK - 1, oob_is_err=False).then_inc(y_stored[i % 3], 16)

            def resid(b):
                rows = ds(b * TPB, TPB)
                if some(b):
                    pool.wait_ge(resid_ready, b)
                wait_apart_pool("x1_added", x1_ready, b + 1)
                nc.gpsimd.tensor_tensor(x_sb[:, rows, :], x_sb[:, rows, :], x1_sb[:, rows, :], ALU.add).then_inc(resid_ready, 1)

            def step(k, m=None, staged_pair=None):
                def tiles(some_of):
                    for i in some_of if m is not None else ():
                        scatter_y(m, i)

                if some(0 if m is None else m):
                    tiles((-1,))
                if exists(k + 3):
                    rstd1_of(k + 3)
                tiles((0, 1))
                if exists(k + 2) and not early(k + 2):
                    rotate(nc.gpsimd, pool, k + 2)
                tiles((2, 3, 4))
                if staged_pair is not None:
                    for p in range(2):
                        scatter(staged_pair, p)
                if exists(k - 2):
                    rstd2_of(k - 2)
                    resid(k - 2)

            pool.wait_ge(xn_kept, GROUPS_A)
            rstd1_of(0)
            nc.gpsimd.tensor_tensor(x_sb, x_sb, bc(bf2_sb.rearrange("p (a d) -> p a d", a=1), [P, NT, D]),
                                    ALU.add).then_inc(resid_part, 1)
            pool.wait_ge(resid_part, 1)
            rstd1_of(1)
            rstd1_of(2)
            pool.wait_ge(slots_ready, 1)
            pool.wait_ge(xs_zeroed, 16 * ((SLOT_TILES + 7) // 8))
            for p in range(2):
                scatter(0, p)
            for k in range(LEAD):
                step(k, staged_pair=k + 1)
            step(LEAD, 0)
            with pool.Fori(1, MSTEPS - 3) as m:
                step(m + LEAD, m)
            for m in range(MSTEPS - 3, MSTEPS):
                step(m + LEAD, m)
            scatter_y(MSTEPS, -1)
            for k in range(B - 1, B + 2):
                step(k)

        @block.vector
        def _(dve):
            nc.vector.memset(ones_sb, 1.0)
            nc.vector.memset(kT, 0.0)
            for p in range(2):
                last = nc.vector.memset(vbd[:, p, 0, :], 0.0)
            last.then_inc(consts_set, 1)

            def stats_of_x(g, p, first):
                wait_apart_dve("aggr_a", aggr_a, g)
                for j in range(4):
                    last = nc.vector.bn_stats(stA[:, j, :], x_sb[:, ds(4 * g + j, 1), :].rearrange("p a d -> p (a d)"))
                last.then_inc(stats_a, 1)
                wait_apart_dve("stats_a", stats_a, g + 1)
                for j in range(4):
                    last = nc.vector.bn_aggr(mvA[:, p, j, :], stA[:, j, :])
                last.then_inc(aggr_a, 1)

            def normalise(g, p, first):
                dve.wait_ge(rstd_a, g + 1)
                if not first:
                    dve.wait_ge(xnT_psum, g - 1)
                    dve.wait_ge(xn_kept, g - 1)
                    dve.wait_ge(xb_kept, g - 1)
                for j in range(4):
                    last = nc.vector.tensor_scalar(
                        xnst[:, p, j, :], x_sb[:, ds(4 * g + j, 1), :].rearrange("p a d -> p (a d)"),
                        mvA[:, p, j, 0:1], rsA[:, p, j:j + 1], ALU.subtract, ALU.mult)
                last.then_inc(xn_ready, 1)

            def keep_scores(g, p):
                dve.wait_ge(gate_psum, g + 1)
                nc.vector.tensor_copy(sc[:, ds(4 * g, 4), :].rearrange("p t e -> p (t e)"),
                                      bank[2 + p][:, 0:4 * E]).then_inc(gate_kept, 1)

            dve.wait_ge(x_in[0], 16)
            stats_of_x(0, 0, True)
            dve.wait_ge(x_in[1], 16)
            stats_of_x(1, 1, True)
            normalise(0, 0, True)
            dve.wait_ge(x_in[2], 16)
            stats_of_x(2, 0, False)
            normalise(1, 1, True)
            dve.wait_ge(x_in[3], 16)
            with dve.Fori(0, (GROUPS_A - 4) // 2) as i:
                stats_of_x(2 * i + 3, 1, False)
                normalise(2 * i + 2, 0, False)
                keep_scores(2 * i, 0)
                stats_of_x(2 * i + 4, 0, False)
                normalise(2 * i + 3, 1, False)
                keep_scores(2 * i + 1, 1)
            g = GROUPS_A - 4
            stats_of_x(g + 3, 1, False)
            normalise(g + 2, 0, False)
            keep_scores(g, 0)
            normalise(g + 3, 1, False)
            for g in range(GROUPS_A - 3, GROUPS_A):
                keep_scores(g, g % 2)

            def stats_of_xn(b):
                if some(b):
                    dve.wait_ge(h_ready, b)
                    wait_apart_dve("aggr_1", aggr_1, b)
                for t in range(TPB):
                    last = nc.vector.bn_stats(st1[:, t, :], xn_sb[:, ds(b * TPB + t, 1), 0:D].rearrange("p a d -> p (a d)"))
                last.then_inc(stats_1, 1)
                wait_apart_dve("stats_1", stats_1, b + 1)
                for t in range(TPB):
                    last = nc.vector.bn_aggr(mv1[:, t, :], st1[:, t, :])
                last.then_inc(aggr_1, 1)

            def h_of(b):
                dve.wait_ge(rstd_1, b + 1)
                if some(b):
                    dve.wait_ge(hT_psum, b)
                for t in range(TPB):
                    row = ds(b * TPB + t, 1)
                    last = nc.vector.tensor_scalar(
                        hbuf[:, t, :], xn_sb[:, row, 0:D].rearrange("p a d -> p (a d)"),
                        mv1[:, t, 0:1], rstd1[:, t:t + 1], ALU.subtract, ALU.mult)
                last.then_inc(h_ready, 1)

            def bias(b):
                dve.wait_ge(qkv_psum, b + 1)
                if some(b):
                    semaphore, value = rope_count(b - 1)
                    dve.wait_ge(semaphore, value)
                    dve.wait_ge(heads_psum, b)
                src = qkv_bank[:, 0:TPB * 192].rearrange("p (t c) -> p t c", t=TPB)
                nc.vector.tensor_tensor(qkb, src[:, :, 0:160],
                                        bc(bqkv_sb[:, 0:160].rearrange("p (a c) -> p a c", a=1), [P, TPB, 160]), ALU.add)
                for t in range(TPB):
                    last = nc.vector.tensor_tensor(
                        vb[:, t], bc(src[:, t, 160:192].rearrange("p (a c) -> p a c", a=1), [P, G, 32]),
                        bc(bqkv_sb[:, 160:192].rearrange("p (a c) -> p a c", a=1), [P, G, 32]), ALU.add)
                last.then_inc(qkv_biased, 1)

            def values_T(b):
                dve.wait_ge(heads_psum, b + 1)
                if some(b):
                    dve.wait_ge(vbd_ready, b)
                nc.vector.transpose(vt, qkv_bank[:, 0:T]).then_inc(vt_ready, 1)

            steps = [0]

            def link(ins):
                steps[0] += 1
                ins.then_inc(route_chain, 1)
                dve.wait_ge(route_chain, steps[0])

            dve.wait_ge(xn_kept, GROUPS_A)
            stats_of_xn(0)
            dve.wait_ge(gate_kept, GROUPS_A)
            full = [P, NT, E]

            def per_tok(ap):
                return bc(ap.rearrange("p (t a) -> p t a", a=1), full)

            def per_exp(ap):
                return bc(ap.rearrange("p (a e) -> p a e", a=1), full)

            rest = sc
            for c in range(2):
                link(nc.vector.tensor_reduce(top[:, c, :], rest, AX.X, ALU.max))
                link(nc.vector.tensor_tensor(tmp[:, 0], rest, per_tok(top[:, c, :]), ALU.is_ge))
                link(nc.vector.tensor_tensor(tmp[:, 0], tmp[:, 0], per_exp(rev_sb), ALU.mult))
                link(nc.vector.tensor_reduce(pick, tmp[:, 0], AX.X, ALU.max))
                link(nc.vector.tensor_tensor(oh[:, c], tmp[:, 0], per_tok(pick), ALU.is_equal))
                if c == 0:
                    link(nc.vector.scalar_tensor_tensor(tmp[:, 1], oh[:, 0], -3e38, sc, ALU.mult, ALU.add))
                    rest = tmp[:, 1]
            nc.vector.tensor_tensor(asum, oh[:, 0], oh[:, 1], ALU.add).then_inc(pairs_ready, 1)
            h_of(0)
            stats_of_xn(1)
            link(nc.vector.scalar_tensor_tensor(tmp[:, 0], sc, -1.0, sc, ALU.mult, ALU.max))
            for c in range(2):
                link(nc.vector.tensor_tensor(dist[:, c], per_tok(top[:, c, :]), sc, ALU.subtract))
                link(nc.vector.tensor_tensor(tmp[:, 1], tmp[:, 0], per_tok(top[:, c, :]), ALU.max))
                link(nc.vector.scalar_tensor_tensor(keep[:, c], tmp[:, 1], JITTER2, dist[:, c], ALU.mult, ALU.is_ge))
            link(nc.vector.tensor_tensor(tmp[:, 0], keep[:, 1], oh[:, 0], ALU.mult))
            link(nc.vector.tensor_tensor(keep[:, 1], keep[:, 1], tmp[:, 0], ALU.subtract))
            nc.vector.tensor_scalar(dist, dist, 0.0, None, ALU.max).then_inc(dist_ready, 1)

            dve.wait_ge(ranks_psum, 1)
            link(nc.vector.tensor_copy(tot.rearrange("p t e -> p (t e)"), bank[6][:, 256:512]))
            for e in range(E):
                last = nc.vector.tensor_tensor_scan(incl[:, :, e], ones_sb[:, 0:NT], tot[:, :, e], 0.0, ALU.mult, ALU.add)
            link(last)
            link(nc.vector.tensor_tensor(slotm, incl, tot, ALU.subtract))
            link(nc.vector.tensor_tensor(slotm.rearrange("p t e -> p (t e)"), bank[6][:, 0:256],
                                         slotm.rearrange("p t e -> p (t e)"), ALU.add))
            link(nc.vector.tensor_scalar(cnt[:, 0, :], incl[:, NT - 1, :], 1.0 / P, (P - 1) / P - 0.498, ALU.mult, ALU.add))
            link(nc.vector.tensor_scalar(cnt[:, 0, :], cnt[:, 0, :], 8388608.0, None, ALU.add))
            link(nc.vector.tensor_scalar(cnt[:, 0, :], cnt[:, 0, :], -8388608.0, None, ALU.add))
            link(nc.vector.tensor_tensor_scan(cnt[:, 1, :], ones_sb[:, 0:E], cnt[:, 0, :], 0.0, ALU.mult, ALU.add))
            link(nc.vector.tensor_tensor(cnt[:, 2, :], cnt[:, 1, :], cnt[:, 0, :], ALU.subtract))
            link(nc.vector.tensor_scalar(cnt[:, 2, :], cnt[:, 2, :], float(P), None, ALU.mult))
            link(nc.vector.tensor_tensor(slotm, slotm, per_exp(cnt[:, 2, :]), ALU.add))
            for c in range(2):
                link(nc.vector.tensor_tensor(tmp[:, c], slotm, oh[:, c], ALU.mult))
                link(nc.vector.tensor_reduce(slotf[:, :, c], tmp[:, c], AX.X, ALU.add))
            nc.vector.tensor_scalar(xn_sb[:, :, D], slotgrid_sb[:, 0:NT], 2.0, None, ALU.mult)
            nc.vector.tensor_copy(xn_sb[:, :, D + 1], slotf[:, :, 1])
            nc.vector.tensor_copy(slot, slotf).then_inc(slots_ready, 1)
            dve.wait_ge(small_in, 16 * N_SMALL)
            dve.wait_ge(gate_in, 32)
            nc.vector.tensor_copy(identb_sb, ident_sb)
            for p in range(2):
                last = nc.vector.tensor_copy(
                    vbd[:, p, 1:NBLK + 1, NKV * HD:VW],
                    bc(vmask_sb[:, NKV * HD:VW].rearrange("p (a c) -> p a c", a=1), [P, NBLK, NKV]))
            last.then_inc(consts_set, 1)


            h_of(1)
            bias(0)
            rotate(nc.vector, dve, 0)
            stats_of_xn(2)
            values_T(0)
            h_of(2)
            bias(1)
            rotate(nc.vector, dve, 1)

            grid3 = [P, SLOT_TILES, 7]
            link(nc.vector.tensor_tensor(past.rearrange("p (j e) -> p j e", e=7), grid_sb.rearrange("p (j e) -> p j e", e=7),
                                         bc(cnt[:, 1, 0:7].rearrange("p (a e) -> p a e", a=1), grid3), ALU.is_ge))
            link(nc.vector.tensor_reduce(tef, past.rearrange("p (j e) -> p j e", e=7), AX.X, ALU.add))
            nc.vector.tensor_scalar(te, tef, float(ESTRIDE), None, ALU.mult).then_inc(experts_ready, 1)
            dve.wait_ge(route_exp, 1)
            link(nc.vector.tensor_tensor(tmp, dist, keep, ALU.mult))
            for c in range(2):
                link(nc.vector.tensor_reduce(mult[:, :, c], tmp[:, c], AX.X, ALU.add))
            nc.vector.reciprocal(mult, mult).then_inc(mult_ready, 1)

            def values(b, p):
                dve.wait_ge(vt_ready, b + 1)
                if some(b - 1):
                    dve.wait_ge(pv_psum, b - 1)
                nc.vector.tensor_tensor(
                    vbd[:, p, 1:NBLK + 1, 0:NKV * HD], vt.rearrange("p (n c) -> p n c", n=NBLK),
                    bc(vmask_sb[:, 0:NKV * HD].rearrange("p (a c) -> p a c", a=1), [P, NBLK, NKV * HD]),
                    ALU.mult).then_inc(vbd_ready, 1)

            def shift(b, u):
                dve.wait_ge(scores_psum, UNITS * b + u + 1)
                for n in range(2):
                    src = bank[u % 2][:, n * 256:(n + 1) * 256].rearrange("p (h g k) -> p g h k", h=2, k=WIN)
                    last = nc.vector.tensor_reduce(rmax[:, u, n, :], src, AX.XY, ALU.max)
                last.then_inc(rowmax_ready, 1)
                dve.wait_ge(rowmax_ready, UNITS * b + u + 1)
                if some(b):
                    dve.wait_ge(pT_ready, UNITS * b + u - (UNITS - 1))
                for n in range(2):
                    shape = [P, 2, G, WIN]
                    last = nc.vector.tensor_tensor(
                        S[:, u, n * 256:(n + 1) * 256].rearrange("p (h g k) -> p h g k", h=2, k=WIN),
                        bank[u % 2][:, n * 256:(n + 1) * 256].rearrange("p (h g k) -> p h g k", h=2, k=WIN),
                        bc(rmax[:, u, n, :].rearrange("p (a g b) -> p a g b", a=1, b=1), shape), ALU.subtract)
                last.then_inc(shifted, 1)

            def weights_T(b, u):
                dve.wait_ge(exp_ready, UNITS * b + u + 1)
                if some(b):
                    dve.wait_ge(pv_psum, b)
                nc.vector.transpose(pT[:, 4 * u:4 * u + 4].rearrange("p n g q -> p (n g q)"), S[:, u, :]).then_inc(pT_ready, 1)

            def norm(b):
                dve.wait_ge(pv_psum, b + 1)
                pv = turn_bank[:, 0:NBLK * VW].rearrange("p (n c) -> p n c", c=VW)
                nc.vector.reciprocal(rsum, pv[:, :, NKV * HD:VW]).then_inc(rsum_ready, 1)
                dve.wait_ge(rsum_ready, b + 1)
                nc.vector.tensor_tensor(
                    on.rearrange("p (n h d) -> p n h d", h=NKV, d=HD),
                    pv[:, :, 0:NKV * HD].rearrange("p n (h d) -> p n h d", d=HD),
                    bc(rsum.rearrange("p n (h a) -> p n h a", a=1), [P, NBLK, NKV, HD]), ALU.mult).then_inc(pv_normed, 1)
                dve.wait_ge(pv_normed, b + 1)
                nc.vector.transpose(outT, on).then_inc(outT_ready, 1)

            def residual(b):
                dve.wait_ge(wo_psum, b + 1)
                rows = ds(b * TPB, TPB)
                nc.vector.tensor_tensor(x1_sb[:, rows, :], qkv_bank[:, T:2 * T].rearrange("p (t d) -> p t d", t=TPB),
                                        x1_sb[:, rows, :], ALU.add).then_inc(x1_ready, 1)
                wait_apart_dve("x1_ready", x1_ready, b + 1)
                for t in range(TPB):
                    last = nc.vector.bn_stats(st2[:, t, :], x1_sb[:, ds(b * TPB + t, 1), :].rearrange("p a d -> p (a d)"))
                last.then_inc(stats_2, 1)
                if some(b):
                    dve.wait_ge(h2_ready, b)
                wait_apart_dve("stats_2", stats_2, b + 1)
                for t in range(TPB):
                    nc.vector.bn_aggr(mv2[:, t, :], st2[:, t, :]).then_inc(aggr_2, 1)

            def h2_of(b):
                dve.wait_ge(rstd_2, b + 1)
                if some(b):
                    dve.wait_ge(h2T_psum, b)
                for t in range(TPB):
                    last = nc.vector.tensor_scalar(
                        h2[:, t, :], x1_sb[:, ds(b * TPB + t, 1), :].rearrange("p a d -> p (a d)"),
                        mv2[:, t, 0:1], rstd2[:, t:t + 1], ALU.subtract, ALU.mult)
                last.then_inc(h2_ready, 1)

            def gated(m, i):
                j, p, b = TILES * m + i, i % 2, i % 3
                dve.wait_ge(slots_in[b], 16 * (TILES // 3 * m + i // 3 + 1))
                if some(TILES // 3 * m + i // 3):
                    dve.wait_ge(y_stored[b], 16 * (TILES // 3 * m + i // 3))
                nc.vector.scalar_tensor_tensor(pair[:, b:b + 1], xsb[:, b, D + 1:XW], slotgrid_sb[:, ds(j, 1)],
                                               xsb[:, b, D:D + 1], ALU.is_equal, ALU.add).then_inc(pair_ready, 1)
                dve.wait_ge(h3_psum, j + 1)
                dve.wait_ge(silu_ready, j + 1)
                if some(j - 1):
                    dve.wait_ge(iT_psum, j - 1)
                nc.vector.tensor_tensor(inter[:, p, :], h3_bank[:, 0:FE], act1[:, p, :], ALU.mult).then_inc(inter_ready, 1)

            def inter_T(m, i):
                j, p = TILES * m + i, i % 2
                dve.wait_ge(iT_psum, j + 1)
                if some(j - 1):
                    dve.wait_ge(y_psum, j - 1)
                nc.vector.tensor_copy(iT[:, p, :], iT_bank[0:FP, :]).then_inc(iT_ready, 1)

            def step(k, p, m=None):
                def tile_gated(i):
                    if m is not None:
                        gated(m, i)

                def tile_T(i):
                    if m is not None:
                        inter_T(m, i)

                if exists(k - 2):
                    norm(k - 2)
                if exists(k + 3):
                    stats_of_xn(k + 3)
                tile_gated(0)
                if exists(k - 1):
                    weights_T(k - 1, 0)
                    weights_T(k - 1, 1)
                if exists(k):
                    values(k, p)
                tile_T(0)
                if exists(k + 1):
                    values_T(k + 1)
                if exists(k):
                    shift(k, 0)
                tile_gated(1)
                if exists(k - 1):
                    weights_T(k - 1, 2)
                tile_T(1)
                if exists(k):
                    shift(k, 1)
                tile_gated(2)
                if exists(k + 2):
                    bias(k + 2)
                    if early(k + 2):
                        rotate(nc.vector, dve, k + 2)
                if exists(k - 1):
                    weights_T(k - 1, 3)
                if exists(k + 3):
                    h_of(k + 3)
                tile_T(2)
                if exists(k):
                    shift(k, 2)
                tile_gated(3)
                tile_T(3)
                if exists(k):
                    shift(k, 3)
                tile_gated(4)
                tile_T(4)
                tile_gated(5)
                if exists(k - 2):
                    residual(k - 2)
                tile_T(5)
                if exists(k - 2):
                    h2_of(k - 2)

            dve.wait_ge(xb_kept, GROUPS_A)
            dve.wait_ge(consts_set, 2)
            for k in range(LEAD):
                step(k, k % 2)
            step(LEAD, LEAD % 2, 0)
            with dve.Fori(0, (MSTEPS - 4) // 2) as i:
                step(2 * i + LEAD + 1, (LEAD + 1) % 2, 2 * i + 1)
                step(2 * i + LEAD + 2, LEAD % 2, 2 * i + 2)
            for m in range(MSTEPS - 3, MSTEPS):
                step(m + LEAD, (m + LEAD) % 2, m)

            def finish(i):
                p = i % 2
                dve.wait_ge(down_psum, i + 1)
                dve.wait_ge(resid_ready, 2 * i + 2)
                if i >= 2:
                    dve.wait_ge(stored[p], 16 * (i // 2))
                nc.vector.tensor_tensor(osb[:, p], bank[6 + p].rearrange("p (t d) -> p t d", t=4),
                                        x_sb[:, 4 * i:4 * i + 4, :], ALU.add).then_inc(ff_added, 1)
                dve.wait_ge(ff_added, i + 1)
                dve.wait_ge(pairs_in[i % 4], 16 * (i // 4 + 1))
                for c in range(2):
                    for t in range(4):
                        last = nc.vector.scalar_tensor_tensor(
                            osb[:, p, t, :], yrow[:, i % 4, t, c * D:(c + 1) * D], mult[:, 4 * i + t, c:c + 1],
                            osb[:, p, t, :], ALU.mult, ALU.add)
                    last.then_inc((first_added, combined)[c], 1)
                    if c == 0:
                        dve.wait_ge(first_added, i + 1)

            step(B - 1, (B - 1) % 2)
            step(B, B % 2)
            dve.wait_ge(mult_ready, 1)
            finish(0)
            finish(1)
            step(B + 1, (B + 1) % 2)
            for i in range(2, GROUPS_A):
                finish(i)

        @block.scalar
        def _(act):
            act.dma_start(ident_sb, ident).then_inc(gate_in, 16)
            act.dma_start(gate_sb, gate).then_inc(gate_in, 16)
            act.dma_start(maskb_sb, maskadd).then_inc(mask_in, 16)

            def keep_xn(g, p):
                act.wait_ge(xn_ready, g + 1)
                nc.scalar.activation(xn_sb[:, ds(4 * g, 4), 0:D], xnst[:, p], ACT.Copy).then_inc(xn_kept, 1)

            def take_xnT(g, p, first):
                act.wait_ge(xnT_psum, g + 1)
                if not first:
                    act.wait_ge(gate_psum, g - 1)
                nc.scalar.activation(xnT[:, p, :], bank[p], ACT.Copy).then_inc(xnT_ready, 1)

            for p in range(2):
                keep_xn(p, p)
                take_xnT(p, p, True)
            with act.Fori(1, GROUPS_A // 2) as i:
                for p in range(2):
                    keep_xn(2 * i + p, p)
                    take_xnT(2 * i + p, p, False)

            act.wait_ge(dist_ready, 1)
            nc.scalar.activation(dist, dist, ACT.Exp, scale=-1.0).then_inc(route_exp, 1)

            act.wait_ge(small_in, 16 * N_SMALL)

            def take_hT(b):
                act.wait_ge(hT_psum, b + 1)
                if some(b):
                    act.wait_ge(qkv_psum, b)
                nc.scalar.activation(hT, turn_bank[:, T:2 * T], ACT.Identity, bias=b1c, scale=g1c).then_inc(hT_ready, 1)

            def take_h2T(b):
                act.wait_ge(h2T_psum, b + 1)
                nc.scalar.activation(h2T_sb[:, ds(b * T, T)], turn_bank[:, 0:T], ACT.Identity, bias=b2c, scale=g2c
                                     ).then_inc(h2T_ready, 1)

            def take_keys(b, p):
                act.wait_ge(heads_psum, b + 1)
                if some(b - 1):
                    act.wait_ge(scores_psum, G * (b - 1))
                for g in range(G):
                    rows = slice(g * 32, (g + 1) * 32)
                    last = nc.scalar.activation(kT[rows, p, g, WIN:WIN + T], turn_bank[rows, T:2 * T], ACT.Copy)
                last.then_inc(kT_ready, 1)

            def take_queries(b, p):
                for h in range(NKV):
                    last = nc.scalar.activation(qbd[:, p, :, h, :], turn_bank[:, 0:T].rearrange("p (n q) -> p n q", q=WIN),
                                                ACT.Copy, scale=qmask_sb[:, h:h + 1])
                last.then_inc(qbd_ready, 1)

            def exps(b, g):
                act.wait_ge(shifted, G * b + g + 1)
                nc.scalar.activation(S[:, g, :], S[:, g, :], ACT.Exp).then_inc(exp_ready, 1)

            def take_xsT(m, i):
                j, p = TILES * m + i, i % 2
                act.wait_ge(xsT_psum, j + 1)
                if some(j - 1):
                    act.wait_ge(h3_psum, j - 1)
                nc.scalar.activation(xsT[:, p, :], y_bank[:, D:D + P], ACT.Copy).then_inc(xsT_ready, 1)

            def silu(m, i):
                j, p = TILES * m + i, i % 2
                act.wait_ge(h1_psum, j + 1)
                if some(j - 1):
                    act.wait_ge(inter_ready, j - 1)
                nc.scalar.activation(act1[:, p, :], h1_bank[:, 0:FE], ACT.Silu).then_inc(silu_ready, 1)

            def take_y(m, i):
                act.wait_ge(y_psum, TILES * m + i + 1)
                if some(TILES // 3 * m + i // 3):
                    act.wait_ge(y_stored[i % 3], 16 * (TILES // 3 * m + i // 3))
                nc.scalar.activation(ysb[:, i % 3, :], y_bank[:, 0:D], ACT.Copy).then_inc(y_ready, 1)

            def gelu(i):
                for c in range(FC):
                    act.wait_ge(up_psum, FC * i + c + 1)
                    if i >= 4:
                        act.wait_ge(down_psum, i - 3)
                    nc.scalar.activation(gT[i % 4][:, c, :], bank[4 + c % 2], ACT.Gelu, bias=cols_sb[:, 4 + c:5 + c]
                                         ).then_inc(gelu_ready, 1)

            def step(k, p, m=None):
                def slots_T(i):
                    if m is not None and within(TILES * m + i + 2):
                        take_xsT(m, i + 2)

                def tile(i):
                    if is_last(k) and i in (0, 1, 3, 5):
                        gelu((0, 1, 3, 5).index(i))
                    if m is not None:
                        silu(m, i)
                        if some(TILES * m + i):
                            take_y(m, i - 1)
                        if i not in (3, 4):
                            slots_T(i)

                tile(0)
                if exists(k + 1):
                    take_keys(k + 1, 1 - p)
                    take_queries(k + 1, 1 - p)
                for i in range(1, 4):
                    tile(i)
                if exists(k + 3):
                    take_hT(k + 3)
                if exists(k - 3):
                    take_h2T(k - 3)
                slots_T(3)
                tile(4)
                if exists(k):
                    for u in range(UNITS):
                        exps(k, u)
                slots_T(4)
                tile(5)

            take_hT(0)
            take_hT(1)
            take_keys(0, 0)
            take_queries(0, 0)
            take_hT(2)
            for k in range(LEAD):
                step(k, k % 2)
            take_xsT(0, 0)
            take_xsT(0, 1)
            step(LEAD, LEAD % 2, 0)
            with act.Fori(0, (MSTEPS - 4) // 2) as i:
                step(2 * i + LEAD + 1, (LEAD + 1) % 2, 2 * i + 1)
                step(2 * i + LEAD + 2, LEAD % 2, 2 * i + 2)
            for m in range(MSTEPS - 3, MSTEPS):
                step(m + LEAD, (m + LEAD) % 2, m)
            take_y(MSTEPS, -1)
            step(B - 1, (B - 1) % 2)
            for k in range(B, B + 3):
                gelu(k - B + 4)
                step(k, k % 2)
            gelu(GROUPS_A - 1)

        @block.tensor
        def _(pe):
            def transpose_xn(g, p, first):
                pe.wait_ge(xn_ready, g + 1)
                if not first:
                    pe.wait_ge(xnT_ready, g - 1)
                for j in range(4):
                    last = nc.tensor.transpose(bank[p][:, j * P:(j + 1) * P], xnst[:, p, j, :], ident_sb)
                last.then_inc(xnT_psum, 1)

            def gates(g, p, first):
                pe.wait_ge(xnT_ready, g + 1)
                if not first:
                    pe.wait_ge(gate_kept, g - 1)
                for j in range(4):
                    last = nc.tensor.matmul(bank[2 + p][:, j * E:(j + 1) * E], xnT[:, p, j * P:(j + 1) * P], gate_sb,
                                            start=True, stop=True)
                last.then_inc(gate_psum, 1)

            pe.wait_ge(gate_in, 32)
            transpose_xn(0, 0, True)
            transpose_xn(1, 1, True)
            gates(0, 0, True)
            transpose_xn(2, 0, False)
            gates(1, 1, True)
            with pe.Fori(0, (GROUPS_A - 4) // 2) as i:
                transpose_xn(2 * i + 3, 1, False)
                gates(2 * i + 2, 0, False)
                transpose_xn(2 * i + 4, 0, False)
                gates(2 * i + 3, 1, False)
            transpose_xn(GROUPS_A - 1, 1, False)
            gates(GROUPS_A - 2, 0, False)
            gates(GROUPS_A - 1, 1, False)

            pe.wait_ge(small_in, 16 * N_SMALL)
            pe.wait_ge(consts_set, 1)
            pe.wait_ge(pairs_ready, 1)
            flat = asum.rearrange("p t e -> p (t e)")
            nc.tensor.matmul(bank[6][:, 0:256], tri_sb, flat, start=True, stop=True)
            nc.tensor.matmul(bank[6][:, 256:512], ones_sb, flat, start=True, stop=True).then_inc(ranks_psum, 1)

            def transpose_h(b):
                pe.wait_ge(h_ready, b + 1)
                if some(b):
                    pe.wait_ge(hT_ready, b)
                for t in range(TPB):
                    last = nc.tensor.transpose(turn_bank[:, T + t * P:T + (t + 1) * P], hbuf[:, t, :], ident_sb)
                last.then_inc(hT_psum, 1)

            def qkv(b):
                pe.wait_ge(hT_ready, b + 1)
                if some(b):
                    pe.wait_ge(qkv_biased, b)
                    pe.wait_ge(vt_ready, b)
                if some(b - 4):
                    pe.wait_ge(x1_ready, b - 4)
                for t in range(TPB):
                    last = nc.tensor.matmul(qkv_bank[:, t * 192:(t + 1) * 192], hT[:, t * P:(t + 1) * P], wqkv_sb,
                                            start=True, stop=True)
                last.then_inc(qkv_psum, 1)

            def heads(b, hT_out):
                pe.wait_ge(qkv_biased, b + 1)
                semaphore, value = rope_count(b)
                pe.wait_ge(semaphore, value)
                pe.wait_ge(hT_ready, hT_out)
                if some(b - 2):
                    pe.wait_ge(pv_normed, b - 2)
                if some(b - 3):
                    pe.wait_ge(x1_ready, b - 3)
                for t in range(TPB):
                    cols = slice(t * P, (t + 1) * P)
                    nc.tensor.transpose(turn_bank[:, cols], qr[:, t, :], ident_sb)
                    nc.tensor.transpose(turn_bank[:, T + t * P:T + (t + 1) * P], kr[:, t].rearrange("p g c -> p (g c)"), ident_sb)
                    last = nc.tensor.transpose(qkv_bank[:, cols], vb[:, t].rearrange("p g c -> p (g c)"), ident_sb)
                last.then_inc(heads_psum, 1)

            def scores(b, p, u):
                if u == 0:
                    pe.wait_ge(qbd_ready, b + 1)
                    pe.wait_ge(kT_ready, b + 1)
                if some(UNITS * b + u - 1):
                    pe.wait_ge(shifted, UNITS * b + u - 1)
                nc.tensor.matmul(bank[u % 2], identb_sb,
                                 bc(maskb_sb[:, 4 * u * WIN:(4 * u + 4) * WIN].rearrange("p (h a k) -> p h a k", a=1, k=WIN),
                                    [P, 4, G, WIN]), start=True, stop=False)
                for i in range(2):
                    n = 2 * u + i
                    last = nc.tensor.matmul(
                        bank[u % 2][:, i * 256:(i + 1) * 256], qbd[:, p, n].rearrange("p h q -> p (h q)"),
                        kT[:, p, :, n * WIN:n * WIN + KW].rearrange("p g (h k) -> p h g k", k=WIN), start=False, stop=(i == 1))
                last.then_inc(scores_psum, 1)

            def transpose_h2(b):
                pe.wait_ge(h2_ready, b + 1)
                if some(b):
                    pe.wait_ge(h2T_ready, b)
                for t in range(TPB):
                    last = nc.tensor.transpose(turn_bank[:, t * P:(t + 1) * P], h2[:, t, :], ident_sb)
                last.then_inc(h2T_psum, 1)

            def attend(b, p, half, hT_out, h2T_out):
                if half == 0:
                    pe.wait_ge(pT_ready, UNITS * b + UNITS)
                    pe.wait_ge(vbd_ready, b + 1)
                    pe.wait_ge(hT_ready, hT_out)
                    if some(h2T_out):
                        pe.wait_ge(h2T_ready, h2T_out)
                for n in range(half * NBLK // 2, (half + 1) * NBLK // 2):
                    for i in range(2):
                        last = nc.tensor.matmul(turn_bank[:, n * VW:(n + 1) * VW],
                                                pT[:, 2 * n + i].rearrange("p g q -> p (g q)"),
                                                vbd[:, p, n + i, :], start=(i == 0), stop=(i == 1))
                if half == 1:
                    last.then_inc(pv_psum, 1)

            def project(b, qkv_out, vt_out):
                pe.wait_ge(outT_ready, b + 1)
                pe.wait_ge(qkv_biased, qkv_out)
                pe.wait_ge(vt_ready, vt_out)
                if some(b):
                    pe.wait_ge(x1_ready, b)
                for t in range(TPB):
                    last = nc.tensor.matmul(qkv_bank[:, T + t * P:T + (t + 1) * P], outT[:, t * P:(t + 1) * P], wo_sb,
                                            start=True, stop=True)
                last.then_inc(wo_psum, 1)

            def expert_of(j):
                return pe.value_load(te[0:1, ds(j, 1)], min_val=0, max_val=(E - 1) * ESTRIDE)

            def transpose_xs(m, i):
                j = TILES * m + i
                pe.wait_ge(slots_in[i % 3], 16 * (TILES // 3 * m + i // 3 + 1))
                if some(j):
                    pe.wait_ge(xsT_ready, j)
                if some(j - 2):
                    pe.wait_ge(y_ready, j - 2)
                nc.tensor.transpose(y_bank[:, D:D + P], xsb[:, i % 3, 0:D], ident_sb).then_inc(xsT_psum, 1)

            def up_products(m, i, at):
                j, p = TILES * m + i, i % 2
                pe.wait_ge(xsT_ready, j + 1)
                if some(j):
                    pe.wait_ge(silu_ready, j)
                    pe.wait_ge(inter_ready, j)
                nc.tensor.matmul(h1_bank[:, 0:FE], xsT[:, p, :], w1_sb[:, ds(at, FE)], start=True, stop=True).then_inc(h1_psum, 1)
                nc.tensor.matmul(h3_bank[:, 0:FE], xsT[:, p, :], w3_sb[:, ds(at, FE)], start=True, stop=True).then_inc(h3_psum, 1)

            def transpose_inter(m, i):
                j, p = TILES * m + i, i % 2
                pe.wait_ge(inter_ready, j + 1)
                if some(j):
                    pe.wait_ge(iT_ready, j)
                for c in range(EC):
                    last = nc.tensor.transpose(iT_bank[0:FP, c * P:(c + 1) * P], inter[:, p, c * FP:(c + 1) * FP], ident_sb)
                last.then_inc(iT_psum, 1)

            def down_product(m, i, xsT_out, at):
                j, p = TILES * m + i, i % 2
                pe.wait_ge(iT_ready, j + 1)
                pe.wait_ge(xsT_ready, xsT_out)
                if some(j):
                    pe.wait_ge(y_ready, j)
                for c in range(EC):
                    last = nc.tensor.matmul(y_bank[:, 0:D], iT[:, p, c * P:(c + 1) * P], w2_sb[:, ds(at + c * P, P)],
                                            start=(c == 0), stop=(c == EC - 1))
                last.then_inc(y_psum, 1)

            def up(i):
                pe.wait_ge(h2T_ready, 2 * i + 2)
                for c in range(FC):
                    if FC * i + c >= 2:
                        pe.wait_ge(gelu_ready, FC * i + c - 1)
                    elif c == 0:
                        pe.wait_ge(silu_ready, SLOT_TILES)
                    else:
                        pe.wait_ge(inter_ready, SLOT_TILES)
                    nc.tensor.matmul(bank[4 + c % 2], wf1_sb[:, c * P:(c + 1) * P], h2T_sb[:, i * 512:(i + 1) * 512],
                                     start=True, stop=True).then_inc(up_psum, 1)

            def down(i):
                pe.wait_ge(gelu_ready, FC * i + FC)
                if i >= 2:
                    pe.wait_ge(ff_added, i - 1)
                elif i == 1:
                    pe.wait_ge(y_ready, SLOT_TILES)
                else:
                    pe.wait_ge(iT_ready, SLOT_TILES)
                for t in range(4):
                    for c in range(FC):
                        last = nc.tensor.matmul(bank[6 + i % 2][:, t * D:(t + 1) * D], gT[i % 4][:, c, t * P:(t + 1) * P],
                                                wf2_sb[:, c, :], start=(c == 0), stop=(c == FC - 1))
                last.then_inc(down_psum, 1)

            def last_step_part(i):
                if i in (2, 4):
                    down(i // 2 - 1)
                else:
                    up((0, 1, 3, 5).index(i))

            def step(k, p, m=None):
                def tile_up(i):
                    if is_last(k):
                        last_step_part(i)
                    if m is not None and i > 0:
                        if within(TILES * m + i):
                            up_products(m, i, expert[i])
                        down_product(m, i - 1, TILES * m + i + 2 if within(TILES * m + i + 1) else SLOT_TILES,
                                     expert[i - 1])

                def tile_T(i):
                    if m is not None:
                        if i == 0:
                            expert[0] = expert_of(TILES * m)
                        if within(TILES * m + i + 1):
                            expert[i + 1] = expert_of(TILES * m + i + 1)
                        transpose_inter(m, i)
                        if within(TILES * m + i + 2):
                            transpose_xs(m, i + 2)

                hT_out = k + 4 if exists(k + 3) else B
                expert = {}

                tile_up(0)
                if exists(k):
                    scores(k, p, 0)
                if exists(k + 1):
                    heads(k + 1, k + 3 if exists(k + 2) else B)
                tile_T(0)
                tile_up(1)
                if exists(k):
                    scores(k, p, 1)
                if exists(k + 2):
                    qkv(k + 2)
                tile_T(1)
                tile_up(2)
                if exists(k):
                    scores(k, p, 2)
                tile_T(2)
                tile_up(3)
                if exists(k):
                    scores(k, p, 3)
                if exists(k + 1):
                    pe.wait_ge(kT_ready, k + 2)
                    pe.wait_ge(qbd_ready, k + 2)
                elif exists(k - 2):
                    pe.wait_ge(pv_normed, k - 1)
                if exists(k - 3):
                    transpose_h2(k - 3)
                if exists(k + 3):
                    transpose_h(k + 3)
                tile_T(3)
                tile_up(4)
                if exists(k - 1):
                    attend(k - 1, 1 - p, 0, hT_out, k - 2)
                tile_T(4)
                tile_up(5)
                if exists(k - 2):
                    project(k - 2, k + 3 if exists(k + 2) else B, k + 2 if exists(k + 1) else B)
                if exists(k - 1):
                    attend(k - 1, 1 - p, 1, hT_out, k - 2)
                tile_T(5)
                if m is not None:
                    tile_up(TILES)

            pe.wait_ge(mask_in, 16)
            transpose_h(0)
            qkv(0)
            transpose_h(1)
            heads(0, 2)
            qkv(1)
            pe.wait_ge(kT_ready, 1)
            pe.wait_ge(qbd_ready, 1)
            transpose_h(2)
            for k in range(LEAD):
                step(k, k % 2)
            pe.wait_ge(experts_ready, 1)
            pe.wait_ge(weights_in, 48)
            transpose_xs(0, 0)
            transpose_xs(0, 1)
            up_products(0, 0, expert_of(0))
            step(LEAD, LEAD % 2, 0)
            with pe.Fori(0, (MSTEPS - 4) // 2) as i:
                step(2 * i + LEAD + 1, (LEAD + 1) % 2, 2 * i + 1)
                step(2 * i + LEAD + 2, LEAD % 2, 2 * i + 2)
            for m in range(MSTEPS - 3, MSTEPS):
                step(m + LEAD, (m + LEAD) % 2, m)
            step(B - 1, (B - 1) % 2)
            for k in range(B, B + 3):
                up(k - B + 4)
                step(k, k % 2)
                down(k - B + 2)
            up(GROUPS_A - 1)
            for i in range(5, GROUPS_A):
                down(i)


def constants():
    f32 = np.float32
    p = np.arange(P)
    half = HD // 2
    theta = (1.0 / 10000.0 ** (np.arange(half, dtype=f32) / f32(half))).astype(f32)
    pos = np.arange(T, dtype=f32)
    freqs = np.outer(pos, theta).astype(f32)
    c, s = np.cos(freqs).astype(f32), np.sin(freqs).astype(f32)
    cosf = np.tile(np.concatenate([c, c], 1), (1, 20)).reshape(TPB, P, 160).transpose(1, 0, 2).reshape(P, -1)
    sinf = np.tile(np.concatenate([-s, s], 1), (1, 20)).reshape(TPB, P, 160).transpose(1, 0, 2).reshape(P, -1)
    q, k = (p % WIN)[:, None], np.arange(KW)[None, :]
    valid = (k - WIN <= q) & (k > q)
    allowed = np.repeat(valid[:, None, :], NBLK, 1)
    allowed[:, 0, :WIN] = False
    maskadd = np.where(allowed, 0.0, NEG).reshape(P, -1).astype(f32)
    qmask = np.where((p // HD % NKV)[:, None] == np.arange(NKV), 1.0 / np.sqrt(f32(HD)), 0.0).astype(f32)
    col = np.concatenate([np.repeat(np.arange(NKV), HD), np.arange(NKV)])
    vmask = ((p // WIN)[:, None] == col).astype(f32)
    tri = (p[:, None] < p[None, :]).astype(f32)
    rev = np.broadcast_to(E - np.arange(E), (P, E)).astype(f32)
    grid = np.broadcast_to(np.arange(SLOT_TILES)[:, None], (P, SLOT_TILES, 7)).reshape(P, -1).astype(f32)
    slotgrid = (np.arange(SLOT_TILES)[None, :] * P + p[:, None]).astype(f32)
    return {"slotgrid": slotgrid, "ident": np.eye(P, dtype=f32), "cosf": cosf, "sinf": sinf, "maskadd": maskadd, "qmask": qmask,
            "vmask": vmask, "tri": tri, "rev": rev, "tilegrid": grid}


def laid_out(i):
    def rows(v):
        return np.broadcast_to(v, (P, v.shape[0]))

    heads = (NKV, G, HD)
    wq = i["L0_attn_Wq"].reshape(D, *heads).transpose(0, 2, 1, 3).reshape(D, D)
    bq = i["L0_attn_bq"].reshape(heads).transpose(1, 0, 2).reshape(D)

    def experts(w):
        wide = np.zeros((D, E, ESTRIDE), w.dtype)
        wide[:, :, :FE] = w.transpose(2, 0, 1)
        return wide.reshape(D, -1)

    w2 = i["L0_ffn_w2"].reshape(E, D, EC, FP).transpose(3, 0, 2, 1).reshape(FP, -1)
    return {
        "x": i["L0_attn_x"].reshape(NTOK, D),
        "wqkv": np.concatenate([wq, i["L0_attn_Wk"], i["L0_attn_Wv"]], 1),
        "bqkv": rows(np.concatenate([bq, i["L0_attn_bk"], i["L0_attn_bv"]])),
        "wo": i["L0_attn_Wo"].reshape(*heads, D).transpose(1, 0, 2, 3).reshape(D, D),
        "bo": rows(i["L0_attn_bo"]),
        "g1": i["L0_attn_g1"].reshape(D, 1), "b1": i["L0_attn_b1"].reshape(D, 1),
        "g2": i["L0_attn_g2"].reshape(D, 1), "b2": i["L0_attn_b2"].reshape(D, 1),
        "wf1": i["L0_attn_Wf1"], "bf1": i["L0_attn_bf1"].reshape(FC, P).T,
        "wf2": i["L0_attn_Wf2"].reshape(FC, P, D).transpose(1, 0, 2).reshape(P, -1),
        "bf2": rows(i["L0_attn_bf2"]),
        "gate": i["L0_ffn_gate_w"].T,
        "w1": experts(i["L0_ffn_w1"]), "w3": experts(i["L0_ffn_w3"]), "w2": w2,
    }


def kernel(**inputs):
    import concourse.bacc as bacc
    import ml_dtypes
    from concourse.bass_utils import run_bass_kernel_spmd

    arrays = laid_out({k: np.asarray(v) for k, v in inputs.items()})
    arrays.update(constants())
    arrays["maskadd"] = arrays["maskadd"].astype(ml_dtypes.bfloat16)
    nc = bacc.Bacc("TRN2", target_bir_lowering=False, num_devices=1)
    feeds, aps = {}, {}
    for name, a in arrays.items():
        a = np.ascontiguousarray(a)
        feeds[f"in_{name}"] = a
        aps[name] = nc.dram_tensor(f"in_{name}", a.shape, mybir.dt.from_np(a.dtype), kind="ExternalInput").ap()
    for name, shape in (("xs", (SLOT_TILES * P, XW)), ("ys", (2 * NTOK, D))):
        aps[name] = nc.dram_tensor(f"scratch_{name}", shape, mybir.dt.float32, kind="Internal").ap()
    aps["out"] = nc.dram_tensor("out_dram", (NTOK, D), mybir.dt.float32, kind="ExternalOutput").ap()
    layer(nc, **aps)
    r = run_bass_kernel_spmd(nc, [feeds], core_ids=[0])
    return r.results[0]["out_dram"].reshape(B, T, D)
```

```python
from contextlib import ExitStack

import numpy as np

import concourse.bass as bass
from concourse import mybir

P = 128
B, T, D = 16, 256, 128
NTOK = B * T
NT = NTOK // P
TPB = T // P
NH, NKV, HD = 16, 4, 8
G = NH // NKV
WIN = 32
NBLK = T // WIN
KW = 2 * WIN
UNITS = NBLK // 2
assert 2 * G * KW == 512 and UNITS == G
DFF = 512
FC = DFF // P
E, FE = 8, 448
EC = 4
FP = FE // EC
ESTRIDE = 512
LEAD = 3
TILES = 6
EARLY = LEAD + 1
Y_TILE = 3
MSTEPS = B - 1 - LEAD
SLOT_TILES = TILES * MSTEPS
assert SLOT_TILES >= (2 * NTOK + E * (P - 1)) // P
EPS = 1e-5
JITTER2 = 0.02
GROUPS_A = NT // 4
assert GROUPS_A // 2 == 1 + LEAD
VW = NKV * HD + NKV
XW = D + 2
NO_PAIR = 1e6
NEG = -1e30


def layer(nc, x, wqkv, bqkv, wo, bo, g1, b1, g2, b2, wf1, bf1, wf2, bf2, gate, w1, w3, w2,
          ident, cosf, sinf, maskadd, qmask, vmask, tri, rev, tilegrid, slotgrid, xs, ys, out):
    F32, F32R, BF16, I32 = mybir.dt.float32, mybir.dt.float32r, mybir.dt.bfloat16, mybir.dt.int32
    ALU, ACT, AX = mybir.AluOpType, mybir.ActivationFunctionType, mybir.AxisListType
    ds = bass.ds
    ctx = ExitStack()
    with ctx:
        def sb(name, shape, dt=F32):
            return ctx.enter_context(nc.sbuf_tensor(name, shape, dt))[:]

        def sem(name):
            return ctx.enter_context(nc.semaphore(name))

        x_sb = sb("x_sb", [P, NT, D])
        xn_sb = sb("xn_sb", [P, NT, XW])
        h2T_sb = sb("h2T_sb", [P, NTOK])
        w1_sb = sb("w1_sb", [P, E * ESTRIDE])
        w3_sb = sb("w3_sb", [P, E * ESTRIDE])
        w2_sb = sb("w2_sb", [FP, E * ESTRIDE])
        w1_high = x_sb.rearrange("p t d -> p (t d)")
        w3_high = sb("w3_high", [P, E * ESTRIDE])
        wqkv_sb = sb("wqkv_sb", [P, 192])
        bqkv_sb = sb("bqkv_sb", [P, 192])
        wo_sb = sb("wo_sb", [P, D])
        bo_sb = sb("bo_sb", [P, D])
        bf2_sb = sb("bf2_sb", [P, D])
        wf1_sb = sb("wf1_sb", [P, DFF])
        wf2_sb = sb("wf2_sb", [P, FC, D])
        cols_sb = sb("cols_sb", [P, 4 + FC])
        gate_sb = sb("gate_sb", [P, E])
        ident_sb = sb("ident_sb", [P, P])
        identb_sb = sb("identb_sb", [P, P], BF16)
        maskb_sb = sb("maskb_sb", [P, NBLK * KW], BF16)
        cos_sb = sb("cos_sb", [P, TPB * 160])
        sin_sb = sb("sin_sb", [P, TPB * 160])
        qmask_sb = sb("qmask_sb", [P, NKV])
        vmask_sb = sb("vmask_sb", [P, VW])
        tri_sb = sb("tri_sb", [P, P])
        ones_sb = sb("ones_sb", [P, P])
        rev_sb = sb("rev_sb", [P, E])
        grid_sb = sb("grid_sb", [P, SLOT_TILES * 7])
        blank_sb = sb("blank_sb", [P, 8, XW])
        slotgrid_sb = sb("slotgrid_sb", [P, SLOT_TILES])
        nhalf_sb = sb("nhalf_sb", [P, 4])
        eps_sb = sb("eps_sb", [P, 4])
        spare_sb = sb("spare_sb", [P, 10])

        stA = sb("stA", [P, 4, 6])
        mvA = sb("mvA", [P, 2, 4, 2])
        veA = sb("veA", [P, 4])
        rsA = sb("rsA", [P, 2, 4])
        xnst = sb("xnst", [P, 2, 4, D])
        xnT = sb("xnT", [P, 2, 512])

        used = [0]

        def table(*shape):
            n = int(np.prod(shape))
            used[0] += n
            names = "abcd"[:len(shape)]
            flat = h2T_sb[:, used[0] - n:used[0]]
            return flat.rearrange(f"p ({' '.join(names)}) -> p {' '.join(names)}", **dict(zip(names, shape)))

        sc = table(NT, E)
        oh = table(2, NT, E)
        top = table(2, NT)
        tmp = table(2, NT, E)
        dist = table(2, NT, E)
        keep = table(2, NT, E)
        pick = table(NT)
        asum = table(NT, E)
        tot = table(NT, E)
        incl = table(NT, E)
        slotm = table(NT, E)
        cnt = sb("cnt", [P, 3, E])
        mult = sb("mult", [P, NT, 2])
        slotf = sb("slotf", [P, NT, 2])
        slot = sb("slot", [P, NT, 2], I32)
        tef = sb("tef", [P, SLOT_TILES])
        te = sb("te", [P, SLOT_TILES], I32)

        st1 = sb("st1", [P, TPB, 6])
        mv1 = sb("mv1", [P, TPB, 2])
        ve1 = sb("ve1", [P, TPB])
        rstd1 = sb("rstd1", [P, TPB])
        hbuf = sb("hbuf", [P, TPB, D])
        hT = sb("hT", [P, T])
        qkb = sb("qkb", [P, TPB, 160])
        vb = sb("vb", [P, TPB, G, 32])
        ra = sb("ra", [P, TPB, 160])
        rb = sb("rb", [P, TPB, 160])
        qr = sb("qr", [P, TPB, P])
        kr = sb("kr", [P, TPB, G, 32])
        kT = sb("kT", [P, 2, G, WIN + T])
        qbd = sb("qbd", [P, 2, NBLK, NKV, WIN])
        vt = sb("vt", [P, T])
        vbd = sb("vbd", [P, 2, NBLK + 1, VW])
        rmax = sb("rmax", [P, UNITS, 2, G])
        S = sb("S", [P, UNITS, 512])
        past = S.rearrange("p u c -> p (u c)")[:, 0:SLOT_TILES * 7]
        pT = sb("pT", [P, 2 * NBLK, G, WIN])
        rsum = sb("rsum", [P, NBLK, NKV])
        on = sb("on", [P, T])
        outT = sb("outT", [P, T])
        st2 = sb("st2", [P, TPB, 6])
        mv2 = sb("mv2", [P, TPB, 2])
        ve2 = sb("ve2", [P, TPB])
        rstd2 = sb("rstd2", [P, TPB])
        h2 = sb("h2", [P, TPB, D])

        xsb = sb("xsb", [P, 3, XW])
        pair = sb("pair", [P, 3], I32)
        xsT = sb("xsT", [P, 2, 2, P])
        act1 = sb("act1", [P, 2, FE])
        inter = sb("inter", [P, 2, FE])
        iT = xnT[0:FP]
        ysb = sb("ysb", [P, 3, D])

        gT = [w.rearrange("p (b c n) -> p b c n", b=2, c=FC)[:, b] for w in (w1_sb, w3_sb) for b in range(2)]
        yrow = w3_high.rearrange("p (b t c) -> p b t c", b=4, t=4)

        bank = [ctx.enter_context(nc.psum_tensor(f"bank{i}", [P, 512], F32))[:] for i in range(8)]
        qkv_bank, turn_bank = bank[2], bank[3]
        h1_bank, h3_bank, iT_bank, y_bank = bank[4:8]

        small_in, x_in, weights_in = sem("small_in"), [sem(f"x_in{i}") for i in range(4)], [sem(f"weights_in{i}") for i in range(3)]
        mask_in, gate_in = sem("mask_in"), sem("gate_in")
        zeros_set, pool_consts, consts_set = sem("zeros_set"), sem("pool_consts"), sem("consts_set")
        xs_zeroed = sem("xs_zeroed")
        stats_a, aggr_a, rstd_a, var_a = sem("stats_a"), sem("aggr_a"), sem("rstd_a"), sem("var_a")
        xn_ready, stats_1, aggr_1, rstd_1, var_1 = (sem("xn_ready"), sem("stats_1"), sem("aggr_1"),
                                                    sem("rstd_1"), sem("var_1"))
        xn_kept, x_again = sem("xn_kept"), sem("x_again")
        bo_added, high_ready, low_ready, xs_high = sem("bo_added"), sem("high_ready"), sem("low_ready"), sem("xs_high")
        xnT_psum, xnT_ready, gate_psum, gate_kept = (sem("xnT_psum"), sem("xnT_ready"),
                                                     sem("gate_psum"), sem("gate_kept"))
        route_chain, route_exp, ranks_psum, pairs_ready = (sem("route_chain"), sem("route_exp"),
                                                           sem("ranks_psum"), sem("pairs_ready"))
        dist_ready, slots_ready, experts_ready, mult_ready = (sem("dist_ready"), sem("slots_ready"),
                                                              sem("experts_ready"), sem("mult_ready"))
        h_ready, hT_psum, hT_ready, qkv_psum, qkv_biased = (sem("h_ready"), sem("hT_psum"), sem("hT_ready"),
                                                            sem("qkv_psum"), sem("qkv_biased"))
        rope_parts, rope_ready, heads_psum, kT_ready, qbd_ready = (sem("rope_parts"), sem("rope_ready"),
                                                                   sem("heads_psum"), sem("kT_ready"), sem("qbd_ready"))
        rope_parts_dve, rope_ready_dve = sem("rope_parts_dve"), sem("rope_ready_dve")
        vt_ready, vbd_ready, scores_psum, rowmax_ready, shifted = (sem("vt_ready"), sem("vbd_ready"),
                                                                   sem("scores_psum"), sem("rowmax_ready"), sem("shifted"))
        exp_ready, pT_ready, pv_psum, rsum_ready, pv_normed = (sem("exp_ready"), sem("pT_ready"), sem("pv_psum"),
                                                               sem("rsum_ready"), sem("pv_normed"))
        outT_ready, wo_psum, x1_ready, stats_2, aggr_2, var_2, rstd_2 = (
            sem("outT_ready"), sem("wo_psum"), sem("x1_ready"), sem("stats_2"), sem("aggr_2"), sem("var_2"), sem("rstd_2"))
        h2_ready, h2T_psum, h2T_ready = sem("h2_ready"), sem("h2T_psum"), sem("h2T_ready")
        scattered = [sem(f"scattered{i}") for i in range(GROUPS_A)]
        slots_in = [sem(f"slots_in{i}") for i in range(3)]
        xsT_psum, xsT_ready, h1_psum, h3_psum = sem("xsT_psum"), sem("xsT_ready"), sem("h1_psum"), sem("h3_psum")
        silu_ready, inter_ready, iT_psum, iT_ready = sem("silu_ready"), sem("inter_ready"), sem("iT_psum"), sem("iT_ready")
        y_psum, y_ready, y_stored = sem("y_psum"), sem("y_ready"), [sem(f"y_stored{i}") for i in range(3)]
        resid_part, resid_ready = sem("resid_part"), sem("resid_ready")
        up_psum, gelu_ready, down_psum, ff_added = sem("up_psum"), sem("gelu_ready"), sem("down_psum"), sem("ff_added")
        pair_ready, y_waited, pairs_in = sem("pair_ready"), sem("y_waited"), [sem(f"pairs_in{i}") for i in range(4)]
        first_added, second_added, stored = sem("first_added"), sem("second_added"), sem("stored")

        g1c, b1c, g2c, b2c = (cols_sb[:, i:i + 1] for i in range(4))
        N_SMALL = 20

        spare_column = {s: i for i, s in enumerate(("aggr_a", "stats_a", "aggr_1", "stats_1", "x1_ready", "stats_2",
                                                    "y_ready", "bo_added"))}

        def spare_of(name):
            return spare_sb[:, spare_column[name]:spare_column[name] + 1]

        def wait_apart_dve(name, semaphore, value):
            nc.vector.wait_ge(semaphore, value)
            nc.vector.memset(spare_of(name), 0.0)

        def wait_apart_pool(name, semaphore, value):
            nc.gpsimd.wait_ge(semaphore, value)
            return nc.gpsimd.tensor_tensor(spare_of(name), eps_sb[:, 0:1], eps_sb[:, 0:1], ALU.add)

        def bc(ap, shape):
            return ap.broadcast_to(shape)

        def exists(b):
            return not isinstance(b, int) or 0 <= b < B

        def is_last(k):
            return isinstance(k, int) and k == B - 1

        def after_last(k):
            return isinstance(k, int) and k == B

        def within(j):
            return not isinstance(j, int) or j < SLOT_TILES

        def some(n):
            return not isinstance(n, int) or n > 0

        def early(b):
            return isinstance(b, int) and b < EARLY

        def rope_count(b):
            return (rope_ready_dve, b + 1) if early(b) else (rope_ready, b + 1 - EARLY)

        def rotate(ops, eng, b):
            parts, ready, n = (rope_parts_dve, rope_ready_dve, b) if early(b) else (rope_parts, rope_ready, b - EARLY)
            eng.wait_ge(qkv_biased, b + 1)
            flat = "p t c -> p (t c)"
            q4 = qkb.rearrange("p t (n h c) -> p (t n) h c", h=2, c=HD // 2)
            s4 = sin_sb.rearrange("p (n h c) -> p n h c", h=2, c=HD // 2)
            r4 = rb.rearrange("p t (n h c) -> p (t n) h c", h=2, c=HD // 2)
            ops.tensor_tensor(ra.rearrange(flat), qkb.rearrange(flat), cos_sb, ALU.mult)
            ops.tensor_tensor(r4[:, :, 0, :], q4[:, :, 1, :], s4[:, :, 0, :], ALU.mult)
            ops.tensor_tensor(r4[:, :, 1, :], q4[:, :, 0, :], s4[:, :, 1, :], ALU.mult).then_inc(parts, 1)
            eng.wait_ge(parts, n + 1)
            if some(b):
                eng.wait_ge(heads_psum, b)
            ops.tensor_tensor(qr, ra[:, :, 0:P], rb[:, :, 0:P], ALU.add)
            for t in range(TPB):
                last = ops.tensor_tensor(
                    kr[:, t], bc(ra[:, t, P:160].rearrange("p (a c) -> p a c", a=1), [P, G, 32]),
                    bc(rb[:, t, P:160].rearrange("p (a c) -> p a c", a=1), [P, G, 32]), ALU.add)
            last.then_inc(ready, 1)

        block = ctx.enter_context(nc.Block())

        @block.sync
        def _(sp):
            xv = x.rearrange("(t p) d -> p t d", p=P)
            for i in range(4):
                part = slice(4 * i, 4 * i + 4 if i < 3 else NT)
                sp.dma_start(x_sb[:, part, :], xv[:, part, :]).then_inc(x_in[i], 16)
            small = [(wqkv_sb, wqkv), (bqkv_sb, bqkv), (wo_sb, wo), (bo_sb, bo),
                     (bf2_sb, bf2), (wf1_sb, wf1), (cols_sb[:, 0:1], g1), (cols_sb[:, 1:2], b1), (cols_sb[:, 2:3], g2),
                     (cols_sb[:, 3:4], b2), (cols_sb[:, 4:4 + FC], bf1), (cos_sb, cosf), (sin_sb, sinf),
                     (qmask_sb, qmask), (vmask_sb, vmask), (tri_sb, tri), (rev_sb, rev), (slotgrid_sb, slotgrid), (grid_sb, tilegrid),
                     (wf2_sb, wf2.rearrange("p (c d) -> p c d", c=FC))]
            assert len(small) == N_SMALL
            for dst, src in small:
                sp.dma_start(dst, src).then_inc(small_in, 16)
            sp.dma_start(w1_sb, w1).then_inc(weights_in[0], 16)
            sp.wait_ge(zeros_set, 1)
            xz = xs.rearrange("(p r) d -> p (r d)", p=P)
            for r0 in range(0, SLOT_TILES, 8):
                n = min(8, SLOT_TILES - r0) * XW
                sp.dma_start(xz[:, r0 * XW:r0 * XW + n], blank_sb.rearrange("p r d -> p (r d)")[:, 0:n]).then_inc(xs_zeroed, 16)
            sp.dma_start(w3_sb, w3).then_inc(weights_in[1], 16)
            sp.dma_start(w2_sb, w2).then_inc(weights_in[2], 16)

            for g in range(GROUPS_A):
                sp.wait_ge(scattered[g], 8 * 16)

            def load_slots(n, p):
                if some(n):
                    sp.wait_ge(xsT_psum, 3 * n + p - 2)
                    sp.wait_ge(pair_ready, 3 * n + p - 2)
                sp.dma_start(xsb[:, p, :], xs[ds((3 * n + p) * P, P), :]).then_inc(slots_in[p], 16)

            for p in range(3):
                load_slots(0, p)
            with sp.Fori(1, SLOT_TILES // 3) as n:
                for p in range(3):
                    load_slots(n, p)

            sp.wait_ge(h1_psum, SLOT_TILES)
            sp.dma_start(x_sb, xv).then_inc(x_again, 16)
            ov = out.rearrange("(t p) d -> p t d", p=P)
            yv = ys.rearrange("(t p c) d -> p t (c d)", p=P, c=2)
            for p in range(3):
                sp.wait_ge(y_stored[p], 16 * SLOT_TILES // 3)
            sp.wait_ge(h3_psum, SLOT_TILES)

            def load_pairs(i):
                sp.dma_start(yrow[:, i % 4], yv[:, 4 * i:4 * i + 4, :]).then_inc(pairs_in[i % 4], 16)

            for i in range(4):
                load_pairs(i)
            for i in range(GROUPS_A):
                sp.wait_ge(second_added, i + 1)
                if i + 4 < GROUPS_A:
                    load_pairs(i + 4)
                sp.wait_ge(ff_added, i + 1)
                sp.dma_start(ov[:, 4 * i:4 * i + 4, :], x_sb[:, 4 * i:4 * i + 4, :]).then_inc(stored, 16)
            sp.wait_ge(stored, 16 * GROUPS_A)

        @block.gpsimd
        def _(pool):
            nc.gpsimd.memset(blank_sb[:, :, 0:D], 0.0)
            nc.gpsimd.memset(blank_sb[:, :, D:D + 1], NO_PAIR)
            nc.gpsimd.memset(blank_sb[:, :, D + 1:XW], -1.0).then_inc(zeros_set, 1)
            nc.gpsimd.memset(eps_sb, EPS)
            nc.gpsimd.memset(nhalf_sb, -0.5).then_inc(pool_consts, 1)
            pool.wait_ge(pool_consts, 1)

            def group_a1(g, p, first):
                pool.wait_ge(aggr_a, g + 1)
                pool.wait_ge(rstd_a, g)
                nc.gpsimd.tensor_tensor(veA, mvA[:, p, :, 1], eps_sb, ALU.add).then_inc(var_a, 1)
                pool.wait_ge(var_a, g + 1)
                if not first:
                    pool.wait_ge(xn_ready, g - 1)
                nc.gpsimd.tensor_tensor(rsA[:, p, :], veA, nhalf_sb, ALU.pow).then_inc(rstd_a, 1)

            group_a1(0, 0, True)
            group_a1(1, 1, True)
            with pool.Fori(0, (GROUPS_A - 2) // 2) as i:
                group_a1(2 * i + 2, 0, False)
                group_a1(2 * i + 3, 1, False)
            pool.wait_ge(small_in, 16 * N_SMALL)

            def rstd1_of(b):
                pool.wait_ge(aggr_1, b + 1)
                nc.gpsimd.tensor_tensor(ve1, mv1[:, :, 1], eps_sb[:, 0:TPB], ALU.add).then_inc(var_1, 1)
                pool.wait_ge(var_1, b + 1)
                nc.gpsimd.tensor_tensor(rstd1, ve1, nhalf_sb[:, 0:TPB], ALU.pow).then_inc(rstd_1, 1)

            def rstd2_of(b):
                pool.wait_ge(aggr_2, 2 * b + 2)
                nc.gpsimd.tensor_tensor(ve2, mv2[:, :, 1], eps_sb[:, 0:TPB], ALU.add).then_inc(var_2, 1)
                pool.wait_ge(var_2, b + 1)
                nc.gpsimd.tensor_tensor(rstd2, ve2, nhalf_sb[:, 0:TPB], ALU.pow).then_inc(rstd_2, 1)

            def scatter(g):
                for t in range(4 * g, 4 * g + 4):
                    for c in range(2):
                        nc.gpsimd.indirect_dma_start(
                            xs, bass.IndirectOffsetOnAxis(ap=slot[:, t, c:c + 1], axis=0),
                            xn_sb[:, t, :], None).then_inc(scattered[g], 16)

            def scatter_y(m, i):
                if some(TILES * m + i):
                    pool.wait_ge(y_waited, TILES * m + i)
                pool.wait_ge(pair_ready, TILES * m + i + 1)
                wait_apart_pool("y_ready", y_ready, TILES * m + i + 1).then_inc(y_waited, 1)
                nc.gpsimd.indirect_dma_start(
                    ys, bass.IndirectOffsetOnAxis(ap=pair[:, i % 3:i % 3 + 1], axis=0), ysb[:, i % 3, :], None,
                    bounds_check=2 * NTOK - 1, oob_is_err=False).then_inc(y_stored[i % 3], 16)

            def add_bo(b):
                rows = ds(b * TPB, TPB)
                if some(b):
                    pool.wait_ge(bo_added, b)
                wait_apart_pool("bo_added", h_ready, b + 1)
                nc.gpsimd.tensor_tensor(xn_sb[:, rows, 0:D], xn_sb[:, rows, 0:D],
                                        bc(bo_sb.rearrange("p (a d) -> p a d", a=1), [P, TPB, D]), ALU.add).then_inc(bo_added, 1)

            def step(k, m=None, groups=()):
                def tiles(some_of):
                    for i in some_of if m is not None else ():
                        scatter_y(m, i)

                if some(0 if m is None else m):
                    tiles((-1,))
                for g in groups[:1]:
                    scatter(g)
                if exists(k + 3):
                    rstd1_of(k + 3)
                tiles((0, 1))
                for g in groups[1:]:
                    scatter(g)
                if exists(k + 2) and not early(k + 2):
                    rotate(nc.gpsimd, pool, k + 2)
                tiles((2, 3, 4))
                if exists(k - 1):
                    if isinstance(k, int) and k <= LEAD:
                        pool.wait_ge(scattered[(k - 1) // 2], 8 * 16)
                    add_bo(k - 1)
                if exists(k - 2):
                    rstd2_of(k - 2)

            pool.wait_ge(xn_kept, GROUPS_A)
            rstd1_of(0)
            pool.wait_ge(high_ready, 1)
            nc.gpsimd.tensor_tensor(w1_sb.bitcast(F32R), w1_sb, w1_high, ALU.subtract).then_inc(low_ready, 1)
            rstd1_of(1)
            pool.wait_ge(slots_ready, 1)
            pool.wait_ge(xs_zeroed, 16 * ((SLOT_TILES + 7) // 8))
            scatter(0)
            rstd1_of(2)
            scatter(1)
            for k in range(LEAD):
                step(k, groups=(2 * k + 2, 2 * k + 3))
            step(LEAD, 0)
            with pool.Fori(1, MSTEPS - 3) as m:
                step(m + LEAD, m)
            for m in range(MSTEPS - 3, MSTEPS):
                step(m + LEAD, m)
            scatter_y(MSTEPS, -1)
            def resid(i):
                group = slice(4 * i, 4 * i + 4)
                nc.gpsimd.tensor_tensor(x_sb[:, group, :], x_sb[:, group, :],
                                        bc(bf2_sb.rearrange("p (a d) -> p a d", a=1), [P, 4, D]), ALU.add).then_inc(resid_part, 1)
                pool.wait_ge(x1_ready, 2 * i + 2)
                pool.wait_ge(resid_part, i + 1)
                nc.gpsimd.tensor_tensor(x_sb[:, group, :], x_sb[:, group, :], xn_sb[:, group, 0:D], ALU.add).then_inc(resid_ready, 1)

            pool.wait_ge(x_again, 16)
            resid(0)
            resid(1)
            step(B - 1)
            resid(2)
            step(B)
            resid(3)
            step(B + 1)
            for i in range(4, GROUPS_A):
                resid(i)

        @block.vector
        def _(dve):
            nc.vector.memset(ones_sb, 1.0)
            nc.vector.memset(kT, 0.0)
            for p in range(2):
                last = nc.vector.memset(vbd[:, p, 0, :], 0.0)
            last.then_inc(consts_set, 1)

            def stats_of_x(g, p, first):
                wait_apart_dve("aggr_a", aggr_a, g)
                for j in range(4):
                    last = nc.vector.bn_stats(stA[:, j, :], x_sb[:, ds(4 * g + j, 1), :].rearrange("p a d -> p (a d)"))
                last.then_inc(stats_a, 1)
                wait_apart_dve("stats_a", stats_a, g + 1)
                for j in range(4):
                    last = nc.vector.bn_aggr(mvA[:, p, j, :], stA[:, j, :])
                last.then_inc(aggr_a, 1)

            def normalise(g, p, first):
                dve.wait_ge(rstd_a, g + 1)
                if not first:
                    dve.wait_ge(xnT_psum, g - 1)
                    dve.wait_ge(xn_kept, g - 1)
                for j in range(4):
                    last = nc.vector.tensor_scalar(
                        xnst[:, p, j, :], x_sb[:, ds(4 * g + j, 1), :].rearrange("p a d -> p (a d)"),
                        mvA[:, p, j, 0:1], rsA[:, p, j:j + 1], ALU.subtract, ALU.mult)
                last.then_inc(xn_ready, 1)

            def keep_scores(g, p):
                dve.wait_ge(gate_psum, g + 1)
                nc.vector.tensor_copy(sc[:, ds(4 * g, 4), :].rearrange("p t e -> p (t e)"),
                                      bank[2 + p][:, 0:4 * E]).then_inc(gate_kept, 1)

            dve.wait_ge(x_in[0], 16)
            stats_of_x(0, 0, True)
            dve.wait_ge(x_in[1], 16)
            stats_of_x(1, 1, True)
            normalise(0, 0, True)
            dve.wait_ge(x_in[2], 16)
            stats_of_x(2, 0, False)
            normalise(1, 1, True)
            dve.wait_ge(x_in[3], 16)
            with dve.Fori(0, (GROUPS_A - 4) // 2) as i:
                stats_of_x(2 * i + 3, 1, False)
                normalise(2 * i + 2, 0, False)
                keep_scores(2 * i, 0)
                stats_of_x(2 * i + 4, 0, False)
                normalise(2 * i + 3, 1, False)
                keep_scores(2 * i + 1, 1)
            g = GROUPS_A - 4
            stats_of_x(g + 3, 1, False)
            normalise(g + 2, 0, False)
            keep_scores(g, 0)
            normalise(g + 3, 1, False)
            for g in range(GROUPS_A - 3, GROUPS_A):
                keep_scores(g, g % 2)

            def stats_of_xn(b):
                if some(b):
                    dve.wait_ge(h_ready, b)
                    wait_apart_dve("aggr_1", aggr_1, b)
                for t in range(TPB):
                    last = nc.vector.bn_stats(st1[:, t, :], xn_sb[:, ds(b * TPB + t, 1), 0:D].rearrange("p a d -> p (a d)"))
                last.then_inc(stats_1, 1)
                wait_apart_dve("stats_1", stats_1, b + 1)
                for t in range(TPB):
                    last = nc.vector.bn_aggr(mv1[:, t, :], st1[:, t, :])
                last.then_inc(aggr_1, 1)

            def h_of(b):
                dve.wait_ge(rstd_1, b + 1)
                if some(b):
                    dve.wait_ge(hT_psum, b)
                for t in range(TPB):
                    row = ds(b * TPB + t, 1)
                    last = nc.vector.tensor_scalar(
                        hbuf[:, t, :], xn_sb[:, row, 0:D].rearrange("p a d -> p (a d)"),
                        mv1[:, t, 0:1], rstd1[:, t:t + 1], ALU.subtract, ALU.mult)
                last.then_inc(h_ready, 1)

            def bias(b):
                dve.wait_ge(qkv_psum, b + 1)
                if some(b):
                    semaphore, value = rope_count(b - 1)
                    dve.wait_ge(semaphore, value)
                    dve.wait_ge(heads_psum, b)
                src = qkv_bank[:, 0:TPB * 192].rearrange("p (t c) -> p t c", t=TPB)
                nc.vector.tensor_tensor(qkb, src[:, :, 0:160],
                                        bc(bqkv_sb[:, 0:160].rearrange("p (a c) -> p a c", a=1), [P, TPB, 160]), ALU.add)
                for t in range(TPB):
                    last = nc.vector.tensor_tensor(
                        vb[:, t], bc(src[:, t, 160:192].rearrange("p (a c) -> p a c", a=1), [P, G, 32]),
                        bc(bqkv_sb[:, 160:192].rearrange("p (a c) -> p a c", a=1), [P, G, 32]), ALU.add)
                last.then_inc(qkv_biased, 1)

            def values_T(b):
                dve.wait_ge(heads_psum, b + 1)
                if some(b):
                    dve.wait_ge(vbd_ready, b)
                nc.vector.transpose(vt, qkv_bank[:, 0:T]).then_inc(vt_ready, 1)

            steps = [0]

            def link(*together):
                for ins in together:
                    steps[0] += 1
                    ins.then_inc(route_chain, 1)
                dve.wait_ge(route_chain, steps[0])

            dve.wait_ge(xn_kept, GROUPS_A)
            stats_of_xn(0)
            dve.wait_ge(gate_kept, GROUPS_A)
            dve.wait_ge(small_in, 16 * N_SMALL)
            full = [P, NT, E]

            def per_tok(ap):
                return bc(ap.rearrange("p (t a) -> p t a", a=1), full)

            def per_exp(ap):
                return bc(ap.rearrange("p (a e) -> p a e", a=1), full)

            rest = sc
            for c in range(2):
                link(nc.vector.tensor_reduce(top[:, c, :], rest, AX.X, ALU.max))
                link(nc.vector.tensor_tensor(tmp[:, 0], rest, per_tok(top[:, c, :]), ALU.is_ge))
                link(nc.vector.tensor_tensor(tmp[:, 0], tmp[:, 0], per_exp(rev_sb), ALU.mult))
                link(nc.vector.tensor_reduce(pick, tmp[:, 0], AX.X, ALU.max))
                link(nc.vector.tensor_tensor(oh[:, c], tmp[:, 0], per_tok(pick), ALU.is_equal))
                if c == 0:
                    link(nc.vector.scalar_tensor_tensor(tmp[:, 1], oh[:, 0], -3e38, sc, ALU.mult, ALU.add))
                    rest = tmp[:, 1]
            nc.vector.tensor_tensor(asum, oh[:, 0], oh[:, 1], ALU.add).then_inc(pairs_ready, 1)
            nc.vector.tensor_scalar(xn_sb[:, :, D], slotgrid_sb[:, 0:NT], 2.0, None, ALU.mult)
            h_of(0)
            stats_of_xn(1)
            dve.wait_ge(ranks_psum, 1)
            link(nc.vector.tensor_copy(tot.rearrange("p t e -> p (t e)"), bank[6][:, 256:512]))
            for e in range(E):
                last = nc.vector.tensor_tensor_scan(incl[:, :, e], ones_sb[:, 0:NT], tot[:, :, e], 0.0, ALU.mult, ALU.add)
            link(last)
            link(nc.vector.tensor_tensor(slotm, incl, tot, ALU.subtract),
                 nc.vector.tensor_scalar(cnt[:, 0, :], incl[:, NT - 1, :], 1.0 / P, (P - 1) / P - 0.498, ALU.mult, ALU.add))
            link(nc.vector.tensor_tensor(slotm.rearrange("p t e -> p (t e)"), bank[6][:, 0:256],
                                         slotm.rearrange("p t e -> p (t e)"), ALU.add),
                 nc.vector.tensor_scalar(cnt[:, 0, :], cnt[:, 0, :], 8388608.0, None, ALU.add))
            link(nc.vector.tensor_scalar(cnt[:, 0, :], cnt[:, 0, :], -8388608.0, float(P), ALU.add, ALU.mult))
            link(nc.vector.tensor_tensor_scan(cnt[:, 1, :], ones_sb[:, 0:E], cnt[:, 0, :], 0.0, ALU.mult, ALU.add))
            link(nc.vector.tensor_tensor(cnt[:, 2, :], cnt[:, 1, :], cnt[:, 0, :], ALU.subtract))
            link(nc.vector.tensor_tensor(slotm, slotm, per_exp(cnt[:, 2, :]), ALU.add))
            link(nc.vector.tensor_tensor(tmp, bc(slotm.rearrange("p (c t) e -> p c t e", c=1), [P, 2, NT, E]), oh, ALU.mult))
            link(nc.vector.tensor_reduce(slotf.rearrange("p t c -> p c t"), tmp, AX.X, ALU.add))
            nc.vector.tensor_copy(xn_sb[:, :, D + 1], slotf[:, :, 1])
            nc.vector.tensor_copy(slot, slotf).then_inc(slots_ready, 1)
            link(nc.vector.scalar_tensor_tensor(tmp[:, 0], sc, -1.0, sc, ALU.mult, ALU.max))
            for c in range(2):
                link(nc.vector.tensor_tensor(dist[:, c], per_tok(top[:, c, :]), sc, ALU.subtract))
                link(nc.vector.tensor_tensor(tmp[:, 1], tmp[:, 0], per_tok(top[:, c, :]), ALU.max))
                link(nc.vector.scalar_tensor_tensor(keep[:, c], tmp[:, 1], JITTER2, dist[:, c], ALU.mult, ALU.is_ge))
            link(nc.vector.tensor_tensor(tmp[:, 0], keep[:, 1], oh[:, 0], ALU.mult))
            link(nc.vector.tensor_tensor(keep[:, 1], keep[:, 1], tmp[:, 0], ALU.subtract))
            nc.vector.tensor_scalar(dist, dist, 0.0, None, ALU.max).then_inc(dist_ready, 1)
            dve.wait_ge(gate_in, 32)
            nc.vector.tensor_copy(identb_sb, ident_sb)
            for p in range(2):
                last = nc.vector.tensor_copy(
                    vbd[:, p, 1:NBLK + 1, NKV * HD:VW],
                    bc(vmask_sb[:, NKV * HD:VW].rearrange("p (a c) -> p a c", a=1), [P, NBLK, NKV]))
            last.then_inc(consts_set, 1)


            h_of(1)
            stats_of_xn(2)
            bias(0)
            rotate(nc.vector, dve, 0)
            values_T(0)
            h_of(2)
            bias(1)
            rotate(nc.vector, dve, 1)

            grid3 = [P, SLOT_TILES, 7]
            link(nc.vector.tensor_tensor(past.rearrange("p (j e) -> p j e", e=7), grid_sb.rearrange("p (j e) -> p j e", e=7),
                                         bc(cnt[:, 1, 0:7].rearrange("p (a e) -> p a e", a=1), grid3), ALU.is_ge))
            link(nc.vector.tensor_reduce(tef, past.rearrange("p (j e) -> p j e", e=7), AX.X, ALU.add))
            nc.vector.tensor_scalar(te, tef, float(ESTRIDE), None, ALU.mult).then_inc(experts_ready, 1)
            dve.wait_ge(route_exp, 1)
            link(nc.vector.tensor_tensor(tmp, dist, keep, ALU.mult))
            for c in range(2):
                link(nc.vector.tensor_reduce(mult[:, :, c], tmp[:, c], AX.X, ALU.add))
            nc.vector.reciprocal(mult, mult).then_inc(mult_ready, 1)

            def values(b, p):
                dve.wait_ge(vt_ready, b + 1)
                if some(b - 1):
                    dve.wait_ge(pv_psum, b - 1)
                nc.vector.tensor_tensor(
                    vbd[:, p, 1:NBLK + 1, 0:NKV * HD], vt.rearrange("p (n c) -> p n c", n=NBLK),
                    bc(vmask_sb[:, 0:NKV * HD].rearrange("p (a c) -> p a c", a=1), [P, NBLK, NKV * HD]),
                    ALU.mult).then_inc(vbd_ready, 1)

            def shift(b, u):
                dve.wait_ge(scores_psum, UNITS * b + u + 1)
                for n in range(2):
                    src = bank[u % 2][:, n * 256:(n + 1) * 256].rearrange("p (h g k) -> p g h k", h=2, k=WIN)
                    last = nc.vector.tensor_reduce(rmax[:, u, n, :], src, AX.XY, ALU.max)
                last.then_inc(rowmax_ready, 1)
                dve.wait_ge(rowmax_ready, UNITS * b + u + 1)
                if some(b):
                    dve.wait_ge(pT_ready, UNITS * b + u - (UNITS - 1))
                for n in range(2):
                    shape = [P, 2, G, WIN]
                    last = nc.vector.tensor_tensor(
                        S[:, u, n * 256:(n + 1) * 256].rearrange("p (h g k) -> p h g k", h=2, k=WIN),
                        bank[u % 2][:, n * 256:(n + 1) * 256].rearrange("p (h g k) -> p h g k", h=2, k=WIN),
                        bc(rmax[:, u, n, :].rearrange("p (a g b) -> p a g b", a=1, b=1), shape), ALU.subtract)
                last.then_inc(shifted, 1)

            def weights_T(b, u):
                dve.wait_ge(exp_ready, b + 1)
                if some(b):
                    dve.wait_ge(pv_psum, b)
                nc.vector.transpose(pT[:, 4 * u:4 * u + 4].rearrange("p n g q -> p (n g q)"), S[:, u, :]).then_inc(pT_ready, 1)

            def norm(b):
                dve.wait_ge(pv_psum, b + 1)
                pv = turn_bank[:, 0:NBLK * VW].rearrange("p (n c) -> p n c", c=VW)
                nc.vector.reciprocal(rsum, pv[:, :, NKV * HD:VW]).then_inc(rsum_ready, 1)
                dve.wait_ge(rsum_ready, b + 1)
                nc.vector.tensor_tensor(
                    on.rearrange("p (n h d) -> p n h d", h=NKV, d=HD),
                    pv[:, :, 0:NKV * HD].rearrange("p n (h d) -> p n h d", d=HD),
                    bc(rsum.rearrange("p n (h a) -> p n h a", a=1), [P, NBLK, NKV, HD]), ALU.mult).then_inc(pv_normed, 1)
                dve.wait_ge(pv_normed, b + 1)
                nc.vector.transpose(outT, on).then_inc(outT_ready, 1)

            def residual(b):
                dve.wait_ge(wo_psum, b + 1)
                dve.wait_ge(bo_added, b + 1)
                rows = ds(b * TPB, TPB)
                nc.vector.tensor_tensor(xn_sb[:, rows, 0:D], qkv_bank[:, T:2 * T].rearrange("p (t d) -> p t d", t=TPB),
                                        xn_sb[:, rows, 0:D], ALU.add).then_inc(x1_ready, 1)
                wait_apart_dve("x1_ready", x1_ready, b + 1)
                for t in range(TPB):
                    last = nc.vector.bn_stats(st2[:, t, :], xn_sb[:, ds(b * TPB + t, 1), 0:D].rearrange("p a d -> p (a d)"))
                last.then_inc(stats_2, 1)
                if some(b):
                    dve.wait_ge(h2_ready, b)
                wait_apart_dve("stats_2", stats_2, b + 1)
                for t in range(TPB):
                    nc.vector.bn_aggr(mv2[:, t, :], st2[:, t, :]).then_inc(aggr_2, 1)

            def h2_of(b):
                dve.wait_ge(rstd_2, b + 1)
                if some(b):
                    dve.wait_ge(h2T_psum, b)
                for t in range(TPB):
                    last = nc.vector.tensor_scalar(
                        h2[:, t, :], xn_sb[:, ds(b * TPB + t, 1), 0:D].rearrange("p a d -> p (a d)"),
                        mv2[:, t, 0:1], rstd2[:, t:t + 1], ALU.subtract, ALU.mult)
                last.then_inc(h2_ready, 1)

            def split_xsT(m, i):
                j, p = TILES * m + i, i % 2
                dve.wait_ge(xsT_psum, j + 1)
                if some(j - 1):
                    dve.wait_ge(h3_psum, j - 1)
                nc.vector.tensor_copy(xsT[:, p, 0, :].bitcast(F32R), y_bank[:, D:D + P]).then_inc(xs_high, 1)
                dve.wait_ge(xs_high, j + 1)
                nc.vector.tensor_tensor(xsT[:, p, 1, :].bitcast(F32R), y_bank[:, D:D + P], xsT[:, p, 0, :], ALU.subtract).then_inc(xsT_ready, 1)

            def gated(m, i):
                j, p, b = TILES * m + i, i % 2, i % 3
                dve.wait_ge(slots_in[b], 16 * (TILES // 3 * m + i // 3 + 1))
                if some(TILES // 3 * m + i // 3):
                    dve.wait_ge(y_stored[b], 16 * (TILES // 3 * m + i // 3))
                nc.vector.scalar_tensor_tensor(pair[:, b:b + 1], xsb[:, b, D + 1:XW], slotgrid_sb[:, ds(j, 1)],
                                               xsb[:, b, D:D + 1], ALU.is_equal, ALU.add).then_inc(pair_ready, 1)
                dve.wait_ge(h3_psum, j + 1)
                dve.wait_ge(silu_ready, j + 1)
                if some(j - 1):
                    dve.wait_ge(iT_psum, j - 1)
                nc.vector.tensor_tensor(inter[:, p, :], h3_bank[:, 0:FE], act1[:, p, :], ALU.mult).then_inc(inter_ready, 1)

            def take_y(m, i):
                dve.wait_ge(y_psum, TILES * m + i + 1)
                if some(TILES // 3 * m + i // 3):
                    dve.wait_ge(y_stored[i % 3], 16 * (TILES // 3 * m + i // 3))
                nc.vector.tensor_copy(ysb[:, i % 3, :], y_bank[:, 0:D]).then_inc(y_ready, 1)

            def add_experts(i):
                dve.wait_ge(resid_ready, i + 1)
                if i == 0:
                    dve.wait_ge(ff_added, i + 1)
                dve.wait_ge(pairs_in[i % 4], 16 * (i // 4 + 1))
                for c in range(2):
                    for t in range(4 * i, 4 * i + 4):
                        last = nc.vector.scalar_tensor_tensor(
                            x_sb[:, t, :], yrow[:, i % 4, t % 4, c * D:(c + 1) * D], mult[:, t, c:c + 1],
                            x_sb[:, t, :], ALU.mult, ALU.add)
                    last.then_inc((first_added, second_added)[c], 1)
                    dve.wait_ge((first_added, second_added)[c], i + 1)

            def finish(i):
                group = slice(4 * i, 4 * i + 4)
                dve.wait_ge(down_psum, i + 1)
                dve.wait_ge(resid_ready, i + 1)
                nc.vector.tensor_tensor(x_sb[:, group, :], bank[6 + i % 2].rearrange("p (t d) -> p t d", t=4),
                                        x_sb[:, group, :], ALU.add).then_inc(ff_added, 1)

            def step(k, p, m=None):
                def tile_split(i):
                    if m is not None and within(TILES * m + i):
                        split_xsT(m, i)

                def tile_gated(i):
                    if m is not None:
                        gated(m, i)

                tile_split(1)
                tile_gated(0)
                if exists(k - 1):
                    weights_T(k - 1, 1)
                if exists(k):
                    values(k, p)
                if exists(k - 3):
                    h2_of(k - 3)
                if exists(k + 3):
                    stats_of_xn(k + 3)
                if exists(k + 1):
                    values_T(k + 1)
                if exists(k - 1):
                    weights_T(k - 1, 0)
                tile_split(2)
                tile_gated(1)
                if exists(k):
                    shift(k, 0)
                if exists(k - 1):
                    weights_T(k - 1, 2)
                tile_split(3)
                tile_gated(2)
                if exists(k + 3):
                    h_of(k + 3)
                if exists(k):
                    shift(k, 1)
                if exists(k - 1):
                    weights_T(k - 1, 3)
                tile_split(4)
                tile_gated(3)
                if exists(k + 2):
                    bias(k + 2)
                    if early(k + 2):
                        rotate(nc.vector, dve, k + 2)
                if exists(k):
                    shift(k, 2)
                if after_last(k):
                    add_experts(0)
                    add_experts(1)
                tile_split(5)
                if exists(k):
                    shift(k, 3)
                tile_gated(4)
                if m is not None:
                    take_y(m, Y_TILE)
                tile_split(6)
                tile_gated(5)
                if exists(k - 2):
                    residual(k - 2)
                if exists(k - 1):
                    norm(k - 1)

            dve.wait_ge(consts_set, 2)
            for k in range(LEAD):
                step(k, k % 2)
                if k == 0:
                    dve.wait_ge(high_ready, 2)
                    nc.vector.tensor_tensor(w3_sb.bitcast(F32R), w3_sb, w3_high, ALU.subtract).then_inc(low_ready, 1)
            split_xsT(0, 0)
            step(LEAD, LEAD % 2, 0)
            with dve.Fori(0, (MSTEPS - 4) // 2) as i:
                step(2 * i + LEAD + 1, (LEAD + 1) % 2, 2 * i + 1)
                step(2 * i + LEAD + 2, LEAD % 2, 2 * i + 2)
            for m in range(MSTEPS - 3, MSTEPS):
                step(m + LEAD, (m + LEAD) % 2, m)

            step(B - 1, (B - 1) % 2)
            dve.wait_ge(mult_ready, 1)
            finish(0)
            step(B, B % 2)
            finish(1)
            step(B + 1, (B + 1) % 2)
            step(B + 2, B % 2)
            add_experts(2)
            for i in range(2, GROUPS_A):
                if i + 1 < GROUPS_A:
                    add_experts(i + 1)
                finish(i)

        @block.scalar
        def _(act):
            act.dma_start(ident_sb, ident).then_inc(gate_in, 16)
            act.dma_start(gate_sb, gate).then_inc(gate_in, 16)
            act.dma_start(maskb_sb, maskadd).then_inc(mask_in, 16)

            def keep_xn(g, p):
                act.wait_ge(xn_ready, g + 1)
                nc.scalar.activation(xn_sb[:, ds(4 * g, 4), 0:D], xnst[:, p], ACT.Copy).then_inc(xn_kept, 1)

            def take_xnT(g, p, first):
                act.wait_ge(xnT_psum, g + 1)
                if not first:
                    act.wait_ge(gate_psum, g - 1)
                nc.scalar.activation(xnT[:, p, :], bank[p], ACT.Copy).then_inc(xnT_ready, 1)

            for p in range(2):
                keep_xn(p, p)
                take_xnT(p, p, True)
            with act.Fori(1, GROUPS_A // 2) as i:
                for p in range(2):
                    keep_xn(2 * i + p, p)
                    take_xnT(2 * i + p, p, False)

            for c, (w, high) in enumerate(((w1_sb, w1_high), (w3_sb, w3_high))):
                act.wait_ge(weights_in[c], 16)
                nc.scalar.activation(high.bitcast(F32R), w, ACT.Copy).then_inc(high_ready, 1)

            act.wait_ge(dist_ready, 1)
            nc.scalar.activation(dist, dist, ACT.Exp, scale=-1.0).then_inc(route_exp, 1)

            act.wait_ge(small_in, 16 * N_SMALL)

            def take_hT(b):
                act.wait_ge(hT_psum, b + 1)
                if some(b):
                    act.wait_ge(qkv_psum, b)
                nc.scalar.activation(hT, turn_bank[:, T:2 * T], ACT.Identity, bias=b1c, scale=g1c).then_inc(hT_ready, 1)

            def take_h2T(b):
                act.wait_ge(h2T_psum, b + 1)
                nc.scalar.activation(h2T_sb[:, ds(b * T, T)], turn_bank[:, 0:T], ACT.Identity, bias=b2c, scale=g2c
                                     ).then_inc(h2T_ready, 1)

            def take_keys(b, p):
                act.wait_ge(heads_psum, b + 1)
                if some(b - 1):
                    act.wait_ge(scores_psum, G * (b - 1))
                for g in range(G):
                    rows = slice(g * 32, (g + 1) * 32)
                    last = nc.scalar.activation(kT[rows, p, g, WIN:WIN + T], turn_bank[rows, T:2 * T], ACT.Copy)
                last.then_inc(kT_ready, 1)

            def take_queries(b, p):
                for h in range(NKV):
                    last = nc.scalar.activation(qbd[:, p, :, h, :], turn_bank[:, 0:T].rearrange("p (n q) -> p n q", q=WIN),
                                                ACT.Copy, scale=qmask_sb[:, h:h + 1])
                last.then_inc(qbd_ready, 1)

            def exps(b):
                act.wait_ge(shifted, UNITS * b + UNITS)
                nc.scalar.activation(S, S, ACT.Exp).then_inc(exp_ready, 1)

            def silu(m, i):
                j, p = TILES * m + i, i % 2
                act.wait_ge(h1_psum, j + 1)
                if some(j - 1):
                    act.wait_ge(inter_ready, j - 1)
                nc.scalar.activation(act1[:, p, :], h1_bank[:, 0:FE], ACT.Silu).then_inc(silu_ready, 1)

            def take_y(m, i):
                act.wait_ge(y_psum, TILES * m + i + 1)
                if some(TILES // 3 * m + i // 3):
                    act.wait_ge(y_stored[i % 3], 16 * (TILES // 3 * m + i // 3))
                nc.scalar.activation(ysb[:, i % 3, :], y_bank[:, 0:D], ACT.Copy).then_inc(y_ready, 1)

            def take_iT(m, i):
                j, p = TILES * m + i, i % 2
                act.wait_ge(iT_psum, j + 1)
                if some(j - 1):
                    act.wait_ge(y_psum, j - 1)
                nc.scalar.activation(iT[:, p, :], iT_bank[0:FP, :], ACT.Copy).then_inc(iT_ready, 1)

            def gelu(i):
                for c in range(FC):
                    act.wait_ge(up_psum, FC * i + c + 1)
                    if i >= 4:
                        act.wait_ge(down_psum, i - 3)
                    nc.scalar.activation(gT[i % 4][:, c, :], bank[4 + c % 2], ACT.Gelu, bias=cols_sb[:, 4 + c:5 + c]
                                         ).then_inc(gelu_ready, 1)

            def step(k, p, m=None):
                def tile(i):
                    if is_last(k) and i in (0, 1, 3, 5):
                        gelu((0, 1, 3, 5).index(i))
                    if m is not None:
                        silu(m, i)
                        if some(TILES * m + i) and i - 1 != Y_TILE:
                            take_y(m, i - 1)

                def tile_T(i):
                    if m is not None:
                        take_iT(m, i)
                tile(0)
                tile_T(0)
                if exists(k + 1):
                    take_keys(k + 1, 1 - p)
                tile(1)
                tile_T(1)
                tile(2)
                if exists(k + 1):
                    take_queries(k + 1, 1 - p)
                tile_T(2)
                tile(3)
                if exists(k + 3):
                    take_hT(k + 3)
                if exists(k - 3):
                    take_h2T(k - 3)
                tile_T(3)
                tile(4)
                if exists(k):
                    exps(k)
                tile_T(4)
                tile(5)
                tile_T(5)

            take_hT(0)
            take_hT(1)
            take_keys(0, 0)
            take_queries(0, 0)
            take_hT(2)
            for k in range(LEAD):
                step(k, k % 2)
            step(LEAD, LEAD % 2, 0)
            with act.Fori(0, (MSTEPS - 4) // 2) as i:
                step(2 * i + LEAD + 1, (LEAD + 1) % 2, 2 * i + 1)
                step(2 * i + LEAD + 2, LEAD % 2, 2 * i + 2)
            for m in range(MSTEPS - 3, MSTEPS):
                step(m + LEAD, (m + LEAD) % 2, m)
            take_y(MSTEPS, -1)
            step(B - 1, (B - 1) % 2)
            gelu(4)
            for k in range(B, B + 3):
                step(k, k % 2)
                gelu(k - B + 5)

        @block.tensor
        def _(pe):
            def transpose_xn(g, p, first):
                pe.wait_ge(xn_ready, g + 1)
                if not first:
                    pe.wait_ge(xnT_ready, g - 1)
                for j in range(4):
                    last = nc.tensor.transpose(bank[p][:, j * P:(j + 1) * P], xnst[:, p, j, :], ident_sb)
                last.then_inc(xnT_psum, 1)

            def gates(g, p, first):
                pe.wait_ge(xnT_ready, g + 1)
                if not first:
                    pe.wait_ge(gate_kept, g - 1)
                for j in range(4):
                    last = nc.tensor.matmul(bank[2 + p][:, j * E:(j + 1) * E], xnT[:, p, j * P:(j + 1) * P], gate_sb,
                                            start=True, stop=True)
                last.then_inc(gate_psum, 1)

            pe.wait_ge(gate_in, 32)
            transpose_xn(0, 0, True)
            transpose_xn(1, 1, True)
            gates(0, 0, True)
            transpose_xn(2, 0, False)
            gates(1, 1, True)
            with pe.Fori(0, (GROUPS_A - 4) // 2) as i:
                transpose_xn(2 * i + 3, 1, False)
                gates(2 * i + 2, 0, False)
                transpose_xn(2 * i + 4, 0, False)
                gates(2 * i + 3, 1, False)
            transpose_xn(GROUPS_A - 1, 1, False)
            gates(GROUPS_A - 2, 0, False)
            gates(GROUPS_A - 1, 1, False)

            pe.wait_ge(small_in, 16 * N_SMALL)
            pe.wait_ge(consts_set, 1)
            pe.wait_ge(pairs_ready, 1)
            flat = asum.rearrange("p t e -> p (t e)")
            nc.tensor.matmul(bank[6][:, 0:256], tri_sb, flat, start=True, stop=True)
            nc.tensor.matmul(bank[6][:, 256:512], ones_sb, flat, start=True, stop=True).then_inc(ranks_psum, 1)

            def transpose_h(b):
                pe.wait_ge(h_ready, b + 1)
                if some(b):
                    pe.wait_ge(hT_ready, b)
                for t in range(TPB):
                    last = nc.tensor.transpose(turn_bank[:, T + t * P:T + (t + 1) * P], hbuf[:, t, :], ident_sb)
                last.then_inc(hT_psum, 1)

            def qkv(b):
                pe.wait_ge(hT_ready, b + 1)
                if some(b):
                    pe.wait_ge(qkv_biased, b)
                    pe.wait_ge(vt_ready, b)
                if some(b - 4):
                    pe.wait_ge(x1_ready, b - 4)
                for t in range(TPB):
                    last = nc.tensor.matmul(qkv_bank[:, t * 192:(t + 1) * 192], hT[:, t * P:(t + 1) * P], wqkv_sb,
                                            start=True, stop=True)
                last.then_inc(qkv_psum, 1)

            def heads(b, hT_out):
                pe.wait_ge(qkv_biased, b + 1)
                semaphore, value = rope_count(b)
                pe.wait_ge(semaphore, value)
                pe.wait_ge(hT_ready, hT_out)
                if some(b - 2):
                    pe.wait_ge(pv_normed, b - 2)
                if some(b - 3):
                    pe.wait_ge(x1_ready, b - 3)
                for t in range(TPB):
                    cols = slice(t * P, (t + 1) * P)
                    nc.tensor.transpose(turn_bank[:, cols], qr[:, t, :], ident_sb)
                    nc.tensor.transpose(turn_bank[:, T + t * P:T + (t + 1) * P], kr[:, t].rearrange("p g c -> p (g c)"), ident_sb)
                    last = nc.tensor.transpose(qkv_bank[:, cols], vb[:, t].rearrange("p g c -> p (g c)"), ident_sb)
                last.then_inc(heads_psum, 1)

            def scores(b, p, u):
                if u == 0:
                    pe.wait_ge(qbd_ready, b + 1)
                    pe.wait_ge(kT_ready, b + 1)
                if some(UNITS * b + u - 1):
                    pe.wait_ge(shifted, UNITS * b + u - 1)
                nc.tensor.matmul(bank[u % 2], identb_sb,
                                 bc(maskb_sb[:, 4 * u * WIN:(4 * u + 4) * WIN].rearrange("p (h a k) -> p h a k", a=1, k=WIN),
                                    [P, 4, G, WIN]), start=True, stop=False)
                for i in range(2):
                    n = 2 * u + i
                    last = nc.tensor.matmul(
                        bank[u % 2][:, i * 256:(i + 1) * 256], qbd[:, p, n].rearrange("p h q -> p (h q)"),
                        kT[:, p, :, n * WIN:n * WIN + KW].rearrange("p g (h k) -> p h g k", k=WIN), start=False, stop=(i == 1))
                last.then_inc(scores_psum, 1)

            def transpose_h2(b):
                pe.wait_ge(h2_ready, b + 1)
                if some(b):
                    pe.wait_ge(h2T_ready, b)
                for t in range(TPB):
                    last = nc.tensor.transpose(turn_bank[:, t * P:(t + 1) * P], h2[:, t, :], ident_sb)
                last.then_inc(h2T_psum, 1)

            def attend(b, p, quarter, hT_out, h2T_out):
                if quarter == 0:
                    pe.wait_ge(pT_ready, UNITS * b + UNITS)
                    pe.wait_ge(vbd_ready, b + 1)
                    pe.wait_ge(hT_ready, hT_out)
                    if some(h2T_out):
                        pe.wait_ge(h2T_ready, h2T_out)
                for n in range(quarter * NBLK // 4, (quarter + 1) * NBLK // 4):
                    for i in range(2):
                        last = nc.tensor.matmul(turn_bank[:, n * VW:(n + 1) * VW],
                                                pT[:, 2 * n + i].rearrange("p g q -> p (g q)"),
                                                vbd[:, p, n + i, :], start=(i == 0), stop=(i == 1))
                if quarter == 3:
                    last.then_inc(pv_psum, 1)

            def project(b, qkv_out, vt_out):
                pe.wait_ge(outT_ready, b + 1)
                pe.wait_ge(qkv_biased, qkv_out)
                pe.wait_ge(vt_ready, vt_out)
                if some(b):
                    pe.wait_ge(x1_ready, b)
                for t in range(TPB):
                    last = nc.tensor.matmul(qkv_bank[:, T + t * P:T + (t + 1) * P], outT[:, t * P:(t + 1) * P], wo_sb,
                                            start=True, stop=True)
                last.then_inc(wo_psum, 1)

            def expert_of(j):
                return pe.value_load(te[0:1, ds(j, 1)], min_val=0, max_val=(E - 1) * ESTRIDE)

            def transpose_xs(m, i):
                j = TILES * m + i
                pe.wait_ge(slots_in[i % 3], 16 * (TILES // 3 * m + i // 3 + 1))
                if some(j):
                    pe.wait_ge(xsT_ready, j)
                if some(j - 2):
                    pe.wait_ge(y_ready, j - 2)
                nc.tensor.transpose(y_bank[:, D:D + P], xsb[:, i % 3, 0:D], ident_sb).then_inc(xsT_psum, 1)

            def up_products(m, i, at):
                j, p = TILES * m + i, i % 2
                pe.wait_ge(xsT_ready, j + 1)
                if some(j):
                    pe.wait_ge(silu_ready, j)
                    pe.wait_ge(inter_ready, j)
                for to, high, low, done in ((h1_bank, w1_high, w1_sb, h1_psum), (h3_bank, w3_high, w3_sb, h3_psum)):
                    for n, (rows, w) in enumerate(((0, high), (0, low), (1, high))):
                        last = nc.tensor.matmul(to[:, 0:FE], xsT[:, p, rows, :].bitcast(F32R), w[:, ds(at, FE)].bitcast(F32R),
                                                start=(n == 0), stop=(n == 2))
                    last.then_inc(done, 1)

            def transpose_inter(m, i):
                j, p = TILES * m + i, i % 2
                pe.wait_ge(inter_ready, j + 1)
                if some(j):
                    pe.wait_ge(iT_ready, j)
                for c in range(EC):
                    last = nc.tensor.transpose(iT_bank[0:FP, c * P:(c + 1) * P], inter[:, p, c * FP:(c + 1) * FP], ident_sb)
                last.then_inc(iT_psum, 1)

            def down_product(m, i, xsT_out, at):
                j, p = TILES * m + i, i % 2
                pe.wait_ge(iT_ready, j + 1)
                pe.wait_ge(xsT_ready, xsT_out)
                if some(j):
                    pe.wait_ge(y_ready, j)
                for c in range(EC):
                    last = nc.tensor.matmul(y_bank[:, 0:D], iT[:, p, c * P:(c + 1) * P], w2_sb[:, ds(at + c * P, P)],
                                            start=(c == 0), stop=(c == EC - 1))
                last.then_inc(y_psum, 1)

            def up(i, chunks=range(FC)):
                pe.wait_ge(h2T_ready, 2 * i + 2)
                for c in chunks:
                    if FC * i + c >= 2:
                        pe.wait_ge(gelu_ready, FC * i + c - 1)
                    elif c == 0:
                        pe.wait_ge(silu_ready, SLOT_TILES)
                    else:
                        pe.wait_ge(inter_ready, SLOT_TILES)
                    nc.tensor.matmul(bank[4 + c % 2], wf1_sb[:, c * P:(c + 1) * P], h2T_sb[:, i * 512:(i + 1) * 512],
                                     start=True, stop=True).then_inc(up_psum, 1)

            def down(i):
                pe.wait_ge(gelu_ready, FC * i + FC)
                if i >= 2:
                    pe.wait_ge(ff_added, i - 1)
                elif i == 1:
                    pe.wait_ge(y_ready, SLOT_TILES)
                else:
                    pe.wait_ge(iT_ready, SLOT_TILES)
                for t in range(4):
                    for c in range(FC):
                        last = nc.tensor.matmul(bank[6 + i % 2][:, t * D:(t + 1) * D], gT[i % 4][:, c, t * P:(t + 1) * P],
                                                wf2_sb[:, c, :], start=(c == 0), stop=(c == FC - 1))
                last.then_inc(down_psum, 1)

            def last_step_part(i):
                if i in (2, 4):
                    down(i // 2 - 1)
                else:
                    up((0, 1, 3, 5).index(i))

            def step(k, p, m=None):
                def tile_up(i):
                    if is_last(k):
                        last_step_part(i)
                    if m is not None and i > 0 and within(TILES * m + i):
                        up_products(m, i, expert[i])
                        if within(TILES * m + i + 1):
                            transpose_xs(m, i + 1)
                    if m is not None:
                        if i == 0 and some(m):
                            expert[-1] = expert_of(TILES * m - 1)
                        if 0 < i < TILES and within(TILES * m + i + 1):
                            expert[i + 1] = expert_of(TILES * m + i + 1)

                def tile_down(i):
                    if m is not None and i == 0:
                        expert[0] = expert_of(TILES * m)
                    if m is not None and some(TILES * m + i + 1):
                        down_product(m, i, TILES * m + i + 3 if within(TILES * m + i + 2) else SLOT_TILES, expert[i])

                def tile_T(i):
                    if m is not None:
                        if i == 0:
                            expert[1] = expert_of(TILES * m + 1)
                        transpose_inter(m, i)

                hT_out = k + 4 if exists(k + 3) else B
                expert = {}

                tile_up(0)
                if exists(k):
                    scores(k, p, 0)
                if exists(k + 1):
                    heads(k + 1, k + 3 if exists(k + 2) else B)
                tile_down(-1)
                tile_T(0)
                tile_up(1)
                if exists(k):
                    scores(k, p, 1)
                if exists(k + 2):
                    qkv(k + 2)
                tile_down(0)
                tile_T(1)
                tile_up(2)
                if exists(k):
                    scores(k, p, 2)
                tile_down(1)
                tile_T(2)
                tile_up(3)
                if exists(k):
                    scores(k, p, 3)
                if exists(k + 1):
                    pe.wait_ge(kT_ready, k + 2)
                    pe.wait_ge(qbd_ready, k + 2)
                elif exists(k - 2):
                    pe.wait_ge(pv_normed, k - 1)
                if exists(k - 3):
                    transpose_h2(k - 3)
                if exists(k + 3):
                    transpose_h(k + 3)
                tile_down(2)
                tile_T(3)
                tile_up(4)
                if exists(k - 1):
                    attend(k - 1, 1 - p, 0, hT_out, k - 2)
                tile_down(3)
                if after_last(k):
                    up(5, (0, 1))
                if exists(k - 1):
                    attend(k - 1, 1 - p, 1, hT_out, k - 2)
                tile_T(4)
                tile_up(5)
                if after_last(k):
                    up(5, (2, 3))
                if exists(k - 2):
                    project(k - 2, k + 3 if exists(k + 2) else B, k + 2 if exists(k + 1) else B)
                if exists(k - 1):
                    attend(k - 1, 1 - p, 2, hT_out, k - 2)
                tile_down(4)
                if exists(k - 1):
                    attend(k - 1, 1 - p, 3, hT_out, k - 2)
                tile_T(5)
                if m is not None:
                    tile_up(TILES)

            pe.wait_ge(mask_in, 16)
            transpose_h(0)
            qkv(0)
            transpose_h(1)
            heads(0, 2)
            qkv(1)
            pe.wait_ge(kT_ready, 1)
            pe.wait_ge(qbd_ready, 1)
            transpose_h(2)
            for k in range(LEAD):
                step(k, k % 2)
            pe.wait_ge(experts_ready, 1)
            pe.wait_ge(low_ready, 2)
            pe.wait_ge(weights_in[2], 16)
            transpose_xs(0, 0)
            up_products(0, 0, expert_of(0))
            transpose_xs(0, 1)
            step(LEAD, LEAD % 2, 0)
            with pe.Fori(0, (MSTEPS - 4) // 2) as i:
                step(2 * i + LEAD + 1, (LEAD + 1) % 2, 2 * i + 1)
                step(2 * i + LEAD + 2, LEAD % 2, 2 * i + 2)
            for m in range(MSTEPS - 3, MSTEPS):
                step(m + LEAD, (m + LEAD) % 2, m)
            down_product(MSTEPS - 1, TILES - 1, SLOT_TILES, expert_of(SLOT_TILES - 1))
            step(B - 1, (B - 1) % 2)
            up(4)
            for k in range(B, B + 3):
                step(k, k % 2)
                if k > B:
                    up(k - B + 5)
                down(k - B + 2)
            for i in range(5, GROUPS_A):
                down(i)


def constants():
    f32 = np.float32
    p = np.arange(P)
    half = HD // 2
    theta = (1.0 / 10000.0 ** (np.arange(half, dtype=f32) / f32(half))).astype(f32)
    pos = np.arange(T, dtype=f32)
    freqs = np.outer(pos, theta).astype(f32)
    c, s = np.cos(freqs).astype(f32), np.sin(freqs).astype(f32)
    cosf = np.tile(np.concatenate([c, c], 1), (1, 20)).reshape(TPB, P, 160).transpose(1, 0, 2).reshape(P, -1)
    sinf = np.tile(np.concatenate([-s, s], 1), (1, 20)).reshape(TPB, P, 160).transpose(1, 0, 2).reshape(P, -1)
    q, k = (p % WIN)[:, None], np.arange(KW)[None, :]
    valid = (k - WIN <= q) & (k > q)
    allowed = np.repeat(valid[:, None, :], NBLK, 1)
    allowed[:, 0, :WIN] = False
    maskadd = np.where(allowed, 0.0, NEG).reshape(P, -1).astype(f32)
    qmask = np.where((p // HD % NKV)[:, None] == np.arange(NKV), 1.0 / np.sqrt(f32(HD)), 0.0).astype(f32)
    col = np.concatenate([np.repeat(np.arange(NKV), HD), np.arange(NKV)])
    vmask = ((p // WIN)[:, None] == col).astype(f32)
    tri = (p[:, None] < p[None, :]).astype(f32)
    rev = np.broadcast_to(E - np.arange(E), (P, E)).astype(f32)
    grid = np.broadcast_to(P * np.arange(SLOT_TILES)[:, None], (P, SLOT_TILES, 7)).reshape(P, -1).astype(f32)
    slotgrid = (np.arange(SLOT_TILES)[None, :] * P + p[:, None]).astype(f32)
    return {"slotgrid": slotgrid, "ident": np.eye(P, dtype=f32), "cosf": cosf, "sinf": sinf, "maskadd": maskadd, "qmask": qmask,
            "vmask": vmask, "tri": tri, "rev": rev, "tilegrid": grid}


def laid_out(i):
    def rows(v):
        return np.broadcast_to(v, (P, v.shape[0]))

    heads = (NKV, G, HD)
    wq = i["L0_attn_Wq"].reshape(D, *heads).transpose(0, 2, 1, 3).reshape(D, D)
    bq = i["L0_attn_bq"].reshape(heads).transpose(1, 0, 2).reshape(D)

    def experts(w):
        wide = np.zeros((D, E, ESTRIDE), w.dtype)
        wide[:, :, :FE] = w.transpose(2, 0, 1)
        return wide.reshape(D, -1)

    w2 = i["L0_ffn_w2"].reshape(E, D, EC, FP).transpose(3, 0, 2, 1).reshape(FP, -1)
    return {
        "x": i["L0_attn_x"].reshape(NTOK, D),
        "wqkv": np.concatenate([wq, i["L0_attn_Wk"], i["L0_attn_Wv"]], 1),
        "bqkv": rows(np.concatenate([bq, i["L0_attn_bk"], i["L0_attn_bv"]])),
        "wo": i["L0_attn_Wo"].reshape(*heads, D).transpose(1, 0, 2, 3).reshape(D, D),
        "bo": rows(i["L0_attn_bo"]),
        "g1": i["L0_attn_g1"].reshape(D, 1), "b1": i["L0_attn_b1"].reshape(D, 1),
        "g2": i["L0_attn_g2"].reshape(D, 1), "b2": i["L0_attn_b2"].reshape(D, 1),
        "wf1": i["L0_attn_Wf1"], "bf1": i["L0_attn_bf1"].reshape(FC, P).T,
        "wf2": i["L0_attn_Wf2"].reshape(FC, P, D).transpose(1, 0, 2).reshape(P, -1),
        "bf2": rows(i["L0_attn_bf2"]),
        "gate": i["L0_ffn_gate_w"].T,
        "w1": experts(i["L0_ffn_w1"]), "w3": experts(i["L0_ffn_w3"]), "w2": w2,
    }


def kernel(**inputs):
    import concourse.bacc as bacc
    import ml_dtypes
    from concourse.bass_utils import run_bass_kernel_spmd

    arrays = laid_out({k: np.asarray(v) for k, v in inputs.items()})
    arrays.update(constants())
    arrays["maskadd"] = arrays["maskadd"].astype(ml_dtypes.bfloat16)
    nc = bacc.Bacc("TRN2", target_bir_lowering=False, num_devices=1)
    feeds, aps = {}, {}
    for name, a in arrays.items():
        a = np.ascontiguousarray(a)
        feeds[f"in_{name}"] = a
        aps[name] = nc.dram_tensor(f"in_{name}", a.shape, mybir.dt.from_np(a.dtype), kind="ExternalInput").ap()
    for name, shape in (("xs", (SLOT_TILES * P, XW)), ("ys", (2 * NTOK, D))):
        aps[name] = nc.dram_tensor(f"scratch_{name}", shape, mybir.dt.float32, kind="Internal").ap()
    aps["out"] = nc.dram_tensor("out_dram", (NTOK, D), mybir.dt.float32, kind="ExternalOutput").ap()
    layer(nc, **aps)
    r = run_bass_kernel_spmd(nc, [feeds], core_ids=[0])
    return r.results[0]["out_dram"].reshape(B, T, D)
```
